# Optimizing a Trainium2 kernel written in Bass

```python
import numpy as np
import jax
import jax.numpy as jnp

def _softmax(x, axis=-1):
    return jax.nn.softmax(x, axis=axis)

def _gelu(x):
    return jax.nn.gelu(x, approximate=True)

def _silu(x):
    return jax.nn.silu(x)

def _sigmoid(x):
    return jax.nn.sigmoid(x)

def _layernorm(x, axis=-1, eps=1e-05):
    m = jnp.mean(x, axis=axis, keepdims=True)
    v = jnp.var(x, axis=axis, keepdims=True)
    return (x - m) / jnp.sqrt(v + eps)

def _scatter_add(tgt, idx, src, axis=0):
    return tgt.at[idx].add(src)

def _segment_sum(src, seg, n):
    return jax.ops.segment_sum(src, seg, n)
kernel_name = 'mk_perceiver_d1_seqx_r2_d97167'

def setup_inputs(seed: int=0):
    np.random.seed(seed)
    _w = jnp.asarray

    def _rec_inputs():
        import jax
        import jax.numpy as jnp
        _rk = jax.random.key(seed)
        x = -0.0001661 + 0.9999 * jax.random.normal(jax.random.fold_in(_rk, 1), (2, 512, 512), jnp.float32)
        _lenS = 512 - jax.random.randint(jax.random.fold_in(_rk, 7), (2,), 0, max(1, 512 // 4) + 1, jnp.int32)
        _lenS2 = 8192 - jax.random.randint(jax.random.fold_in(_rk, 8), (2,), 0, max(1, 8192 // 4) + 1, jnp.int32)
        _ctx_1024P = jax.random.normal(jax.random.fold_in(_rk, 11), (2, 16, 512), jnp.float32)
        _ctx_1024c = jax.random.dirichlet(jax.random.fold_in(_rk, 511), 0.3 * jnp.ones((16,), jnp.float32), (2, 8192))
        _ctx_1024t = jnp.einsum('bsk,bkd->bsd', _ctx_1024c, _ctx_1024P)
        _ctx_1024t = _ctx_1024t * jax.lax.rsqrt(jnp.mean(jnp.square(_ctx_1024t)) + 1e-12) * 0.953939
        ctx_1024 = -0.000119273 + 0.999915 * (_ctx_1024t + 0.3 * jax.random.normal(jax.random.fold_in(_rk, 611), (2, 8192, 512), jnp.float32))
        return (x, ctx_1024)
    x, ctx_1024 = _rec_inputs()

    def _L0_xattn_setup():
        import jax, jax.numpy as jnp
        import numpy as np
        B, LQ, LK = (8, 1024, 1024)
        HIST_DIM, COMB_DIM, FUSION_DIM = (512, 512, 512)

        def _linear_params(key, in_dim, out_dim):
            k1, k2 = jax.random.split(key)
            bound = 1.0 / np.sqrt(in_dim)
            W = jax.random.uniform(k1, (out_dim, in_dim), jnp.float32, -bound, bound)
            b = jax.random.uniform(k2, (out_dim,), jnp.float32, -bound, bound)
            return (W, b)

        def _lin(x, W, b):
            return jnp.einsum('bld,fd->blf', x, W) + b
        key = jax.random.key(seed)
        ks = jax.random.split(key, 8)
        hW, hb = _linear_params(ks[0], HIST_DIM, FUSION_DIM)
        cW, cb = _linear_params(ks[1], COMB_DIM, FUSION_DIM)
        qW, qb = _linear_params(ks[2], FUSION_DIM, FUSION_DIM)
        kW, kb = _linear_params(ks[3], FUSION_DIM, FUSION_DIM)
        vW, vb = _linear_params(ks[4], FUSION_DIM, FUSION_DIM)
        oW, ob = _linear_params(ks[5], FUSION_DIM, FUSION_DIM)
        return {'history_features': jax.random.normal(ks[6], (B, LQ, HIST_DIM), jnp.float32), 'combined_features': jax.random.normal(ks[7], (B, LK, COMB_DIM), jnp.float32), 'hW': hW, 'hb': hb, 'cW': cW, 'cb': cb, 'qW': qW, 'qb': qb, 'kW': kW, 'kb': kb, 'vW': vW, 'vb': vb, 'oW': oW, 'ob': ob}
    _L0_xattn_all = _L0_xattn_setup()
    _L0_xattn_in = {k: v for k, v in _L0_xattn_all.items() if k in ('hW', 'hb', 'cW', 'cb', 'qW', 'qb', 'kW', 'kb', 'vW', 'vb', 'oW', 'ob')}
    del _L0_xattn_all

    def _L0_attn_setup():
        import jax, jax.numpy as jnp
        import numpy as np
        B_SZ, L_SEQ, D_MODEL, D_STATE = (4, 1024, 512, 16)

        def _ssm_scan(u, A_log, B_param, C_param, log_dt):
            L = u.shape[1]
            dt = jnp.clip(jnp.exp(log_dt), 0.0001, 1.0)
            A_bar = jnp.exp(-jnp.exp(A_log) * dt[:, None])
            A_bar = jnp.clip(A_bar, 1e-08, 1.0 - 1e-08)
            log_A = jnp.log(A_bar)
            t_idx = jnp.arange(L, dtype=jnp.float32)
            A_powers = jnp.exp(t_idx[:, None, None] * log_A[None, :, :])
            cb_dt = C_param * B_param * dt[:, None]
            kernel = jnp.einsum('ldn,dn->ld', A_powers, cb_dt)
            n_fft = 2 * L
            Kf = jnp.fft.rfft(kernel, n=n_fft, axis=0)
            Uf = jnp.fft.rfft(u, n=n_fft, axis=1)
            y = jnp.fft.irfft(Uf * Kf[None], n=n_fft, axis=1)[:, :L]
            return y.astype(u.dtype)
        key = jax.random.key(seed)
        ks = jax.random.split(key, 6)
        x = jax.random.normal(ks[0], (B_SZ, L_SEQ, D_MODEL), jnp.float32)
        A_log = jnp.clip(jnp.log(jnp.arange(1, D_STATE + 1, dtype=jnp.float32)), -7.0, None)
        A_log = jnp.broadcast_to(A_log[None, :], (D_MODEL, D_STATE)).astype(jnp.float32)
        B_param = 0.02 * jax.random.normal(ks[1], (D_MODEL, D_STATE), jnp.float32)
        C_param = 0.02 * jax.random.normal(ks[2], (D_MODEL, D_STATE), jnp.float32)
        log_dt = 0.01 * jax.random.normal(ks[3], (D_MODEL,), jnp.float32) - 4.0
        in_w = jax.random.normal(ks[4], (2 * D_MODEL, D_MODEL), jnp.float32) / np.sqrt(D_MODEL).astype(np.float32)
        in_b = jnp.zeros((2 * D_MODEL,), jnp.float32)
        out_w = jax.random.normal(ks[5], (D_MODEL, D_MODEL), jnp.float32) / np.sqrt(D_MODEL).astype(np.float32)
        out_b = jnp.zeros((D_MODEL,), jnp.float32)
        ln_g = jnp.ones((D_MODEL,), jnp.float32)
        ln_b = jnp.zeros((D_MODEL,), jnp.float32)
        return {'x': x, 'A_log': A_log, 'B_param': B_param, 'C_param': C_param, 'log_dt': log_dt, 'in_w': in_w, 'in_b': in_b, 'out_w': out_w, 'out_b': out_b, 'ln_g': ln_g, 'ln_b': ln_b}
    _L0_attn_all = _L0_attn_setup()
    _L0_attn_in = {k: v for k, v in _L0_attn_all.items() if k in ('A_log', 'B_param', 'C_param', 'log_dt', 'in_w', 'in_b', 'out_w', 'out_b', 'ln_g', 'ln_b')}
    del _L0_attn_all

    def _L0_ffn_setup():
        import jax, jax.numpy as jnp
        import numpy as np
        NUM_EXPERTS = 8
        D_MODEL = 512
        D_OUT = 512
        key = jax.random.key(seed)
        ks = jax.random.split(key, 5)
        B, S = (2, 1024)
        x = jax.random.normal(ks[0], (B, S, D_MODEL), dtype=jnp.float32)
        gate_w = jax.random.normal(ks[1], (D_MODEL, NUM_EXPERTS), dtype=jnp.float32) * 0.02
        gate_b = jnp.zeros((NUM_EXPERTS,), dtype=jnp.float32)
        expert_w = jax.random.normal(ks[2], (NUM_EXPERTS, D_MODEL, D_OUT), dtype=jnp.float32) * 0.02
        expert_b = jnp.zeros((NUM_EXPERTS, D_OUT), dtype=jnp.float32)
        return {'x': x, 'gate_w': gate_w, 'gate_b': gate_b, 'expert_w': expert_w, 'expert_b': expert_b}
    _L0_ffn_all = _L0_ffn_setup()
    _L0_ffn_in = {k: v for k, v in _L0_ffn_all.items() if k in ('gate_w', 'gate_b', 'expert_w', 'expert_b')}
    del _L0_ffn_all
    return {'x': x, 'ctx_1024': ctx_1024, 'L0_xattn_hW': _L0_xattn_in['hW'], 'L0_xattn_hb': _L0_xattn_in['hb'], 'L0_xattn_cW': _L0_xattn_in['cW'], 'L0_xattn_cb': _L0_xattn_in['cb'], 'L0_xattn_qW': _L0_xattn_in['qW'], 'L0_xattn_qb': _L0_xattn_in['qb'], 'L0_xattn_kW': _L0_xattn_in['kW'], 'L0_xattn_kb': _L0_xattn_in['kb'], 'L0_xattn_vW': _L0_xattn_in['vW'], 'L0_xattn_vb': _L0_xattn_in['vb'], 'L0_xattn_oW': _L0_xattn_in['oW'], 'L0_xattn_ob': _L0_xattn_in['ob'], 'L0_attn_A_log': _L0_attn_in['A_log'], 'L0_attn_B_param': _L0_attn_in['B_param'], 'L0_attn_C_param': _L0_attn_in['C_param'], 'L0_attn_log_dt': _L0_attn_in['log_dt'], 'L0_attn_in_w': _L0_attn_in['in_w'], 'L0_attn_in_b': _L0_attn_in['in_b'], 'L0_attn_out_w': _L0_attn_in['out_w'], 'L0_attn_out_b': _L0_attn_in['out_b'], 'L0_attn_ln_g': _L0_attn_in['ln_g'], 'L0_attn_ln_b': _L0_attn_in['ln_b'], 'L0_ffn_gate_w': _L0_ffn_in['gate_w'], 'L0_ffn_gate_b': _L0_ffn_in['gate_b'], 'L0_ffn_expert_w': _L0_ffn_in['expert_w'], 'L0_ffn_expert_b': _L0_ffn_in['expert_b']}

def reference(x, ctx_1024, L0_xattn_hW, L0_xattn_hb, L0_xattn_cW, L0_xattn_cb, L0_xattn_qW, L0_xattn_qb, L0_xattn_kW, L0_xattn_kb, L0_xattn_vW, L0_xattn_vb, L0_xattn_oW, L0_xattn_ob, L0_attn_A_log, L0_attn_B_param, L0_attn_C_param, L0_attn_log_dt, L0_attn_in_w, L0_attn_in_b, L0_attn_out_w, L0_attn_out_b, L0_attn_ln_g, L0_attn_ln_b, L0_ffn_gate_w, L0_ffn_gate_b, L0_ffn_expert_w, L0_ffn_expert_b):
    import jax
    import jax.numpy as jnp

    def _L0_xattn_ref(history_features, combined_features, hW, hb, cW, cb, qW, qb, kW, kb, vW, vb, oW, ob):
        import jax, jax.numpy as jnp
        import numpy as np
        B, LQ, LK = (8, 1024, 1024)
        HIST_DIM, COMB_DIM, FUSION_DIM = (512, 512, 512)

        def _linear_params(key, in_dim, out_dim):
            k1, k2 = jax.random.split(key)
            bound = 1.0 / np.sqrt(in_dim)
            W = jax.random.uniform(k1, (out_dim, in_dim), jnp.float32, -bound, bound)
            b = jax.random.uniform(k2, (out_dim,), jnp.float32, -bound, bound)
            return (W, b)

        def _lin(x, W, b):
            return jnp.einsum('bld,fd->blf', x, W) + b
        h = _lin(history_features, hW, hb)
        c = _lin(combined_features, cW, cb)
        q = _lin(h, qW, qb)
        k = _lin(c, kW, kb)
        v = _lin(c, vW, vb)
        scale = 1.0 / jnp.sqrt(jnp.float32(FUSION_DIM))
        scores = jnp.einsum('bqf,bkf->bqk', q, k) * scale
        attn = jax.nn.softmax(scores, axis=-1)
        attn_out = jnp.einsum('bqk,bkf->bqf', attn, v)
        return _lin(attn_out + q, oW, ob)

    def _L0_attn_ref(x, A_log, B_param, C_param, log_dt, in_w, in_b, out_w, out_b, ln_g, ln_b):
        import jax, jax.numpy as jnp
        import numpy as np
        B_SZ, L_SEQ, D_MODEL, D_STATE = (4, 1024, 512, 16)

        def _ssm_scan(u, A_log, B_param, C_param, log_dt):
            L = u.shape[1]
            dt = jnp.clip(jnp.exp(log_dt), 0.0001, 1.0)
            A_bar = jnp.exp(-jnp.exp(A_log) * dt[:, None])
            A_bar = jnp.clip(A_bar, 1e-08, 1.0 - 1e-08)
            log_A = jnp.log(A_bar)
            t_idx = jnp.arange(L, dtype=jnp.float32)
            A_powers = jnp.exp(t_idx[:, None, None] * log_A[None, :, :])
            cb_dt = C_param * B_param * dt[:, None]
            kernel = jnp.einsum('ldn,dn->ld', A_powers, cb_dt)
            n_fft = 2 * L
            Kf = jnp.fft.rfft(kernel, n=n_fft, axis=0)
            Uf = jnp.fft.rfft(u, n=n_fft, axis=1)
            y = jnp.fft.irfft(Uf * Kf[None], n=n_fft, axis=1)[:, :L]
            return y.astype(u.dtype)
        x = x.astype(jnp.float32)
        residual = x
        mu = jnp.mean(x, axis=-1, keepdims=True)
        var = jnp.mean(jnp.square(x - mu), axis=-1, keepdims=True)
        xn = (x - mu) * jax.lax.rsqrt(var + 1e-05) * ln_g + ln_b
        xz = xn @ in_w.T + in_b
        x_proj, z = (xz[..., :D_MODEL], xz[..., D_MODEL:])
        z = jax.nn.silu(z)
        y = _ssm_scan(x_proj, A_log, B_param, C_param, log_dt)
        y = y * z
        y = y @ out_w.T + out_b
        return jnp.clip(y + residual, -10.0, 10.0)

    def _L0_ffn_ref(x, gate_w, gate_b, expert_w, expert_b):
        import jax, jax.numpy as jnp
        import numpy as np
        NUM_EXPERTS = 8
        D_MODEL = 512
        D_OUT = 512
        orig_shape = x.shape
        xt = x.reshape(-1, D_MODEL)
        logits = xt @ gate_w + gate_b
        gates = jax.nn.softmax(logits, axis=-1)
        sel = jnp.argmax(gates, axis=-1)
        onehot = jax.nn.one_hot(sel, NUM_EXPERTS, dtype=xt.dtype)
        y_all = jnp.einsum('td,edh->eth', xt, expert_w) + expert_b[:, None, :]
        out = jnp.einsum('te,eth->th', onehot, y_all)
        return out.reshape(*orig_shape[:-1], D_OUT)
    x = x + _L0_xattn_ref(_layernorm(x, axis=-1), ctx_1024, L0_xattn_hW, L0_xattn_hb, L0_xattn_cW, L0_xattn_cb, L0_xattn_qW, L0_xattn_qb, L0_xattn_kW, L0_xattn_kb, L0_xattn_vW, L0_xattn_vb, L0_xattn_oW, L0_xattn_ob)
    x = x + _L0_attn_ref(_layernorm(x, axis=-1), L0_attn_A_log, L0_attn_B_param, L0_attn_C_param, L0_attn_log_dt, L0_attn_in_w, L0_attn_in_b, L0_attn_out_w, L0_attn_out_b, L0_attn_ln_g, L0_attn_ln_b)
    x = x + _L0_ffn_ref(_layernorm(x, axis=-1), L0_ffn_gate_w, L0_ffn_gate_b, L0_ffn_expert_w, L0_ffn_expert_b)
    return x

_drawn_inputs = setup_inputs


def setup_inputs(seed=0):
    import zlib

    import numpy as np

    out = dict(_drawn_inputs(seed))
    spreads = {'L0_attn_in_b': (0.0, 0.8),
     'L0_attn_out_b': (0.0, 0.1),
     'L0_attn_ln_g': (1.0, 0.6),
     'L0_attn_ln_b': (0.0, 0.8),
     'L0_ffn_gate_b': (0.0, 0.1),
     'L0_ffn_expert_b': (0.0, 0.1)}
    factors = {'L0_xattn_cb': 3.928,
     'L0_xattn_qb': 2.705,
     'L0_xattn_kW': 8.0,
     'L0_xattn_kb': 8.0,
     'L0_attn_A_log': 8.0,
     'L0_attn_B_param': 8.0,
     'L0_attn_C_param': 8.0,
     'L0_attn_log_dt': 8.0,
     'L0_attn_in_w': 8.0,
     'L0_attn_out_w': 8.0}
    for name, (base, spread) in spreads.items():
        noise = np.random.default_rng([zlib.crc32(name.encode()), seed]).standard_normal(out[name].shape)
        drawn = base * np.exp(spread * noise) if base else spread * noise
        out[name] = jnp.asarray(drawn.astype(out[name].dtype))
    for name, factor in factors.items():
        out[name] = (out[name] * factor).astype(out[name].dtype)
    return out
```

```python
from contextlib import ExitStack

import concourse.bass as bass
from concourse import mybir

F32 = mybir.dt.float32
F32R = mybir.dt.float32r
I32 = mybir.dt.int32
ALU = mybir.AluOpType
ACT = mybir.ActivationFunctionType
AX_X = mybir.AxisListType.X

P = 128
B, S, D = 2, 512, 512
T = D // P
L = 8192
CH = 512
NCH = L // CH
NS = 16
E = 8
UN = 8
STEPS = NCH * T
TRIPS = STEPS // UN
SCANS = NS * T
MTRIPS = E * T // UN
NBANK = 8
EPS = 1e-5
SCALE = float(D) ** -0.5
LOWEST = -3.0e38
PASSES = ((0, 0), (0, 1), (1, 0))
EXPM1_DOUBLINGS = 8
RSQRT_SEED = float(0x5F3759DF)



def tiles(*names):
    return [f"{n}.{k}" for n in names for k in range(T)]


def mid_jobs(b):
    return [f"{n}@{b}" for n in tiles("pooledT", "vWT", "ctx_to_v", "oWT", "attn", "x_attn", "inT0", "inT1",
                                      "normT", "u", "z")]


def out_jobs(b):
    return [f"{n}@{b}" for n in tiles("outT", "x_ssm")]


def expert_jobs(b):
    return [f"{n}@{b}" for n in tiles("ffnT") + ["logits", "onehotT"] + tiles("expert_bias")
            + [f"expert.{n}" for n in range(E * T)]]


PREP_JOBS = ["vectors"] + tiles("xT0", "qWT", "x_to_q", "q0", "xT1", "q1", "kWT", "q_to_ctx", "qc0", "qc1") + ["key_bias"]
JOBS = (PREP_JOBS + mid_jobs(0) + out_jobs(0) + mid_jobs(1) + expert_jobs(0) + out_jobs(1) + expert_jobs(1))
JOB = {name: n for n, name in enumerate(JOBS)}
ROUNDED_KINDS = ("xT0", "xT1", "qWT", "x_to_q", "kWT", "q_to_ctx", "qc0", "pooledT", "vWT", "ctx_to_v", "oWT",
                 "inT0", "inT1", "outT", "ffnT")
ROUND = {name: k for k, name in enumerate(n for n in JOBS if n.split(".")[0] in ROUNDED_KINDS)}
SPLITS = (["hW", "q0", "cW", "q1"] + ["cW@0", "attn@0", "norm@0", "qc1", "gated@0"] + ["cW@1", "attn@1", "norm@1"]
          + [f"W{e}@0" for e in range(E)] + ["gated@1"] + [f"W{e}@1" for e in range(E)])
SPLIT = {name: T * n for n, name in enumerate(SPLITS)}
ROWS = {name: n + 1 for n, name in enumerate(["x0", "x1", "pooled@0", "norm@0", "ffn@0", "pooled@1", "norm@1", "ffn@1"])}
LOADS = [("qW", 0), ("hW", 1)]
for _b in range(B):
    LOADS += [(f"chunk{_c}@{_b}", _c % 2) for _c in range(NCH)]
    if _b == 1:
        LOADS += [("out_w@0", 1)]
    LOADS += [(f"vW@{_b}", 0), (f"cW@{_b}", 1), (f"oW@{_b}", 0), (f"in0@{_b}", 1), (f"in1@{_b}", 0)]
LOADS += [(f"W{_e}@0", _e % 2) for _e in range(E)] + [("out_w@1", 1)] + [(f"W{_e}@1", _e % 2) for _e in range(E)]
BUF, LANDED = {}, {}
_seen = [0, 0]
for _name, _buf in LOADS:
    _seen[_buf] += 1
    BUF[_name], LANDED[_name] = _buf, 16 * _seen[_buf]


def build(nc, x, ctx_in, hW, hb, cW, cb, qW, qb, kW, kb, vW, vb, oW, ob, A_log, B_param, C_param, log_dt,
          in_w, in_b, out_w, out_b, ln_g, ln_b, gate_w, gate_b, expert_w, expert_b, out):
    with ExitStack() as ctx:
        def sb(name, shape, dt=F32):
            return ctx.enter_context(nc.sbuf_tensor(name, shape, dt))

        def sem(name):
            return ctx.enter_context(nc.semaphore(name))

        hl = [sb(f"hl_{n}", [P, 2, T, D], F32R) for n in "ABCDE"]
        hlA, hlB, hlC, hlD, hlE = hl
        nat = [hlA, hlB]
        ctxT = [hlC, hlE]
        qc_hl = hlD
        probsT = [sb(f"probsT{n}", [P, 2, T, P], F32R) for n in range(2)]
        stage = [sb(f"stage{n}", [P, T, D]) for n in range(2)]
        probs = [sb(f"probs{n}", [P, CH]) for n in range(2)]
        rows = sb("rows", [P, T, D])
        qT = sb("qT", [P, B, T, S])
        qc1 = sb("qc1", [P, T, S])
        xb = sb("xb", [P, B, T, D])
        uT = sb("uT", [P, T, S])
        zT = sb("zT", [P, T, S])
        yT = sb("yT", [P, T, S])
        h = [sb(f"h{n}", [P, S]) for n in range(2)]
        resid = sb("resid", [P, T, D])
        ident = sb("ident", [P, P])
        obB = sb("obB", [P, D])
        outbB = sb("outbB", [P, D])
        eb = sb("eb", [E, D])
        onehotT = sb("onehotT", [E, T * P])
        vrows = sb("vrows", [32, P])
        vecs = sb("vecs", [P, 32])
        gate_raw = sb("gate_raw", [P, T, E])
        gate_hl = sb("gate_hl", [P, 2, T, E], F32R)
        gbB = sb("gbB", [P, E])
        desc = sb("desc", [P, E])
        logit = sb("logit", [P, T, E])
        pick = sb("pick", [P, T, E])
        onehot = sb("onehot", [P, T, E])
        lmax = sb("lmax", [P, 2, T])
        bnst = sb("bnst", [P, T, 6])
        mv = sb("mv", [P, T, 2])
        rstd = sb("rstd", [P, T])
        var = sb("var", [P, T])
        seed = sb("seed", [P, T], I32)
        newton = sb("newton", [P, T])
        qbias = sb("qbias", [P, T])
        kbias = sb("kbias", [P, T])
        vbias = sb("vbias", [P, T])
        kq = sb("kq", [P, B * T])
        mrun = sb("mrun", [P, 2, T])
        mx = sb("mx", [P, T])
        nbias = sb("nbias", [P, T])
        dmax = sb("dmax", [P, T])
        alpha = sb("alpha", [P, T])
        rsum = sb("rsum", [P, T])
        lsum = sb("lsum", [P, T])
        ssm_in = sb("ssm_in", [P, 3, T, NS])
        ssm_w = sb("ssm_w", [P, 4, T, NS])
        dtv = sb("dtv", [P, T])
        abar = sb("abar", [P, NS, T])
        cbdt = sb("cbdt", [P, NS, T])

        bank = [ctx.enter_context(nc.psum_tensor(f"bank{n}", [P, 512], F32)) for n in range(NBANK)]
        sbank, tbank, obank, cbank = bank[0:2], bank[2:4], bank[4:6], bank[6:8]

        in_x = [sem(f"in_x{b}") for b in range(B)]
        in_stage = [sem(f"in_stage{n}") for n in range(2)]
        in_k, in_c, in_v, in_vec, in_bias, in_ssm, in_small = (sem(n) for n in (
            "in_k", "in_c", "in_v", "in_vec", "in_bias", "in_ssm", "in_small"))
        stored = sem("stored")
        ident_zero, ident_ready, desc_ready = sem("ident_zero"), sem("ident_ready"), sem("desc_ready")
        filled, rounded, evacuated = sem("filled"), sem("rounded"), sem("evacuated")
        split_hi, split_done = sem("split_hi"), sem("split_done")
        rows_ready = sem("rows_ready")
        link_done = sem("link_done")
        vectors_ready, ssm_exp, gate_ready, kbias_ready = (sem(n) for n in (
            "vectors_ready", "ssm_exp", "gate_ready", "kbias_ready"))
        x_biased, resid_biased = sem("x_biased"), sem("resid_biased")
        z_exp, y_zeroed, gated, onehot_ready = sem("z_exp"), sem("y_zeroed"), sem("gated"), sem("onehot_ready")
        sums_zeroed = sem("sums_zeroed")
        scores_ready, stat_done, max_ready, dmax_ready, probs_ready, alpha_ready = (sem(n) for n in (
            "scores_ready", "stat_done", "max_ready", "dmax_ready", "probs_ready", "alpha_ready"))
        pT_ready, pT_hi, pT_split = sem("pT_ready"), sem("pT_hi"), sem("pT_split")
        cT_ready, cT_hi, cT_split = sem("cT_ready"), sem("cT_hi"), sem("cT_split")
        nat_hi, nat_split = sem("nat_hi"), sem("nat_split")
        pv_ready, sums_updated = sem("pv_ready"), sem("sums_updated")
        scanned, scaled, summed = sem("scanned"), sem("scaled"), sem("summed")

        block = ctx.enter_context(nc.Block())

        def matrix(w):
            return w.rearrange("(t p) n -> p t n", p=P)

        def across(v):
            return v.rearrange("(a n) -> a n", a=1).partition_broadcast(P)

        ctx_rows = ctx_in.rearrange("b (c p j) d -> (b c) p j d", p=P, j=T)
        experts = expert_w.rearrange("e (t p) n -> e p t n", p=P)

        def wait_pos(eng, s, base, value):
            if not isinstance(value, int) or value > 0:
                eng.wait_ge(s, value + base)

        def trips(eng, n, body):
            body(0, True, False)
            with eng.Fori(1, n - 1) as t:
                body(t, False, False)
            body(n - 1, False, True)

        @block.sync
        def _(sp):
            def load(name, src):
                sp.dma_start(stage[BUF[name]][:], src).then_inc(in_stage[BUF[name]], 16)

            sp.dma_start(xb[:, 0], matrix(x[0])).then_inc(in_x[0], 16)
            load("qW", matrix(qW))
            for k, v in ((0, qb), (4, kb), (8, vb), (12, in_b), (20, ln_g), (24, ln_b), (28, log_dt)):
                n = v.shape[0] // P
                sp.dma_start(vrows[k:k + n, :], v.rearrange("(t p) -> t p", p=P)).then_inc(in_vec, 16)
            load("hW", matrix(hW))
            sp.dma_start(probs[0][:], across(hb)).then_inc(in_bias, 16)
            sp.dma_start(probs[1][:], across(cb)).then_inc(in_bias, 16)
            sp.dma_start(xb[:, 1], matrix(x[1])).then_inc(in_x[1], 16)
            sp.dma_start(zT[:], matrix(cW)).then_inc(in_c, 16)
            sp.dma_start(uT[:], matrix(kW)).then_inc(in_k, 16)
            sp.dma_start(yT[:], matrix(vW)).then_inc(in_v, 16)
            for k, v in enumerate((A_log, B_param, C_param)):
                sp.dma_start(ssm_in[:, k], matrix(v)).then_inc(in_ssm, 16)
            sp.dma_start(obB[:], across(ob)).then_inc(in_small, 16)
            sp.dma_start(outbB[:], across(out_b)).then_inc(in_small, 16)
            sp.dma_start(gbB[:], across(gate_b)).then_inc(in_small, 16)
            sp.dma_start(gate_raw[:], matrix(gate_w)).then_inc(in_small, 16)
            sp.dma_start(eb[:], expert_b).then_inc(in_small, 16)

            def attention_loads(b):
                for c in range(2):
                    load(f"chunk{c}@{b}", ctx_rows[b * NCH + c])
                with sp.Fori(0, NCH // 2 - 1) as t:
                    for c in range(2):
                        sp.wait_ge(cT_ready, t * UN + (b * STEPS + T * (c + 1)))
                        sp.wait_ge(nat_split, t * UN + (b * STEPS + T * (c + 1)))
                        sp.dma_start(stage[c][:], ctx_rows[bass.ds(t * 2 + (b * NCH + 2 + c), 1)].rearrange(
                            "a p j d -> p (a j) d")).then_inc(in_stage[c], 16)

            def mid_loads(b):
                if b == 1:
                    sp.wait_ge(cT_ready, (b + 1) * STEPS)
                    sp.wait_ge(nat_split, (b + 1) * STEPS)
                    load("out_w@0", matrix(out_w))
                sp.wait_ge(cT_ready, (b + 1) * STEPS)
                sp.wait_ge(nat_split, (b + 1) * STEPS)
                load(f"vW@{b}", matrix(vW))
                if b == 1:
                    sp.wait_ge(filled, JOB["outT.3@0"] + 1)
                load(f"cW@{b}", matrix(cW))
                sp.wait_ge(filled, JOB[f"vWT.3@{b}"] + 1)
                load(f"oW@{b}", matrix(oW))
                sp.wait_ge(split_done, SPLIT[f"cW@{b}"] + T)
                load(f"in0@{b}", matrix(in_w[0:D]))
                sp.wait_ge(filled, JOB[f"oWT.3@{b}"] + 1)
                load(f"in1@{b}", matrix(in_w[D:2 * D]))

            def expert_loads(b):
                load(f"W0@{b}", experts[0])
                if b == 1:
                    sp.wait_ge(filled, JOB["outT.3@1"] + 1)
                load(f"W1@{b}", experts[1])
                for e in range(2, E):
                    sp.wait_ge(split_done, SPLIT[f"W{e - 2}@{b}"] + T)
                    load(f"W{e}@{b}", experts[e])

            sp.wait_ge(filled, JOB["qWT.3"] + 1)
            sp.wait_ge(split_done, SPLIT["hW"] + T)
            sp.wait_ge(evacuated, JOB["q0.0"] + 1)
            attention_loads(0)
            mid_loads(0)
            sp.wait_ge(filled, JOB["inT1.3@0"] + 1)
            attention_loads(1)
            mid_loads(1)
            sp.wait_ge(filled, JOB["inT1.3@1"] + 1)
            expert_loads(0)
            sp.wait_ge(split_done, SPLIT["W7@0"] + T)
            load("out_w@1", matrix(out_w))
            sp.wait_ge(evacuated, JOB[f"expert.{E * T - 1}@0"] + 1)
            sp.dma_start(matrix(out[0]), xb[:, 0]).then_inc(stored, 16)
            expert_loads(1)
            for t in range(T):
                sp.wait_ge(evacuated, JOB[f"expert.{E * T - T + t}@1"] + 1)
                sp.dma_start(matrix(out[1])[:, t], xb[:, 1, t]).then_inc(stored, 16)
            sp.wait_ge(stored, 16 * (1 + T))

        @block.tensor
        def _(pe):
            def open_bank(name):
                n = JOB[name]
                if n >= NBANK:
                    pe.wait_ge(evacuated, n - NBANK + 1)
                return bank[n % NBANK]

            def product(dst, lhs, k, rhs):
                for t in range(T):
                    for a, c in PASSES:
                        last = nc.tensor.matmul(dst, lhs[:, a, t, k * P:(k + 1) * P], rhs[:, c, t, :],
                                                start=(t == 0 and (a, c) == PASSES[0]),
                                                stop=(t == T - 1 and (a, c) == PASSES[-1]))
                return last

            def turned(dst, src, k):
                for t in range(T):
                    last = nc.tensor.transpose(dst[:, t * P:(t + 1) * P], src[:, t, k * P:(k + 1) * P], ident[:])
                return last

            def evacuated_from(name):
                pe.wait_ge(evacuated, JOB[name] + 1)

            def split_of(name):
                pe.wait_ge(split_done, SPLIT[name] + T)

            def transposes(name, src):
                for k in range(T):
                    job = name.replace("#", str(k))
                    turned(open_bank(job), src, k).then_inc(filled, 1)

            def products(name, lhs, rhs):
                for k in range(T):
                    job = name.replace("#", str(k))
                    product(open_bank(job)[:], lhs, k, rhs).then_inc(filled, 1)

            def prepare():
                pe.wait_ge(ident_ready, 1)
                pe.wait_ge(in_vec, 16 * 7)
                nc.tensor.transpose(open_bank("vectors")[:, 0:32], vrows[:], ident[0:32, 0:32]).then_inc(filled, 1)
                pe.wait_ge(rows_ready, ROWS["x0"])
                transposes("xT0.#", rows)
                pe.wait_ge(in_stage[0], LANDED["qW"])
                transposes("qWT.#", stage[0])
                split_of("hW")
                evacuated_from("qWT.3")
                products("x_to_q.#", hlB, hlA)
                evacuated_from("x_to_q.3")
                products("q0.#", hlC, hlD)
                pe.wait_ge(rows_ready, ROWS["x1"])
                transposes("xT1.#", resid)
                evacuated_from("xT1.3")
                products("q1.#", hlC, hlD)
                pe.wait_ge(in_k, 16)
                transposes("kWT.#", uT)
                split_of("cW")
                evacuated_from("kWT.3")
                products("q_to_ctx.#", hlD, hlE)
                split_of("q0")
                evacuated_from("q_to_ctx.3")
                products("qc0.#", hlC, hlA)
                split_of("q1")
                products("qc1.#", hlC, hlB)
                pe.wait_ge(kbias_ready, 1)
                dst = open_bank("key_bias")
                for n in range(B * T):
                    for t in range(T):
                        last = nc.tensor.matmul(dst[:, n:n + 1], qT[:, n // T, t, n % T * P:(n % T + 1) * P],
                                                kbias[:, t:t + 1], start=(t == 0), stop=(t == T - 1))
                last.then_inc(filled, 1)

            def attention(b, jobs_before):
                base = b * STEPS
                load0 = [LANDED[f"chunk0@{b}"], LANDED[f"chunk1@{b}"]]

                def turn_context(g, dd):
                    wait_pos(pe, cT_split, base, g - 1)
                    par = g // T % 2 if isinstance(g, int) else None
                    return par

                def context_block(t, u):
                    par, dd = (u // T + 1) % 2, u % T
                    if dd == 0:
                        pe.wait_ge(in_stage[par], (t + (u // T + 1) // 2) * 16 + load0[par])
                    wait_pos(pe, cT_split, base, t * UN + (u + 4 - 1))
                    turned(cbank[dd % 2], stage[par], dd).then_inc(cT_ready, 1)

                def scores(t, u):
                    par, q = u // T % 2, u % T
                    if q == 0:
                        pe.wait_ge(cT_split, t * UN + (base + u + T))
                    wait_pos(pe, probs_ready, base, t * UN + (u - 1))
                    product(sbank[u % 2][:], qc_hl, q, ctxT[par]).then_inc(scores_ready, 1)

                def turn_probs(t, u):
                    pe.wait_ge(probs_ready, t * UN + (base + u + 1))
                    wait_pos(pe, pT_split, base, t * UN + (u - 1))
                    for j in range(T):
                        last = nc.tensor.transpose(tbank[u % 2][:, j * P:(j + 1) * P],
                                                   probs[u % 2][:, j * P:(j + 1) * P], ident[:])
                    last.then_inc(pT_ready, 1)

                def weigh(t, u):
                    par = u // T % 2
                    pe.wait_ge(pT_split, t * UN + (base + u + 1))
                    if u % T == 0:
                        pe.wait_ge(nat_split, t * UN + (base + u + T))
                    wait_pos(pe, sums_updated, 2 * base, t * (2 * UN) + 2 * (u - 1))
                    for j in range(T):
                        for a, c in PASSES:
                            last = nc.tensor.matmul(obank[u % 2][:], probsT[u % 2][:, a, j, :], nat[par][:, c, j, :],
                                                    start=(j == 0 and (a, c) == PASSES[0]),
                                                    stop=(j == T - 1 and (a, c) == PASSES[-1]))
                    last.then_inc(pv_ready, 1)

                def back(t, u, n):
                    return (t, u - n) if u >= n else (t - 1, u - n + UN)

                def trip(t, first, last):
                    for u in range(UN):
                        scores(t, u)
                        if not (first and u < 1):
                            turn_probs(*back(t, u, 1))
                        if not (last and u >= T):
                            context_block(t, u)
                        if not (first and u < 2):
                            weigh(*back(t, u, 2))

                if b == 1:
                    split_of("qc1")
                pe.wait_ge(evacuated, jobs_before)
                pe.wait_ge(in_stage[0], load0[0])
                for dd in range(T):
                    wait_pos(pe, cT_split, base, dd - 1)
                    turned(cbank[dd % 2], stage[0], dd).then_inc(cT_ready, 1)
                trips(pe, TRIPS, trip)
                turn_probs(TRIPS - 1, UN - 1)
                weigh(TRIPS - 1, UN - 2)
                weigh(TRIPS - 1, UN - 1)

            def middle(b):
                pe.wait_ge(rows_ready, ROWS[f"pooled@{b}"])
                transposes(f"pooledT.#@{b}", rows)
                pe.wait_ge(in_stage[0], LANDED[f"vW@{b}"])
                transposes(f"vWT.#@{b}", stage[0])
                split_of(f"cW@{b}")
                evacuated_from(f"vWT.3@{b}")
                products(f"ctx_to_v.#@{b}", hlC, hlB)
                pe.wait_ge(in_stage[0], LANDED[f"oW@{b}"])
                transposes(f"oWT.#@{b}", stage[0])
                evacuated_from(f"ctx_to_v.3@{b}")
                products(f"attn.#@{b}", hlD, hlA)
                split_of(f"attn@{b}")
                evacuated_from(f"oWT.3@{b}")
                products(f"x_attn.#@{b}", hlB, hlE)
                pe.wait_ge(in_stage[1], LANDED[f"in0@{b}"])
                transposes(f"inT0.#@{b}", stage[1])
                pe.wait_ge(in_stage[0], LANDED[f"in1@{b}"])
                transposes(f"inT1.#@{b}", stage[0])
                pe.wait_ge(rows_ready, ROWS[f"norm@{b}"])
                transposes(f"normT.#@{b}", rows)
                split_of(f"norm@{b}")
                products(f"u.#@{b}", hlC, hlA)
                products(f"z.#@{b}", hlD, hlA)

            def project_out(b):
                pe.wait_ge(in_stage[1], LANDED[f"out_w@{b}"])
                transposes(f"outT.#@{b}", stage[1])
                split_of(f"gated@{b}")
                evacuated_from(f"outT.3@{b}")
                products(f"x_ssm.#@{b}", hlA, hlB)

            def mix_experts(b):
                pe.wait_ge(rows_ready, ROWS[f"ffn@{b}"])
                transposes(f"ffnT.#@{b}", qT[:, b])
                evacuated_from(f"ffnT.3@{b}")
                pe.wait_ge(gate_ready, 1)
                dst = open_bank(f"logits@{b}")
                for k in range(T):
                    last = product(dst[:, k * E:(k + 1) * E], hlA, k, gate_hl)
                last.then_inc(filled, 1)
                pe.wait_ge(onehot_ready, b + 1)
                dst = open_bank(f"onehotT@{b}")
                for k in range(T):
                    last = nc.tensor.transpose(dst[0:E, k * P:(k + 1) * P], onehot[:, k, :], ident[:])
                last.then_inc(filled, 1)
                evacuated_from(f"onehotT@{b}")
                for k in range(T):
                    dst = open_bank(f"expert_bias.{k}@{b}")
                    nc.tensor.matmul(dst[:], onehotT[:, k * P:(k + 1) * P], eb[:], start=True, stop=True).then_inc(filled, 1)
                job0, split0 = JOB[f"expert.0@{b}"], SPLIT[f"W0@{b}"]
                with pe.Fori(0, MTRIPS) as t:
                    for u in range(UN):
                        if u % T == 0:
                            pe.wait_ge(split_done, t * UN + (split0 + u + T))
                        pe.wait_ge(evacuated, t * UN + (job0 + u - NBANK + 1))
                        product(bank[(job0 + u) % NBANK][:], hlA, u % T, (hlC, hlD)[u // T]).then_inc(filled, 1)

            prepare()
            attention(0, len(PREP_JOBS))
            middle(0)
            attention(1, JOB["z.3@0"] + 1)
            project_out(0)
            middle(1)
            mix_experts(0)
            project_out(1)
            mix_experts(1)

        @block.scalar
        def _(act):
            def round_job(name, dst):
                act.wait_ge(filled, JOB[name] + 1)
                nc.scalar.activation(dst, bank[JOB[name] % NBANK][:], ACT.Copy).then_inc(rounded, 1)

            def round_jobs(name, slot):
                for k in range(T):
                    round_job(name.replace("#", str(k)), slot[:, 0, k, :])

            def round_tiles(src, slot):
                for k in range(T):
                    nc.scalar.activation(slot[:, 0, k, :], src[:, k, :], ACT.Copy).then_inc(split_hi, 1)

            def round_evacuated(name, src, slot):
                for k in range(T):
                    act.wait_ge(evacuated, JOB[name.replace("#", str(k))] + 1)
                    nc.scalar.activation(slot[:, 0, k, :], src[:, k, :], ACT.Copy).then_inc(split_hi, 1)

            def prepare():
                round_jobs("xT0.#", hlD)
                round_jobs("qWT.#", hlA)
                act.wait_ge(in_stage[1], LANDED["hW"])
                round_tiles(stage[1], hlB)
                round_jobs("x_to_q.#", hlC)
                round_evacuated("q0.#", qT[:, 0], hlA)
                round_jobs("xT1.#", hlD)
                act.wait_ge(in_c, 16)
                round_tiles(zT, hlE)
                round_evacuated("q1.#", qT[:, 1], hlB)
                round_jobs("kWT.#", hlD)
                round_jobs("q_to_ctx.#", hlC)
                round_jobs("qc0.#", hlD)
                act.wait_ge(in_ssm, 16 * 3)
                act.wait_ge(vectors_ready, 1)
                nc.scalar.activation(ssm_w[:, 0], ssm_in[:, 0], ACT.Exp).then_inc(ssm_exp, 1)
                nc.scalar.activation(dtv[:], vecs[:, 28:32], ACT.Exp).then_inc(ssm_exp, 1)

            def attention(b, jobs_before, scan):
                base = b * STEPS
                load0 = [LANDED[f"chunk0@{b}"], LANDED[f"chunk1@{b}"]]

                def natural(t, u):
                    g = u + 2
                    par, j = g // T % 2, g % T
                    if j == 0 or (j == 2 and u == 0):
                        act.wait_ge(in_stage[par], (t + g // T // 2) * 16 + load0[par])
                    wait_pos(act, pv_ready, base, t * UN + (g // T - 1) * T)
                    nc.scalar.activation(nat[par][:, 0, j, :], stage[par][:, j, :], ACT.Copy).then_inc(nat_hi, 1)

                def context_block(t, u):
                    par, dd = (u // T + 1) % 2, u % T
                    act.wait_ge(cT_ready, t * UN + (base + u + T + 1))
                    nc.scalar.activation(ctxT[par][:, 0, dd, :], cbank[dd % 2][:], ACT.Copy).then_inc(cT_hi, 1)

                def turned_probs(t, u):
                    act.wait_ge(pT_ready, t * UN + (base + u + 1))
                    nc.scalar.activation(probsT[u % 2][:, 0], tbank[u % 2][:].rearrange("p (j q) -> p j q", j=T),
                                         ACT.Copy).then_inc(pT_hi, 1)

                def exponentials(t, u):
                    q = u % T
                    wait_pos(act, pT_ready, base, t * UN + (u - 1))
                    wait_pos(act, sums_updated, 2 * base, t * (2 * UN) + 2 * (u - 3))
                    act.wait_ge(max_ready, t * UN + (base + u + 1))
                    nc.scalar.activation(probs[u % 2][:], sbank[u % 2][:], ACT.Exp, bias=nbias[:, q:q + 1], scale=SCALE,
                                         accum_out=rsum[:, q:q + 1]).then_inc(probs_ready, 1)
                    act.wait_ge(dmax_ready, t * UN + (base + u + 1))
                    nc.scalar.activation(alpha[:, q:q + 1], dmax[:, q:q + 1], ACT.Exp, scale=SCALE).then_inc(alpha_ready, 1)

                def trip(t, first, last):
                    for u in range(UN):
                        exponentials(t, u)
                        if not (first and u < 1):
                            turned_probs(*((t, u - 1) if u else (t - 1, UN - 1)))
                        if not (last and u >= T):
                            context_block(t, u)
                        if not (last and u + 2 >= UN):
                            natural(t, u)
                        if scan:
                            scale_state(0, t * UN + u, u)

                act.wait_ge(filled, jobs_before)
                if b == 1:
                    round_tiles(qc1, hlD)
                for dd in range(T):
                    act.wait_ge(cT_ready, base + dd + 1)
                    nc.scalar.activation(ctxT[0][:, 0, dd, :], cbank[dd % 2][:], ACT.Copy).then_inc(cT_hi, 1)
                act.wait_ge(in_stage[0], load0[0])
                for j in range(2):
                    nc.scalar.activation(nat[0][:, 0, j, :], stage[0][:, j, :], ACT.Copy).then_inc(nat_hi, 1)
                trips(act, TRIPS, trip)
                turned_probs(TRIPS - 1, UN - 1)

            def scale_state(b, s, k):
                act.wait_ge(scanned, s + (b * SCANS + 1))
                col = cbdt[:].rearrange("p n d -> p (n d)")[:, bass.ds(s, 1)]
                nc.scalar.activation(h[k % 2][:], h[k % 2][:], ACT.Copy, scale=col).then_inc(scaled, 1)

            def middle(b):
                round_jobs(f"pooledT.#@{b}", hlA)
                round_jobs(f"vWT.#@{b}", hlB)
                act.wait_ge(in_stage[1], LANDED[f"cW@{b}"])
                act.wait_ge(scores_ready, (b + 1) * STEPS)
                round_tiles(stage[1], hlC)
                round_jobs(f"ctx_to_v.#@{b}", hlD)
                round_jobs(f"oWT.#@{b}", hlE)
                round_evacuated(f"attn.#@{b}", qT[:, b], hlB)
                round_jobs(f"inT0.#@{b}", hlC)
                round_jobs(f"inT1.#@{b}", hlD)
                round_evacuated(f"normT.#@{b}", yT, hlA)
                act.wait_ge(evacuated, JOB[f"z.3@{b}"] + 1)
                nc.scalar.activation(yT[:], zT[:], ACT.Exp, scale=-1.0).then_inc(z_exp, 1)

            def project_out(b):
                round_jobs(f"outT.#@{b}", hlB)
                act.wait_ge(gated, b + 1)
                round_tiles(yT, hlA)

            def mix_experts(b, scan):
                round_jobs(f"ffnT.#@{b}", hlA)
                job0 = JOB[f"expert.0@{b}"]
                loads = [LANDED[f"W0@{b}"], LANDED[f"W1@{b}"]]

                def weights(e_par, k, landed, used):
                    act.wait_ge(in_stage[e_par], landed)
                    act.wait_ge(filled, used)
                    nc.scalar.activation((hlC, hlD)[e_par][:, 0, k, :], stage[e_par][:, k, :], ACT.Copy).then_inc(split_hi, 1)

                def trip(t, first, last):
                    for u in range(UN):
                        if not (last and u >= T):
                            par = 1 - u // T
                            weights(par, u % T, (t + u // T) * 16 + loads[par], t * UN + (job0 + u // T * T))
                        if scan:
                            for v in range(2):
                                scale_state(1, t * (2 * UN) + (2 * u + v), v)

                for k in range(T):
                    weights(0, k, loads[0], job0 - 2 * T)
                trips(act, MTRIPS, trip)

            prepare()
            attention(0, len(PREP_JOBS), False)
            middle(0)
            attention(1, JOB["z.3@0"] + 1, True)
            project_out(0)
            middle(1)
            mix_experts(0, True)
            project_out(1)
            mix_experts(1, False)

        @block.vector
        def _(dve):
            links = [0]

            def link(ins):
                links[0] += 1
                ins.then_inc(link_done, 1)
                dve.wait_ge(link_done, links[0])

            def lo_job(name, slot, k):
                dve.wait_ge(rounded, ROUND[name] + 1)
                nc.vector.tensor_tensor(slot[:, 1, k, :], bank[JOB[name] % NBANK][:], slot[:, 0, k, :].bitcast(F32),
                                        ALU.subtract).then_inc(evacuated, 1)

            def lo_jobs(name, slot):
                for k in range(T):
                    lo_job(name.replace("#", str(k)), slot, k)

            def normalize(src, dst):
                for t in range(T):
                    last = nc.vector.bn_stats(bnst[:, t, :], src[:, t, :])
                link(last)
                for t in range(T):
                    last = nc.vector.bn_aggr(mv[:, t, :], bnst[:, t, :])
                link(last)
                link(nc.vector.tensor_scalar(var[:], mv[:, :, 1], EPS, None, ALU.add))
                link(nc.vector.tensor_scalar(seed[:], var[:].bitcast(I32), 1, None, ALU.logical_shift_right))
                link(nc.vector.tensor_scalar(rstd[:].bitcast(I32), seed[:], -1.0, RSQRT_SEED, ALU.mult, ALU.add))
                for _k in range(3):
                    link(nc.vector.tensor_tensor(newton[:], rstd[:], rstd[:], ALU.mult))
                    link(nc.vector.scalar_tensor_tensor(newton[:], newton[:], -0.5, var[:], ALU.mult, ALU.mult))
                    link(nc.vector.scalar_tensor_tensor(rstd[:], newton[:], 1.5, rstd[:], ALU.add, ALU.mult))
                for t in range(T):
                    last = nc.vector.tensor_scalar(dst[:, t, :], src[:, t, :], mv[:, t, 0:1], rstd[:, t:t + 1],
                                                   ALU.subtract, ALU.mult)
                return last

            def folded_bias(dst, w, v, own):
                for t in range(T):
                    link(nc.vector.tensor_tensor_reduce(h[0][:], w[:, t, :], v[:], 1.0, 0.0, ALU.mult, ALU.add,
                                                        dst[:, t:t + 1]))
                return nc.vector.tensor_tensor(dst[:], dst[:], vecs[:, own:own + T], ALU.add)

            def prepare():
                nc.vector.memset(desc[:], 1.0).then_inc(desc_ready, 1)
                for e in range(E - 1):
                    dve.wait_ge(desc_ready, e + 1)
                    nc.vector.memset(desc[:, e:e + 1], float(E - e)).then_inc(desc_ready, 1)
                dve.wait_ge(in_x[0], 16)
                normalize(xb[:, 0], rows).then_inc(rows_ready, 1)
                dve.wait_ge(filled, JOB["vectors"] + 1)
                nc.vector.tensor_copy(vecs[:], bank[JOB["vectors"] % NBANK][:, 0:32]).then_inc(evacuated, 1)
                dve.wait_ge(evacuated, 1)
                nc.vector.tensor_copy(dtv[:], vecs[:, 28:32]).then_inc(vectors_ready, 1)
                lo_jobs("xT0.#", hlD)
                lo_jobs("qWT.#", hlA)
                dve.wait_ge(in_bias, 32)
                link(folded_bias(qbias, stage[0], probs[0], 0))
                dve.wait_ge(in_x[1], 16)
                normalize(xb[:, 1], resid).then_inc(rows_ready, 1)
                lo_jobs("x_to_q.#", hlC)
                for k in range(T):
                    queries(0, k)
                lo_jobs("xT1.#", hlD)
                for k in range(T):
                    queries(1, k)
                dve.wait_ge(in_k, 16)
                folded_bias(kbias, uT, probs[1], 4).then_inc(kbias_ready, 1)
                lo_jobs("kWT.#", hlD)
                dve.wait_ge(in_v, 16)
                link(folded_bias(vbias, yT, probs[1], 8))
                lo_jobs("q_to_ctx.#", hlC)
                lo_jobs("qc0.#", hlD)
                for k in range(T):
                    dve.wait_ge(filled, JOB[f"qc1.{k}"] + 1)
                    nc.vector.tensor_copy(qc1[:, k, :], bank[JOB[f"qc1.{k}"] % NBANK][:]).then_inc(evacuated, 1)
                dve.wait_ge(filled, JOB["key_bias"] + 1)
                nc.vector.tensor_copy(kq[:], bank[JOB["key_bias"] % NBANK][:, 0:B * T]).then_inc(evacuated, 1)

            def queries(b, k):
                dve.wait_ge(filled, JOB[f"q{b}.{k}"] + 1)
                nc.vector.tensor_scalar(qT[:, b, k, :], bank[JOB[f"q{b}.{k}"] % NBANK][:], qbias[:, k:k + 1], None,
                                        ALU.add).then_inc(evacuated, 1)

            def small_parameters():
                dve.wait_ge(in_small, 16 * 5)
                link(nc.vector.tensor_copy(gate_hl[:, 0], gate_raw[:]))
                nc.vector.tensor_tensor(gate_hl[:, 1], gate_raw[:], gate_hl[:, 0].bitcast(F32),
                                        ALU.subtract).then_inc(gate_ready, 1)
                dve.wait_ge(ssm_exp, 2)
                link(nc.vector.tensor_scalar(dtv[:], dtv[:], 1e-4, 1.0, ALU.max, ALU.min))
                ea, w, p, dtb = (ssm_w[:, k] for k in range(4))
                for t in range(T):
                    last = nc.vector.tensor_scalar(w[:, t, :], ea[:, t, :], dtv[:, t:t + 1], -1.0, ALU.mult, ALU.mult)
                link(last)
                link(nc.vector.tensor_tensor(dtb[:], ssm_in[:, 1], ssm_in[:, 2], ALU.mult))
                for t in range(T):
                    last = nc.vector.tensor_scalar(cbdt[:, :, t], dtb[:, t, :], dtv[:, t:t + 1], None, ALU.mult)
                link(last)
                link(nc.vector.tensor_scalar(w[:], w[:], -30.0, 0.5 ** EXPM1_DOUBLINGS, ALU.max, ALU.mult))
                link(nc.vector.tensor_scalar(p[:], w[:], 0.2, 1.0, ALU.mult, ALU.add))
                for k in (4.0, 3.0, 2.0):
                    link(nc.vector.scalar_tensor_tensor(p[:], p[:], 1.0 / k, w[:], ALU.mult, ALU.mult))
                    link(nc.vector.tensor_scalar(p[:], p[:], 1.0, None, ALU.add))
                link(nc.vector.tensor_tensor(p[:], p[:], w[:], ALU.mult))
                for _k in range(EXPM1_DOUBLINGS):
                    link(nc.vector.scalar_tensor_tensor(p[:], p[:], 2.0, p[:], ALU.add, ALU.mult))
                link(nc.vector.tensor_scalar(p[:], p[:], 1.0, 1e-8, ALU.add, ALU.max))
                link(nc.vector.tensor_scalar(abar[:].rearrange("p n t -> p t n"), p[:], 1.0 - 1e-8, None, ALU.min))

            def attention(b, scan):
                base = b * STEPS

                def maxima(t, u):
                    par, q = u // T % 2, u % T
                    col = slice(q, q + 1)
                    dve.wait_ge(scores_ready, t * UN + (base + u + 1))
                    nc.vector.tensor_reduce(mx[:, col], sbank[u % 2][:], AX_X, ALU.max).then_inc(stat_done, 1)
                    dve.wait_ge(stat_done, t * (2 * UN) + (2 * base + 2 * u + 1))
                    nc.vector.tensor_scalar(mrun[:, 1 - par, col], mx[:, col], kq[:, b * T + q:b * T + q + 1], mrun[:, par, col],
                                            ALU.add, ALU.max).then_inc(stat_done, 1)
                    dve.wait_ge(stat_done, t * (2 * UN) + (2 * base + 2 * u + 2))
                    nc.vector.tensor_scalar(nbias[:, col], mrun[:, 1 - par, col], kq[:, b * T + q:b * T + q + 1], -SCALE,
                                            ALU.subtract, ALU.mult).then_inc(max_ready, 1)
                    nc.vector.tensor_tensor(dmax[:, col], mrun[:, par, col], mrun[:, 1 - par, col],
                                            ALU.subtract).then_inc(dmax_ready, 1)

                def turned_probs(t, u):
                    dve.wait_ge(pT_hi, t * UN + (base + u + 1))
                    nc.vector.tensor_tensor(probsT[u % 2][:, 1], tbank[u % 2][:].rearrange("p (j q) -> p j q", j=T),
                                            probsT[u % 2][:, 0].bitcast(F32), ALU.subtract).then_inc(pT_split, 1)

                def context_block(t, u):
                    par, dd = (u // T + 1) % 2, u % T
                    dve.wait_ge(cT_hi, t * UN + (base + u + T + 1))
                    nc.vector.tensor_tensor(ctxT[par][:, 1, dd, :], cbank[dd % 2][:], ctxT[par][:, 0, dd, :].bitcast(F32),
                                            ALU.subtract).then_inc(cT_split, 1)

                def sums(t, u):
                    q = u % T
                    col = slice(q, q + 1)
                    dve.wait_ge(alpha_ready, t * UN + (base + u + 1))
                    dve.wait_ge(probs_ready, t * UN + (base + u + 1))
                    wait_pos(dve, sums_updated, 2 * base, t * (2 * UN) + 2 * (u - 3))
                    nc.vector.scalar_tensor_tensor(lsum[:, col], lsum[:, col], alpha[:, col], rsum[:, col],
                                                   ALU.mult, ALU.add).then_inc(sums_updated, 1)
                    dve.wait_ge(pv_ready, t * UN + (base + u + 1))
                    nc.vector.scalar_tensor_tensor(rows[:, q, :], rows[:, q, :], alpha[:, col], obank[u % 2][:],
                                                   ALU.mult, ALU.add).then_inc(sums_updated, 1)

                def trip(t, first, last):
                    for u in range(UN):
                        maxima(t, u)
                        if not (first and u < 1):
                            turned_probs(*((t, u - 1) if u else (t - 1, UN - 1)))
                        if not (last and u >= T):
                            context_block(t, u)
                        if scan:
                            scan_state(0, t * UN + u, u, first and u < 2)
                        if not (first and u < 2):
                            sums(*((t, u - 2) if u >= 2 else (t - 1, u - 2 + UN)))

                for dd in range(T):
                    dve.wait_ge(cT_hi, base + dd + 1)
                    nc.vector.tensor_tensor(ctxT[0][:, 1, dd, :], cbank[dd % 2][:], ctxT[0][:, 0, dd, :].bitcast(F32),
                                            ALU.subtract).then_inc(cT_split, 1)
                trips(dve, TRIPS, trip)
                turned_probs(TRIPS - 1, UN - 1)
                sums(TRIPS - 1, UN - 2)
                sums(TRIPS - 1, UN - 1)

            def clear_sums(b):
                dve.wait_ge(filled, JOB["xT0.3" if b == 0 else "normT.3@0"] + 1)
                nc.vector.memset(rows[:], 0.0).then_inc(sums_zeroed, 1)
                nc.vector.memset(lsum[:], 0.0).then_inc(sums_zeroed, 1)
                nc.vector.memset(mrun[:, 0], LOWEST).then_inc(sums_zeroed, 1)
                dve.wait_ge(sums_zeroed, 3 * (b + 1))

            def scan_state(b, s, k, first):
                if not first:
                    dve.wait_ge(summed, s + (b * SCANS - 1))
                col = abar[:].rearrange("p n d -> p (n d)")[:, bass.ds(s, 1)]
                nc.vector.tensor_tensor_scan(h[k % 2][:], col.to_broadcast([P, S]), uT[:, k % T, :], 0.0,
                                             ALU.mult, ALU.add).then_inc(scanned, 1)

            def pool_context(b):
                dve.wait_ge(sums_updated, 2 * (b + 1) * STEPS)
                link(nc.vector.reciprocal(lsum[:], lsum[:]))
                for t in range(T):
                    last = nc.vector.tensor_scalar(rows[:, t, :], rows[:, t, :], lsum[:, t:t + 1], None, ALU.mult)
                last.then_inc(rows_ready, 1)

            def middle(b):
                pool_context(b)
                lo_jobs(f"pooledT.#@{b}", hlA)
                lo_jobs(f"vWT.#@{b}", hlB)
                lo_jobs(f"ctx_to_v.#@{b}", hlD)
                lo_jobs(f"oWT.#@{b}", hlE)
                for k in range(T):
                    name = f"attn.{k}@{b}"
                    dve.wait_ge(filled, JOB[name] + 1)
                    nc.vector.scalar_tensor_tensor(qT[:, b, k, :], bank[JOB[name] % NBANK][:], vbias[:, k:k + 1], qT[:, b, k, :],
                                                   ALU.add, ALU.add).then_inc(evacuated, 1)
                dve.wait_ge(x_biased, 1)
                for k in range(T):
                    name = f"x_attn.{k}@{b}"
                    dve.wait_ge(filled, JOB[name] + 1)
                    nc.vector.tensor_tensor(xb[:, b, k, :], bank[JOB[name] % NBANK][:], xb[:, b, k, :],
                                            ALU.add).then_inc(evacuated, 1)
                dve.wait_ge(evacuated, JOB[f"x_attn.3@{b}"] + 1)
                link(normalize(xb[:, b], resid))
                normalize(resid, rows).then_inc(rows_ready, 1)
                lo_jobs(f"inT0.#@{b}", hlC)
                lo_jobs(f"inT1.#@{b}", hlD)
                for k in range(T):
                    name = f"normT.{k}@{b}"
                    dve.wait_ge(filled, JOB[name] + 1)
                    nc.vector.tensor_scalar(yT[:, k, :], bank[JOB[name] % NBANK][:], vecs[:, 20 + k:21 + k], vecs[:, 24 + k:25 + k],
                                            ALU.mult, ALU.add).then_inc(evacuated, 1)
                for name, dst, own in (("u", uT, 12), ("z", zT, 16)):
                    for k in range(T):
                        job = f"{name}.{k}@{b}"
                        dve.wait_ge(filled, JOB[job] + 1)
                        nc.vector.tensor_scalar(dst[:, k, :], bank[JOB[job] % NBANK][:], vecs[:, own + k:own + k + 1], None,
                                                ALU.add).then_inc(evacuated, 1)
                dve.wait_ge(z_exp, b + 1)
                link(nc.vector.tensor_scalar(yT[:], yT[:], 1.0, None, ALU.add))
                link(nc.vector.reciprocal(yT[:], yT[:]))
                link(nc.vector.tensor_tensor(zT[:], zT[:], yT[:], ALU.mult))
                nc.vector.memset(yT[:], 0.0).then_inc(y_zeroed, 1)

            def project_out(b):
                dve.wait_ge(summed, (b + 1) * SCANS)
                nc.vector.tensor_tensor(yT[:], yT[:], zT[:], ALU.mult).then_inc(gated, 1)
                lo_jobs(f"outT.#@{b}", hlB)
                dve.wait_ge(resid_biased, b + 1)
                for k in range(T):
                    name = f"x_ssm.{k}@{b}"
                    dve.wait_ge(filled, JOB[name] + 1)
                    nc.vector.tensor_tensor(resid[:, k, :], bank[JOB[name] % NBANK][:], resid[:, k, :],
                                            ALU.add).then_inc(evacuated, 1)
                    dve.wait_ge(evacuated, JOB[name] + 1)
                    link(nc.vector.tensor_scalar(resid[:, k, :], resid[:, k, :], 10.0, -10.0, ALU.min, ALU.max))
                    link(nc.vector.tensor_tensor(xb[:, b, k, :], xb[:, b, k, :], resid[:, k, :], ALU.add))
                normalize(xb[:, b], qT[:, b]).then_inc(rows_ready, 1)

            def mix_experts(b, scan):
                lo_jobs(f"ffnT.#@{b}", hlA)
                name = f"logits@{b}"
                dve.wait_ge(filled, JOB[name] + 1)
                for k in range(T):
                    last = nc.vector.tensor_tensor(logit[:, k, :], bank[JOB[name] % NBANK][:, k * E:(k + 1) * E], gbB[:], ALU.add)
                last.then_inc(evacuated, 1)
                dve.wait_ge(evacuated, JOB[name] + 1)
                link(nc.vector.tensor_reduce(lmax[:, 0], logit[:], AX_X, ALU.max))
                dve.wait_ge(desc_ready, E)
                for k in range(T):
                    last = nc.vector.scalar_tensor_tensor(pick[:, k, :], logit[:, k, :], lmax[:, 0, k:k + 1], desc[:],
                                                          ALU.is_equal, ALU.mult)
                link(last)
                link(nc.vector.tensor_reduce(lmax[:, 1], pick[:], AX_X, ALU.max))
                for k in range(T):
                    last = nc.vector.tensor_scalar(onehot[:, k, :], pick[:, k, :], lmax[:, 1, k:k + 1], None, ALU.is_equal)
                last.then_inc(onehot_ready, 1)
                name = f"onehotT@{b}"
                dve.wait_ge(filled, JOB[name] + 1)
                nc.vector.tensor_copy(onehotT[:], bank[JOB[name] % NBANK][0:E, :]).then_inc(evacuated, 1)
                for k in range(T):
                    name = f"expert_bias.{k}@{b}"
                    dve.wait_ge(filled, JOB[name] + 1)
                    nc.vector.tensor_tensor(xb[:, b, k, :], bank[JOB[name] % NBANK][:], xb[:, b, k, :],
                                            ALU.add).then_inc(evacuated, 1)
                job0 = JOB[f"expert.0@{b}"]
                weight = onehot[:].rearrange("p t e -> p (t e)")

                def trip(t, first, last):
                    for u in range(UN):
                        k = u % T
                        dve.wait_ge(filled, t * UN + (job0 + u + 1))
                        dve.wait_ge(evacuated, t * UN + (job0 + u + 1 - T))
                        nc.vector.scalar_tensor_tensor(xb[:, b, k, :], bank[(job0 + u) % NBANK][:],
                                                       weight[:, bass.ds(t * 2 + (k * E + u // T), 1)], xb[:, b, k, :],
                                                       ALU.mult, ALU.add).then_inc(evacuated, 1)
                        if scan:
                            for v in range(2):
                                scan_state(1, t * (2 * UN) + (2 * u + v), 2 * u + v, False)

                trips(dve, MTRIPS, trip)

            prepare()
            small_parameters()
            clear_sums(0)
            attention(0, False)
            middle(0)
            clear_sums(1)
            attention(1, True)
            project_out(0)
            middle(1)
            mix_experts(0, True)
            project_out(1)
            mix_experts(1, False)

        @block.gpsimd
        def _(pool):
            nc.gpsimd.memset(ident[:], 0.0).then_inc(ident_zero, 1)
            pool.wait_ge(ident_zero, 1)
            nc.gpsimd.affine_select(out=ident[:], in_=ident[:], compare_op=ALU.not_equal, fill=1.0, base=0,
                                    pattern=[[-1, P]], channel_multiplier=1).then_inc(ident_ready, 1)

            def lo_tiles(name, src, slot):
                for k in range(T):
                    pool.wait_ge(split_hi, SPLIT[name] + k + 1)
                    nc.gpsimd.tensor_tensor(slot[:, 1, k, :], src[:, k, :], slot[:, 0, k, :].bitcast(F32),
                                            ALU.subtract).then_inc(split_done, 1)

            def add_state(b, s, k, first):
                pool.wait_ge(scaled, s + (b * SCANS + 1))
                if not first:
                    pool.wait_ge(summed, s + (b * SCANS - T + 1))
                nc.gpsimd.tensor_tensor(yT[:, k % T, :], yT[:, k % T, :], h[k % 2][:], ALU.add).then_inc(summed, 1)

            def attention(b, scan):
                base = b * STEPS

                def natural(t, u):
                    par, j = (u + 2) // T % 2, (u + 2) % T
                    pool.wait_ge(nat_hi, t * UN + (base + u + 2 + 1))
                    nc.gpsimd.tensor_tensor(nat[par][:, 1, j, :], stage[par][:, j, :], nat[par][:, 0, j, :].bitcast(F32),
                                            ALU.subtract).then_inc(nat_split, 1)

                def trip(t, first, last):
                    for u in range(UN):
                        if not (last and u + 2 >= UN):
                            natural(t, u)
                        if scan:
                            add_state(0, t * UN + u, u, first and u < T)

                if b == 1:
                    lo_tiles("qc1", qc1, hlD)
                for j in range(2):
                    pool.wait_ge(nat_hi, base + j + 1)
                    nc.gpsimd.tensor_tensor(nat[0][:, 1, j, :], stage[0][:, j, :], nat[0][:, 0, j, :].bitcast(F32),
                                            ALU.subtract).then_inc(nat_split, 1)
                trips(pool, TRIPS, trip)

            def middle(b):
                lo_tiles(f"cW@{b}", stage[1], hlC)
                lo_tiles(f"attn@{b}", qT[:, b], hlB)
                pool.wait_ge(rows_ready, ROWS[f"norm@{b}"])
                for t in range(T):
                    last = nc.gpsimd.tensor_tensor(resid[:, t, :], resid[:, t, :], outbB[:], ALU.add)
                last.then_inc(resid_biased, 1)
                lo_tiles(f"norm@{b}", yT, hlA)
                pool.wait_ge(y_zeroed, b + 1)

            def mix_experts(b, scan):
                split0 = SPLIT[f"W0@{b}"]

                def weights(par, k, count):
                    pool.wait_ge(split_hi, count)
                    nc.gpsimd.tensor_tensor((hlC, hlD)[par][:, 1, k, :], stage[par][:, k, :],
                                            (hlC, hlD)[par][:, 0, k, :].bitcast(F32), ALU.subtract).then_inc(split_done, 1)

                def trip(t, first, last):
                    for u in range(UN):
                        if not (last and u >= T):
                            weights(1 - u // T, u % T, t * UN + (split0 + T + u + 1))
                        if scan:
                            for v in range(2):
                                add_state(1, t * (2 * UN) + (2 * u + v), 2 * u + v, first and 2 * u + v < T)

                for k in range(T):
                    weights(0, k, split0 + k + 1)
                trips(pool, MTRIPS, trip)

            lo_tiles("hW", stage[1], hlB)
            lo_tiles("q0", qT[:, 0], hlA)
            lo_tiles("cW", zT, hlE)
            lo_tiles("q1", qT[:, 1], hlB)
            pool.wait_ge(in_small, 16 * 5)
            pool.wait_ge(rows_ready, ROWS["x1"])
            for b in range(B):
                for t in range(T):
                    last = nc.gpsimd.tensor_tensor(xb[:, b, t, :], xb[:, b, t, :], obB[:], ALU.add)
            last.then_inc(x_biased, 1)
            attention(0, False)
            middle(0)
            attention(1, True)
            lo_tiles("gated@0", yT, hlA)
            middle(1)
            mix_experts(0, True)
            lo_tiles("gated@1", yT, hlA)
            mix_experts(1, False)


_INS = ["x", "ctx_1024", "L0_xattn_hW", "L0_xattn_hb", "L0_xattn_cW", "L0_xattn_cb", "L0_xattn_qW", "L0_xattn_qb",
        "L0_xattn_kW", "L0_xattn_kb", "L0_xattn_vW", "L0_xattn_vb", "L0_xattn_oW", "L0_xattn_ob", "L0_attn_A_log",
        "L0_attn_B_param", "L0_attn_C_param", "L0_attn_log_dt", "L0_attn_in_w", "L0_attn_in_b", "L0_attn_out_w",
        "L0_attn_out_b", "L0_attn_ln_g", "L0_attn_ln_b", "L0_ffn_gate_w", "L0_ffn_gate_b", "L0_ffn_expert_w",
        "L0_ffn_expert_b"]
_OUTS = [((B, S, D), "float32")]


def kernel(**inputs):
    import numpy as _np
    import concourse.bacc as _bacc
    from concourse import mybir as _mybir
    from concourse.bass_utils import run_bass_kernel_spmd as _run

    nc = _bacc.Bacc("TRN2", target_bir_lowering=False, num_devices=1)
    arrays, args = {}, []
    for name in _INS:
        a = _np.ascontiguousarray(inputs[name])
        arrays[f"in_{name}_dram"] = a
        args.append(nc.dram_tensor(f"in_{name}_dram", a.shape, _mybir.dt.from_np(a.dtype), kind="ExternalInput").ap())
    for i, (shape, dtype) in enumerate(_OUTS):
        dt = _mybir.dt.from_np(_np.dtype(dtype))
        args.append(nc.dram_tensor(f"out_{i}_dram", shape, dt, kind="ExternalOutput").ap())
    build(nc, *args)
    r = _run(nc, [arrays], core_ids=[0])
    got = tuple(r.results[0][f"out_{i}_dram"] for i in range(len(_OUTS)))
    return got[0]
```

```python
from contextlib import ExitStack

import concourse.bass as bass
from concourse import mybir

F32 = mybir.dt.float32
F32R = mybir.dt.float32r
I32 = mybir.dt.int32
ALU = mybir.AluOpType
ACT = mybir.ActivationFunctionType
AX_X = mybir.AxisListType.X

P = 128
B, S, D = 2, 512, 512
T = D // P
L = 8192
BLOCKS = L // P - T
CH = 512
NCH = L // CH
NS = 16
E = 8
UN = 8
STEPS = NCH * T
TRIPS = STEPS // UN
SCANS = NS * T
MTRIPS = E * T // UN
AHEAD = ((0, 1), (2, 3), (), ())
NBANK = 8
EPS = 1e-5
SCALE = float(D) ** -0.5
LOWEST = -3.0e38
PASSES = ((0, 0), (0, 1), (1, 0))
EXPM1_DOUBLINGS = 8
RSQRT_SEED = float(0x5F3759DF)



def tiles(*names):
    return [f"{n}.{k}" for n in names for k in range(T)]


def mid_jobs(b):
    names = [f"{n}@{b}" for n in tiles("inT0", "pooledT", "inT1")]
    names += [f"{n}@0" for n in tiles("outT")] * b
    names += [f"{n}@{b}" for n in tiles("x_attn")]
    names += [f"{n}@0" for n in tiles("x_ssm")] * b
    names += [f"{n}@{b}" for n in tiles("normT", "u")]
    names += [f"{n}@1" for n in tiles("ctx0T")] * (1 - b)
    names += [f"{n}@{b}" for n in tiles("z")]
    return names + [f"{n}@0" for n in tiles("ffnT") + ["logits", "logit_columns"]] * b


def expert_jobs(b):
    return [f"onehotT@{b}"] + [f"{n}@{b}" for n in tiles("expert_bias") + [f"expert.{n}" for n in range(E * T)]]


PREP_JOBS = (tiles("qWT") + ["vectors"] + tiles("xT0", "x_to_q", "kWT", "q0", "xT1", "q_to_ctx", "q1", "qc0", "vWT", "qc1")
             + ["key_row.0", "key_row.1", "key_bias"] + tiles("ctx_to_v", "oWT") + ["x_bias"] + tiles("ctx_to_x", "qo0", "ctx0T@0", "qo1"))
PREP_JOBS = [n if "@" not in n else "ctx0T" + n[n.index("."):] + "@0" for n in PREP_JOBS]
JOBS = (PREP_JOBS + mid_jobs(0) + mid_jobs(1) + expert_jobs(0)
        + [f"{n}@1" for n in tiles("outT", "x_ssm", "ffnT") + ["logits", "logit_columns"]] + expert_jobs(1))
JOB = {name: n for n, name in enumerate(JOBS)}
AFTER = [JOB[f"inT0.0@{b}"] for b in range(B)]
BANK = [(n - AFTER[int(n >= AFTER[1])] + 6) % NBANK for n in range(len(JOBS))]
ROUNDED_KINDS = ("xT0", "xT1", "qWT", "x_to_q", "kWT", "q_to_ctx", "qc0", "vWT", "ctx_to_v", "oWT", "ctx_to_x",
                 "pooledT", "inT0", "inT1", "outT", "ffnT", "normT", "ctx0T")
ROUND = {name: k for k, name in enumerate(n for n in JOBS if n.split(".")[0] in ROUNDED_KINDS)}
SPLITS = ["hW", "cW", "qc1"] + [f"W{e}@{b}" for b in range(B) for e in range(E)]
SPLIT = {name: T * n for n, name in enumerate(SPLITS)}
KEPT = {name: T * n for n, name in enumerate(["q0", "q1", "gated@0", "gated@1"])}
ROWS = {name: 2 * n + 1 for n, name in enumerate(["x0", "x1", "pooled@0", "norm@0", "pooled@1", "norm@1", "ffn@0", "ffn@1"])}
LOADS = [("qW", 0), ("hW", 1), ("oW", 0)]
for _b in range(B):
    LOADS += [(f"chunk{_c}@{_b}", _c % 2) for _c in range(NCH)] + [(f"in0@{_b}", 0), (f"in1@{_b}", 1)]
LOADS += [("out_w@0", 0)]
for _b in range(B):
    LOADS += [(f"W{_e}@{_b}", _e % 2) for _e in range(E)] + [("out_w@1", 0)] * (_b == 0)
BUF, LANDED = {}, {}
_seen = [0, 0]
for _name, _buf in LOADS:
    _seen[_buf] += 1
    BUF[_name], LANDED[_name] = _buf, 16 * _seen[_buf]


def build(nc, x, ctx_in, hW, hb, cW, cb, qW, qb, kW, kb, vW, vb, oW, ob, A_log, B_param, C_param, log_dt,
          in_w, in_b, out_w, out_b, ln_g, ln_b, gate_w, gate_b, expert_w, expert_b, out):
    with ExitStack() as ctx:
        def sb(name, shape, dt=F32):
            return ctx.enter_context(nc.sbuf_tensor(name, shape, dt))

        def sem(name):
            return ctx.enter_context(nc.semaphore(name))

        hlA, hlB, hlC, hlD, hlE, hlF = (sb(f"hl_{n}", [P, 2, T, D], F32R) for n in "ABCDEF")
        nat = [hlA, hlF]
        ctxT = [hlB, hlC]
        qc_hl = hlD
        ctx_to_x = hlE
        weights_hl = [hlA, hlB]
        vbias_hl = sb("vbias_hl", [P, 2, T], F32R)
        kbias_hl = sb("kbias_hl", [P, 2, T, 2], F32R)
        probsT = [sb(f"probsT{n}", [P, 2, T, P], F32R) for n in range(2)]
        stage = [sb(f"stage{n}", [P, T, D]) for n in range(2)]
        probs = [sb(f"probs{n}", [P, CH]) for n in range(2)]
        rows = sb("rows", [P, T, D])
        qc1 = sb("qc1", [P, T, S])
        xb = sb("xb", [P, B, T, D])
        uT = sb("uT", [P, T, S])
        zT = sb("zT", [P, T, S])
        yT = sb("yT", [P, T, S])
        h = [sb(f"h{n}", [P, S]) for n in range(2)]
        even_h = [[h[0], h[0]], [h[0], probs[0]]]
        resid0 = sb("resid0", [P, T, D])
        resid = [resid0, qc1]
        qT = [rows, resid0]
        ident = sb("ident", [P, P])
        obB = sb("obB", [P, D])
        outbB = sb("outbB", [P, D])
        eb = sb("eb", [E, D])
        onehotT = sb("onehotT", [E, T * P])
        key_row = [h[1], onehotT]
        vrows = sb("vrows", [32, P])
        vecs = sb("vecs", [P, 32])
        gate_raw = sb("gate_raw", [P, T, E])
        gate_hl = sb("gate_hl", [P, 2, T, E], F32R)
        gbB = sb("gbB", [P, E])
        desc = sb("desc", [P, E])
        logit = sb("logit", [P, T, E])
        pick = sb("pick", [P, T, E])
        onehot = sb("onehot", [P, T, E])
        lmax = sb("lmax", [P, 2, T])
        bnst = sb("bnst", [P, T, 6])
        mv = sb("mv", [P, T, 2])
        rstd = sb("rstd", [P, 2, T])
        var = sb("var", [P, 2, T])
        seed = sb("seed", [P, 2, T], I32)
        newton = sb("newton", [P, 2, T])
        inbias = sb("inbias", [P, 2 * T])
        qbias = sb("qbias", [P, T])
        kbias = sb("kbias", [P, T])
        vbias = sb("vbias", [P, T])
        kq = sb("kq", [P, B * T])
        mrun = sb("mrun", [P, 2, T])
        mx = sb("mx", [P, T])
        nbias = sb("nbias", [P, T])
        dmax = sb("dmax", [P, T])
        alpha = sb("alpha", [P, T])
        rsum = sb("rsum", [P, T])
        lsum = sb("lsum", [P, T])
        ssm_in = sb("ssm_in", [P, 3, T, NS])
        ssm_w = sb("ssm_w", [P, 4, T, NS])
        dtv = sb("dtv", [P, T])
        abar = sb("abar", [P, NS, T])
        cbdt = sb("cbdt", [P, NS, T])

        bank = [ctx.enter_context(nc.psum_tensor(f"bank{n}", [P, 512], F32)) for n in range(NBANK)]
        sbank, tbank, obank, cbank = bank[0:2], bank[2:4], bank[4:6], bank[6:8]

        in_x0, in_x1 = [sem(f"in_x0_{n}") for n in range(2)], sem("in_x1")
        in_stage = [sem(f"in_stage{n}") for n in range(2)]
        in_k, in_c, in_v, in_vec, in_bias, in_ssm, in_small = (sem(n) for n in (
            "in_k", "in_c", "in_v", "in_vec", "in_bias", "in_ssm", "in_small"))
        stored = sem("stored")
        ident_zero, ident_ready, desc_ready = sem("ident_zero"), sem("ident_ready"), sem("desc_ready")
        filled, rounded, evacuated = sem("filled"), sem("rounded"), sem("evacuated")
        split_hi, split_done = sem("split_hi"), sem("split_done")
        gated, kept_hi, kept_split = sem("gated"), sem("kept_hi"), sem("kept_split")
        rows_ready = sem("rows_ready")
        link_done = sem("link_done")
        vectors_ready, ssm_exp, gate_ready, kbias_ready = (sem(n) for n in (
            "vectors_ready", "ssm_exp", "gate_ready", "kbias_ready"))
        vbias_ready, bias_row_ready = sem("vbias_ready"), sem("bias_row_ready")
        x_biased, resid_ready, resid_biased = sem("x_biased"), sem("resid_ready"), sem("resid_biased")
        z_gated, y_zeroed, onehot_ready = sem("z_gated"), sem("y_zeroed"), sem("onehot_ready")
        sums_zeroed, inbias_ready, in_lnb = sem("sums_zeroed"), sem("inbias_ready"), sem("in_lnb")
        scores_ready, stat_done, max_ready, dmax_ready, probs_ready, alpha_ready = (sem(n) for n in (
            "scores_ready", "stat_done", "max_ready", "dmax_ready", "probs_ready", "alpha_ready"))
        pT_ready, pT_hi, pT_split = sem("pT_ready"), sem("pT_hi"), sem("pT_split")
        cT_ready, cT_hi, cT_split = sem("cT_ready"), sem("cT_hi"), sem("cT_split")
        nat_hi, nat_split = sem("nat_hi"), sem("nat_split")
        pv_ready, sums_updated = sem("pv_ready"), sem("sums_updated")
        scanned, scaled, summed = sem("scanned"), sem("scaled"), sem("summed")
        odd_scanned, odd_summed = sem("odd_scanned"), sem("odd_summed")

        block = ctx.enter_context(nc.Block())

        def matrix(w):
            return w.rearrange("(t p) n -> p t n", p=P)

        def across(v):
            return v.rearrange("(a n) -> a n", a=1).partition_broadcast(P)

        ctx_rows = ctx_in.rearrange("b (c p j) d -> (b c) p j d", p=P, j=T)
        experts = expert_w.rearrange("e (t p) n -> e p t n", p=P)

        def wait_pos(eng, s, base, value):
            if not isinstance(value, int) or value > 0:
                eng.wait_ge(s, value + base)

        def trips(eng, n, body):
            body(0, True, False)
            with eng.Fori(1, n - 1) as t:
                body(t, False, False)
            body(n - 1, False, True)

        @block.sync
        def _(sp):
            def load(name, src):
                sp.dma_start(stage[BUF[name]][:], src).then_inc(in_stage[BUF[name]], 16)

            for pair in range(2):
                two = slice(2 * pair, 2 * pair + 2)
                sp.dma_start(xb[:, 0, two], matrix(x[0])[:, two]).then_inc(in_x0[pair], 16)
                if pair == 0:
                    load("qW", matrix(qW))
            load("hW", matrix(hW))
            sp.dma_start(zT[:], matrix(cW)).then_inc(in_c, 16)
            sp.dma_start(uT[:], matrix(kW)).then_inc(in_k, 16)
            sp.dma_start(xb[:, 1], matrix(x[1])).then_inc(in_x1, 16)
            sp.dma_start(yT[:], matrix(vW)).then_inc(in_v, 16)

            def attention_loads(b):
                base, blocks = b * STEPS, b * BLOCKS
                sp.wait_ge(filled, JOB[f"ctx0T.3@{b}"] + 1)
                for c in range(2, NCH):
                    if c > 2:
                        sp.wait_ge(cT_ready, blocks + T * (c - 2))
                    sp.wait_ge(nat_split, base + T * (c - 1))
                    load(f"chunk{c}@{b}", ctx_rows[b * NCH + c])
                for c in range(2):
                    sp.wait_ge(cT_ready, blocks + BLOCKS - T + T * c)
                    sp.wait_ge(nat_split, base + STEPS - T + T * c)
                    load(f"in{c}@{b}", matrix(in_w[c * D:(c + 1) * D]))

            def expert_loads(b):
                sp.wait_ge(filled, JOB[f"outT.3@{b}"] + 1)
                load(f"W0@{b}", experts[0])
                if b == 0:
                    sp.wait_ge(filled, JOB["inT1.3@1"] + 1)
                load(f"W1@{b}", experts[1])
                for e in range(2, E):
                    sp.wait_ge(split_done, SPLIT[f"W{e - 2}@{b}"] + T)
                    load(f"W{e}@{b}", experts[e])

            sp.wait_ge(filled, JOB["qWT.3"] + 1)
            sp.wait_ge(evacuated, JOB["q0.0"] + 1)
            load("oW", matrix(oW))
            sp.dma_start(probs[0][:], across(ln_b)).then_inc(in_lnb, 16)
            sp.wait_ge(split_done, SPLIT["hW"] + T)
            load("chunk1@0", ctx_rows[1])
            sp.wait_ge(filled, JOB["kWT.3"] + 1)
            sp.wait_ge(kbias_ready, 1)
            sp.dma_start(uT[:], matrix(in_w[0:D])).then_inc(in_k, 16)
            sp.wait_ge(filled, JOB["vWT.3"] + 1)
            sp.wait_ge(vbias_ready, 1)
            sp.dma_start(yT[:], matrix(in_w[D:2 * D])).then_inc(in_v, 16)
            sp.wait_ge(filled, JOB["oWT.3"] + 1)
            load("chunk0@0", ctx_rows[0])
            attention_loads(0)
            for c in range(2):
                sp.wait_ge(filled, JOB[f"inT{c}.3@0"] + 1)
                load(f"chunk{c}@1", ctx_rows[NCH + c])
            attention_loads(1)
            sp.wait_ge(filled, JOB["inT0.3@1"] + 1)
            load("out_w@0", matrix(out_w))
            expert_loads(0)
            sp.wait_ge(split_done, SPLIT["W6@0"] + T)
            load("out_w@1", matrix(out_w))
            sp.wait_ge(evacuated, JOB[f"expert.{E * T - 1}@0"] + 1)
            sp.dma_start(matrix(out[0]), xb[:, 0]).then_inc(stored, 16)
            expert_loads(1)
            for t in range(T):
                sp.wait_ge(evacuated, JOB[f"expert.{E * T - T + t}@1"] + 1)
                sp.dma_start(matrix(out[1])[:, t], xb[:, 1, t]).then_inc(stored, 16)
            sp.wait_ge(stored, 16 * (1 + T))

        @block.tensor
        def _(pe):
            def open_bank(name):
                n = JOB[name]
                if n >= NBANK:
                    pe.wait_ge(evacuated, n - NBANK + 1)
                return bank[BANK[n]]

            def product(dst, lhs, k, rhs):
                for t in range(T):
                    for a, c in PASSES:
                        last = nc.tensor.matmul(dst, lhs[:, a, t, k * P:(k + 1) * P], rhs[:, c, t, :],
                                                start=(t == 0 and (a, c) == PASSES[0]),
                                                stop=(t == T - 1 and (a, c) == PASSES[-1]))
                return last

            def turned(dst, src, k):
                for t in range(T):
                    last = nc.tensor.transpose(dst[:, t * P:(t + 1) * P], src[:, t, k * P:(k + 1) * P], ident[:])
                return last

            def evacuated_from(name):
                pe.wait_ge(evacuated, JOB[name] + 1)

            def split_of(name):
                pe.wait_ge(split_done, SPLIT[name] + T)

            def kept_split_of(name):
                pe.wait_ge(kept_split, KEPT[name] + T)

            def transposes(name, src):
                for k in range(T):
                    job = name.replace("#", str(k))
                    turned(open_bank(job), src, k).then_inc(filled, 1)

            def row_transposes(name, src, first):
                for k in range(T):
                    pe.wait_ge(rows_ready, first + k // 2)
                    dst = open_bank(name.replace("#", str(k)))
                    for t in range(T):
                        last = nc.tensor.transpose(dst[:, t * P:(t + 1) * P], src[:, k, t * P:(t + 1) * P], ident[:])
                    last.then_inc(filled, 1)

            def products(name, lhs, rhs):
                for k in range(T):
                    job = name.replace("#", str(k))
                    product(open_bank(job)[:], lhs, k, rhs).then_inc(filled, 1)

            def prepare():
                pe.wait_ge(ident_ready, 1)
                pe.wait_ge(in_stage[0], LANDED["qW"])
                transposes("qWT.#", stage[0])
                pe.wait_ge(in_vec, 16 * 7)
                nc.tensor.transpose(open_bank("vectors")[:, 0:32], vrows[:], ident[0:32, 0:32]).then_inc(filled, 1)
                row_transposes("xT0.#", rows, ROWS["x0"])
                split_of("hW")
                evacuated_from("qWT.3")
                products("x_to_q.#", hlB, hlA)
                pe.wait_ge(in_k, 16)
                transposes("kWT.#", uT)
                evacuated_from("x_to_q.3")
                products("q0.#", hlC, hlD)
                row_transposes("xT1.#", resid0, ROWS["x1"])
                split_of("cW")
                products("q_to_ctx.#", hlF, hlE)
                evacuated_from("xT1.3")
                products("q1.#", hlC, hlD)
                kept_split_of("q0")
                evacuated_from("q_to_ctx.3")
                products("qc0.#", hlB, hlA)
                pe.wait_ge(in_v, 16)
                transposes("vWT.#", yT)
                kept_split_of("q1")
                products("qc1.#", hlB, hlF)
                pe.wait_ge(kbias_ready, 1)
                for n in range(B):
                    dst = open_bank(f"key_row.{n}")
                    for t in range(T):
                        for a, c in PASSES:
                            last = nc.tensor.matmul(dst[0:2, :], kbias_hl[:, a, t, :], (hlA, hlF)[n][:, c, t, :],
                                                    start=(t == 0 and (a, c) == PASSES[0]),
                                                    stop=(t == T - 1 and (a, c) == PASSES[-1]))
                    last.then_inc(filled, 1)
                evacuated_from("vWT.3")
                evacuated_from("key_row.1")
                dst = open_bank("key_bias")
                for n in range(B * T):
                    last = nc.tensor.transpose(dst[:, 2 * n:2 * n + 2], key_row[n // T][0:2, n % T * P:(n % T + 1) * P],
                                               ident[0:2, 0:2])
                last.then_inc(filled, 1)
                products("ctx_to_v.#", hlC, hlE)
                pe.wait_ge(in_stage[0], LANDED["oW"])
                transposes("oWT.#", stage[0])
                evacuated_from("oWT.3")
                pe.wait_ge(vbias_ready, 1)
                dst = open_bank("x_bias")
                for t in range(T):
                    for a, c in PASSES:
                        last = nc.tensor.matmul(dst[:], vbias_hl[:, a, t:t + 1].to_broadcast([P, P]), hlC[:, c, t, :],
                                                start=(t == 0 and (a, c) == PASSES[0]),
                                                stop=(t == T - 1 and (a, c) == PASSES[-1]))
                last.then_inc(filled, 1)
                products("ctx_to_x.#", hlB, hlC)
                products("qo0.#", hlA, hlC)
                pe.wait_ge(in_stage[0], LANDED["chunk0@0"])
                transposes("ctx0T.#@0", stage[0])
                products("qo1.#", hlF, hlC)

            def attention(b, jobs_before):
                base, blocks = b * STEPS, b * BLOCKS
                load0 = [LANDED[f"chunk0@{b}"], LANDED[f"chunk1@{b}"]]

                def context_block(t, u):
                    par, dd = (u // T + 1) % 2, u % T
                    if dd == 0:
                        pe.wait_ge(in_stage[par], (t + (u // T + 1) // 2) * 16 + load0[par])
                    wait_pos(pe, cT_split, blocks, t * UN + (u - 1))
                    turned(cbank[dd % 2], stage[par], dd).then_inc(cT_ready, 1)

                def scores(t, u):
                    par, q = u // T % 2, u % T
                    if q == 0:
                        wait_pos(pe, cT_split, blocks, t * UN + u)
                    wait_pos(pe, probs_ready, base, t * UN + (u - 1))
                    product(sbank[u % 2][:], qc_hl, q, ctxT[par]).then_inc(scores_ready, 1)

                def turn_probs(t, u):
                    pe.wait_ge(probs_ready, t * UN + (base + u + 1))
                    wait_pos(pe, pT_split, base, t * UN + (u - 1))
                    for j in range(T):
                        last = nc.tensor.transpose(tbank[u % 2][:, j * P:(j + 1) * P],
                                                   probs[u % 2][:, j * P:(j + 1) * P], ident[:])
                    last.then_inc(pT_ready, 1)

                def weigh(t, u):
                    par = u // T % 2
                    pe.wait_ge(pT_split, t * UN + (base + u + 1))
                    if u % T == 0:
                        pe.wait_ge(nat_split, t * UN + (base + u + T))
                    wait_pos(pe, sums_updated, 2 * base, t * (2 * UN) + 2 * (u - 1))
                    for j in range(T):
                        for a, c in PASSES:
                            last = nc.tensor.matmul(obank[u % 2][:], probsT[u % 2][:, a, j, :], nat[par][:, c, j, :],
                                                    start=(j == 0 and (a, c) == PASSES[0]),
                                                    stop=(j == T - 1 and (a, c) == PASSES[-1]))
                    last.then_inc(pv_ready, 1)

                def back(t, u, n):
                    return (t, u - n) if u >= n else (t - 1, u - n + UN)

                def trip(t, first, last):
                    for u in range(UN):
                        if not (last and u >= T):
                            context_block(t, u)
                        scores(t, u)
                        if first and u == 1:
                            pe.wait_ge(evacuated, jobs_before)
                        if not (first and u < 1):
                            turn_probs(*back(t, u, 1))
                        if not (first and u < 2):
                            weigh(*back(t, u, 2))

                if b == 1:
                    split_of("qc1")
                pe.wait_ge(evacuated, jobs_before - T)
                trips(pe, TRIPS, trip)
                turn_probs(TRIPS - 1, UN - 1)
                weigh(TRIPS - 1, UN - 2)
                pe.wait_ge(in_stage[0], LANDED[f"in0@{b}"])
                pe.wait_ge(cT_split, blocks + BLOCKS)
                pe.wait_ge(probs_ready, base + STEPS)
                transposes(f"inT0.#@{b}", stage[0])
                weigh(TRIPS - 1, UN - 1)

            def middle(b):
                row_transposes(f"pooledT.#@{b}", rows, ROWS[f"pooled@{b}"])
                pe.wait_ge(in_stage[1], LANDED[f"in1@{b}"])
                transposes(f"inT1.#@{b}", stage[1])
                if b == 1:
                    pe.wait_ge(in_stage[0], LANDED["out_w@0"])
                    transposes("outT.#@0", stage[0])
                evacuated_from(f"pooledT.3@{b}")
                products(f"x_attn.#@{b}", hlA, ctx_to_x)
                if b == 1:
                    project_out(0)
                row_transposes(f"normT.#@{b}", rows, ROWS[f"norm@{b}"])
                evacuated_from(f"normT.3@{b}")
                products(f"u.#@{b}", hlB, hlF)
                if b == 0:
                    pe.wait_ge(in_stage[0], LANDED["chunk0@1"])
                    transposes("ctx0T.#@1", stage[0])
                products(f"z.#@{b}", hlC, hlF)
                if b == 1:
                    gate_logits(0)

            def project_out(b):
                kept_split_of(f"gated@{b}")
                evacuated_from(f"outT.3@{b}")
                products(f"x_ssm.#@{b}", hlD if b == 0 else hlC, hlF)

            def gate_logits(b):
                row_transposes(f"ffnT.#@{b}", rows, ROWS[f"ffn@{b}"])
                evacuated_from(f"ffnT.3@{b}")
                pe.wait_ge(gate_ready, 1)
                dst = open_bank(f"logits@{b}")
                for t in range(T):
                    for a, c in PASSES:
                        last = nc.tensor.matmul(dst[0:E, :], gate_hl[:, a, t, :], hlD[:, c, t, :],
                                                start=(t == 0 and (a, c) == PASSES[0]),
                                                stop=(t == T - 1 and (a, c) == PASSES[-1]))
                last.then_inc(filled, 1)
                evacuated_from(f"logits@{b}")
                dst = open_bank(f"logit_columns@{b}")
                for k in range(T):
                    last = nc.tensor.transpose(dst[:, k * E:(k + 1) * E], onehotT[:, k * P:(k + 1) * P], ident[0:E, 0:E])
                last.then_inc(filled, 1)

            def mix_experts(b):
                pe.wait_ge(onehot_ready, b + 1)
                dst = open_bank(f"onehotT@{b}")
                for k in range(T):
                    last = nc.tensor.transpose(dst[0:E, k * P:(k + 1) * P], onehot[:, k, :], ident[:])
                last.then_inc(filled, 1)
                evacuated_from(f"onehotT@{b}")
                for k in range(T):
                    dst = open_bank(f"expert_bias.{k}@{b}")
                    nc.tensor.matmul(dst[:], onehotT[:, k * P:(k + 1) * P], eb[:], start=True, stop=True).then_inc(filled, 1)
                job0, split0 = JOB[f"expert.0@{b}"], SPLIT[f"W0@{b}"]
                with pe.Fori(0, MTRIPS) as t:
                    for u in range(UN):
                        if u % T == 0:
                            pe.wait_ge(split_done, t * UN + (split0 + u + T))
                        pe.wait_ge(evacuated, t * UN + (job0 + u - NBANK + 1))
                        product(bank[BANK[job0 + u]][:], hlD, u % T, weights_hl[u // T]).then_inc(filled, 1)

            prepare()
            attention(0, len(PREP_JOBS))
            middle(0)
            attention(1, JOB["z.3@0"] + 1)
            middle(1)
            mix_experts(0)
            pe.wait_ge(in_stage[0], LANDED["out_w@1"])
            transposes("outT.#@1", stage[0])
            project_out(1)
            gate_logits(1)
            mix_experts(1)

        @block.scalar
        def _(act):
            def round_job(name, dst):
                act.wait_ge(filled, JOB[name] + 1)
                nc.scalar.activation(dst, bank[BANK[JOB[name]]][:], ACT.Copy).then_inc(rounded, 1)

            def round_jobs(name, slot):
                for k in range(T):
                    round_job(name.replace("#", str(k)), slot[:, 0, k, :])

            def round_rows(name, slot):
                for k in range(T):
                    job = name.replace("#", str(k))
                    act.wait_ge(filled, JOB[job] + 1)
                    nc.scalar.activation(slot[:, 0, :, k * P:(k + 1) * P],
                                         bank[BANK[JOB[job]]][:].rearrange("p (t q) -> p t q", t=T), ACT.Copy).then_inc(rounded, 1)

            def round_scaled(name, slot):
                for k in range(T):
                    job = name.replace("#", str(k))
                    act.wait_ge(filled, JOB[job] + 1)
                    nc.scalar.activation(slot[:, 0, k, :], bank[BANK[JOB[job]]][:], ACT.Copy,
                                         scale=vecs[:, 20 + k:21 + k]).then_inc(rounded, 1)

            def round_tiles(src, slot):
                for k in range(T):
                    nc.scalar.activation(slot[:, 0, k, :], src[:, k, :], ACT.Copy).then_inc(split_hi, 1)

            def round_kept(ready, count, src, slot):
                for k in range(T):
                    act.wait_ge(ready, count + k + 1)
                    nc.scalar.activation(slot[:, 0, k, :], src[:, k, :], ACT.Copy).then_inc(kept_hi, 1)

            def small_loads():
                for k, v in ((0, qb), (4, kb), (8, vb), (12, in_b), (20, ln_g), (24, ln_b), (28, log_dt)):
                    n = v.shape[0] // P
                    act.dma_start(vrows[k:k + n, :], v.rearrange("(t p) -> t p", p=P)).then_inc(in_vec, 16)
                act.dma_start(probs[0][:], across(hb)).then_inc(in_bias, 16)
                act.dma_start(probs[1][:], across(cb)).then_inc(in_bias, 16)
                for k, v in enumerate((A_log, B_param, C_param)):
                    act.dma_start(ssm_in[:, k], matrix(v)).then_inc(in_ssm, 16)
                act.dma_start(obB[:], across(ob)).then_inc(in_small, 16)
                act.dma_start(outbB[:], across(out_b)).then_inc(in_small, 16)
                act.dma_start(gbB[:], across(gate_b)).then_inc(in_small, 16)
                act.dma_start(gate_raw[:], matrix(gate_w)).then_inc(in_small, 16)
                act.dma_start(eb[:], expert_b).then_inc(in_small, 16)

            def prepare():
                small_loads()
                round_jobs("qWT.#", hlA)
                act.wait_ge(in_stage[1], LANDED["hW"])
                round_tiles(stage[1], hlB)
                round_rows("xT0.#", hlD)
                act.wait_ge(in_c, 16)
                round_tiles(zT, hlE)
                round_jobs("x_to_q.#", hlC)
                round_jobs("kWT.#", hlF)
                round_kept(evacuated, JOB["q0.0"], qT[0], hlA)
                round_rows("xT1.#", hlD)
                act.wait_ge(in_ssm, 16 * 3)
                act.wait_ge(vectors_ready, 1)
                nc.scalar.activation(ssm_w[:, 0], ssm_in[:, 0], ACT.Exp).then_inc(ssm_exp, 1)
                nc.scalar.activation(dtv[:], vecs[:, 28:32], ACT.Exp).then_inc(ssm_exp, 1)
                round_jobs("q_to_ctx.#", hlB)
                round_kept(evacuated, JOB["q1.0"], qT[1], hlF)
                round_jobs("qc0.#", hlD)
                round_jobs("vWT.#", hlC)
                round_jobs("ctx_to_v.#", hlB)
                round_jobs("oWT.#", hlC)
                round_jobs("ctx_to_x.#", ctx_to_x)
                round_jobs("ctx0T.#@0", ctxT[0])

            def attention(b, jobs_before, scan):
                base, blocks = b * STEPS, b * BLOCKS
                load0 = [LANDED[f"chunk0@{b}"], LANDED[f"chunk1@{b}"]]

                def natural(t, u):
                    g = u + 2
                    par, j = g // T % 2, g % T
                    if j == 0 or (j == 2 and u == 0):
                        act.wait_ge(in_stage[par], (t + g // T // 2) * 16 + load0[par])
                    wait_pos(act, pv_ready, base, t * UN + (g // T - 1) * T)
                    nc.scalar.activation(nat[par][:, 0, j, :], stage[par][:, j, :], ACT.Copy).then_inc(nat_hi, 1)

                def context_block(t, u):
                    par, dd = (u // T + 1) % 2, u % T
                    act.wait_ge(cT_ready, t * UN + (blocks + u + 1))
                    nc.scalar.activation(ctxT[par][:, 0, dd, :], cbank[dd % 2][:], ACT.Copy).then_inc(cT_hi, 1)

                def turned_probs(t, u):
                    act.wait_ge(pT_ready, t * UN + (base + u + 1))
                    nc.scalar.activation(probsT[u % 2][:, 0], tbank[u % 2][:].rearrange("p (j q) -> p j q", j=T),
                                         ACT.Copy).then_inc(pT_hi, 1)

                def exponentials(t, u):
                    q = u % T
                    wait_pos(act, pT_ready, base, t * UN + (u - 1))
                    wait_pos(act, sums_updated, 2 * base, t * (2 * UN) + 2 * (u - 3))
                    act.wait_ge(max_ready, t * UN + (base + u + 1))
                    nc.scalar.activation(probs[u % 2][:], sbank[u % 2][:], ACT.Exp, bias=nbias[:, q:q + 1], scale=SCALE,
                                         accum_out=rsum[:, q:q + 1]).then_inc(probs_ready, 1)
                    act.wait_ge(dmax_ready, t * UN + (base + u + 1))
                    nc.scalar.activation(alpha[:, q:q + 1], dmax[:, q:q + 1], ACT.Exp, scale=SCALE).then_inc(alpha_ready, 1)

                def trip(t, first, last):
                    for u in range(UN):
                        if not (last and u >= T):
                            context_block(t, u)
                        exponentials(t, u)
                        if not (first and u < 1):
                            turned_probs(*((t, u - 1) if u else (t - 1, UN - 1)))
                        if first and scan and u == T:
                            gates(0)
                        if not (last and u + 2 >= UN):
                            natural(t, u)
                        if scan and u % 2 == 0:
                            scale_state(0, t * UN + u, t * T + u // 2, u // 2)

                act.wait_ge(filled, jobs_before)
                act.wait_ge(in_stage[0], load0[0])
                for j in range(2):
                    nc.scalar.activation(nat[0][:, 0, j, :], stage[0][:, j, :], ACT.Copy).then_inc(nat_hi, 1)
                trips(act, TRIPS, trip)
                turned_probs(TRIPS - 1, UN - 1)

            def scale_state(b, s, n, k):
                act.wait_ge(scanned, n + (b * SCANS // 2 + 1))
                col = cbdt[:].rearrange("p n d -> p (n d)")[:, bass.ds(s, 1)]
                nc.scalar.activation(even_h[b][k % 2][:], even_h[b][k % 2][:], ACT.Copy, scale=col).then_inc(scaled, 1)

            def middle(b):
                round_scaled(f"inT0.#@{b}", hlB)
                round_rows(f"pooledT.#@{b}", hlA)
                round_scaled(f"inT1.#@{b}", hlC)
                if b == 0:
                    act.wait_ge(scores_ready, STEPS)
                    round_tiles(qc1, qc_hl)
                else:
                    round_jobs("outT.#@0", hlF)
                    round_kept(gated, 0 * T, yT, hlD)
                round_rows(f"normT.#@{b}", hlF)
                if b == 0:
                    round_jobs("ctx0T.#@1", ctxT[0])
                else:
                    first_weights(0)
                    gates(1)
                    round_rows("ffnT.#@0", hlD)

            def gates(b):
                for k in range(T):
                    act.wait_ge(evacuated, JOB[f"z.{k}@{b}"] + 1)
                    nc.scalar.activation(zT[:, k, :], zT[:, k, :], ACT.Silu).then_inc(z_gated, 1)

            def weights(par, k, landed, used):
                act.wait_ge(in_stage[par], landed)
                act.wait_ge(filled, used)
                nc.scalar.activation(weights_hl[par][:, 0, k, :], stage[par][:, k, :], ACT.Copy).then_inc(split_hi, 1)

            def first_weights(b):
                used = JOB["x_attn.3@1"] if b == 0 else JOB[f"expert.{E * T - T - 1}@0"]
                for k in range(T):
                    weights(0, k, LANDED[f"W0@{b}"], used + 1)

            def mix_experts(b, scan):
                job0 = JOB[f"expert.0@{b}"]
                loads = [LANDED[f"W0@{b}"], LANDED[f"W1@{b}"]]

                def trip(t, first, last):
                    for u in range(UN):
                        for k in AHEAD[u % T] if not (last and u >= T) else ():
                            par = 1 - u // T
                            weights(par, k, (t + u // T) * 16 + loads[par], t * UN + (job0 + u // T * T))
                        if scan:
                            scale_state(1, t * (2 * UN) + 2 * u, t * UN + u, u)

                trips(act, MTRIPS, trip)

            prepare()
            attention(0, len(PREP_JOBS), False)
            middle(0)
            attention(1, JOB["z.3@0"] + 1, True)
            middle(1)
            mix_experts(0, True)
            first_weights(1)
            round_jobs("outT.#@1", hlF)
            round_kept(gated, 1 * T, yT, hlC)
            round_rows("ffnT.#@1", hlD)
            mix_experts(1, False)

        @block.vector
        def _(dve):
            links = [0]

            def link(ins):
                links[0] += 1
                ins.then_inc(link_done, 1)
                dve.wait_ge(link_done, links[0])

            def lo_job(name, slot, k):
                dve.wait_ge(rounded, ROUND[name] + 1)
                nc.vector.tensor_tensor(slot[:, 1, k, :], bank[BANK[JOB[name]]][:], slot[:, 0, k, :].bitcast(F32),
                                        ALU.subtract).then_inc(evacuated, 1)

            def lo_jobs(name, slot):
                for k in range(T):
                    lo_job(name.replace("#", str(k)), slot, k)

            def lo_rows(name, slot):
                for k in range(T):
                    job = name.replace("#", str(k))
                    cols = slice(k * P, (k + 1) * P)
                    dve.wait_ge(rounded, ROUND[job] + 1)
                    nc.vector.tensor_tensor(slot[:, 1, :, cols], bank[BANK[JOB[job]]][:].rearrange("p (t q) -> p t q", t=T),
                                            slot[:, 0, :, cols].bitcast(F32), ALU.subtract).then_inc(evacuated, 1)

            def lo_scaled(name, slot):
                for k in range(T):
                    job = name.replace("#", str(k))
                    dve.wait_ge(rounded, ROUND[job] + 1)
                    nc.vector.scalar_tensor_tensor(slot[:, 1, k, :], bank[BANK[JOB[job]]][:], vecs[:, 20 + k:21 + k],
                                                   slot[:, 0, k, :].bitcast(F32), ALU.mult, ALU.subtract).then_inc(evacuated, 1)

            def normalize(src, pair, dst, dst2=None):
                two = slice(2 * pair, 2 * pair + 2)
                norms = 1 if dst2 is None else 2
                for t in (2 * pair, 2 * pair + 1):
                    last = nc.vector.bn_stats(bnst[:, t, :], src[:, t, :])
                link(last)
                for t in (2 * pair, 2 * pair + 1):
                    last = nc.vector.bn_aggr(mv[:, t, :], bnst[:, t, :])
                link(last)
                link(nc.vector.tensor_scalar(var[:, 0, two], mv[:, two, 1], EPS, None, ALU.add))
                if norms == 2:
                    link(nc.vector.scalar_tensor_tensor(var[:, 1, two], var[:, 0, two], EPS, mv[:, two, 1], ALU.mult, ALU.add))
                v, r, a = (m[:, 0:norms, two] for m in (var, rstd, newton))
                link(nc.vector.tensor_scalar(seed[:, 0:norms, two], v.bitcast(I32), 1, None, ALU.logical_shift_right))
                link(nc.vector.tensor_scalar(r.bitcast(I32), seed[:, 0:norms, two], -1.0, RSQRT_SEED, ALU.mult, ALU.add))
                for _k in range(3):
                    link(nc.vector.tensor_tensor(a, r, r, ALU.mult))
                    link(nc.vector.scalar_tensor_tensor(a, a, -0.5, v, ALU.mult, ALU.mult))
                    link(nc.vector.scalar_tensor_tensor(r, a, 1.5, r, ALU.add, ALU.mult))
                for n, out_rows in ((0, dst),) if dst2 is None else ((1, dst2), (0, dst)):
                    for t in (2 * pair, 2 * pair + 1):
                        last = nc.vector.tensor_scalar(out_rows[:, t, :], src[:, t, :], mv[:, t, 0:1], rstd[:, n, t:t + 1],
                                                       ALU.subtract, ALU.mult)
                    if n == norms - 1:
                        last.then_inc(rows_ready, 1)
                return last

            def keep_and_split(name, make, src, slot):
                for k in range(T + 1):
                    if k < T:
                        make(k)
                    if k > 0:
                        dve.wait_ge(kept_hi, KEPT[name] + k)
                        nc.vector.tensor_tensor(slot[:, 1, k - 1, :], src[:, k - 1, :], slot[:, 0, k - 1, :].bitcast(F32),
                                                ALU.subtract).then_inc(kept_split, 1)

            def folded_bias(dst, w, v, own):
                for t in range(T):
                    link(nc.vector.tensor_tensor_reduce(h[0][:], w[:, t, :], v[:], 1.0, 0.0, ALU.mult, ALU.add,
                                                        dst[:, t:t + 1]))
                return nc.vector.tensor_tensor(dst, dst, vecs[:, own:own + T], ALU.add)

            def prepare():
                nc.vector.memset(desc[:], 1.0).then_inc(desc_ready, 1)
                for e in range(E - 1):
                    dve.wait_ge(desc_ready, e + 1)
                    nc.vector.memset(desc[:, e:e + 1], float(E - e)).then_inc(desc_ready, 1)
                for pair in range(2):
                    dve.wait_ge(in_x0[pair], 16)
                    normalize(xb[:, 0], pair, rows)
                lo_jobs("qWT.#", hlA)
                dve.wait_ge(filled, JOB["vectors"] + 1)
                nc.vector.tensor_copy(vecs[:], bank[BANK[JOB["vectors"]]][:, 0:32]).then_inc(evacuated, 1)
                dve.wait_ge(evacuated, JOB["vectors"] + 1)
                nc.vector.tensor_copy(dtv[:], vecs[:, 28:32]).then_inc(vectors_ready, 1)
                lo_rows("xT0.#", hlD)
                dve.wait_ge(in_bias, 32)
                link(folded_bias(qbias[:], stage[0], probs[0], 0))
                dve.wait_ge(in_x1, 16)
                normalize(xb[:, 1], 0, resid0)
                lo_jobs("x_to_q.#", hlC)
                normalize(xb[:, 1], 1, resid0)
                lo_jobs("kWT.#", hlF)
                keep_and_split("q0", lambda k: queries(0, k), qT[0], hlA)
                lo_rows("xT1.#", hlD)
                dve.wait_ge(in_k, 16)
                link(folded_bias(kbias[:], uT, probs[1], 4))
                for c in range(2):
                    last = nc.vector.tensor_copy(kbias_hl[:, 0, :, c], kbias[:])
                link(last)
                for c in range(2):
                    last = nc.vector.tensor_tensor(kbias_hl[:, 1, :, c], kbias[:], kbias_hl[:, 0, :, c].bitcast(F32), ALU.subtract)
                last.then_inc(kbias_ready, 1)
                lo_jobs("q_to_ctx.#", hlB)
                keep_and_split("q1", lambda k: queries(1, k), qT[1], hlF)
                dve.wait_ge(in_v, 16)
                link(folded_bias(vbias[:], yT, probs[1], 8))
                link(nc.vector.tensor_copy(vbias_hl[:, 0], vbias[:]))
                nc.vector.tensor_tensor(vbias_hl[:, 1], vbias[:], vbias_hl[:, 0].bitcast(F32), ALU.subtract).then_inc(vbias_ready, 1)
                lo_jobs("qc0.#", hlD)
                lo_jobs("vWT.#", hlC)
                small_parameters()
                for k in range(T):
                    dve.wait_ge(filled, JOB[f"qc1.{k}"] + 1)
                    nc.vector.tensor_copy(qc1[:, k, :], bank[BANK[JOB[f"qc1.{k}"]]][:]).then_inc(evacuated, 1)
                for n in range(B):
                    dve.wait_ge(filled, JOB[f"key_row.{n}"] + 1)
                    nc.vector.tensor_copy(key_row[n][0:2, :], bank[BANK[JOB[f"key_row.{n}"]]][0:2, :]).then_inc(evacuated, 1)
                dve.wait_ge(filled, JOB["key_bias"] + 1)
                nc.vector.tensor_copy(kq[:], bank[BANK[JOB["key_bias"]]][:, 0:2 * B * T].rearrange("p (n c) -> p n c", c=2)[:, :, 0]
                                      ).then_inc(evacuated, 1)
                lo_jobs("ctx_to_v.#", hlB)
                lo_jobs("oWT.#", hlC)
                dve.wait_ge(filled, JOB["x_bias"] + 1)
                nc.vector.tensor_tensor(obB[:], bank[BANK[JOB["x_bias"]]][:], obB[:], ALU.add).then_inc(evacuated, 1)
                lo_jobs("ctx_to_x.#", ctx_to_x)
                dve.wait_ge(in_lnb, 16)
                dve.wait_ge(in_k, 32)
                link(folded_bias(inbias[:, 0:T], uT, probs[0], 12))
                dve.wait_ge(in_v, 32)
                folded_bias(inbias[:, T:2 * T], yT, probs[0], 16).then_inc(inbias_ready, 1)
                dve.wait_ge(x_biased, 1)
                for k in range(T):
                    add_to_x(f"qo0.{k}", 0, k)
                lo_jobs("ctx0T.#@0", ctxT[0])
                for k in range(T):
                    add_to_x(f"qo1.{k}", 1, k)

            def add_to_x(job, b, k):
                dve.wait_ge(filled, JOB[job] + 1)
                nc.vector.tensor_tensor(xb[:, b, k, :], bank[BANK[JOB[job]]][:], xb[:, b, k, :],
                                        ALU.add).then_inc(evacuated, 1)

            def queries(b, k):
                dve.wait_ge(filled, JOB[f"q{b}.{k}"] + 1)
                ins = nc.vector.tensor_scalar(qT[b][:, k, :], bank[BANK[JOB[f"q{b}.{k}"]]][:], qbias[:, k:k + 1], None,
                                              ALU.add)
                ins.then_inc(evacuated, 1)

            def small_parameters():
                dve.wait_ge(in_small, 16 * 5)
                link(nc.vector.tensor_copy(gate_hl[:, 0], gate_raw[:]))
                nc.vector.tensor_tensor(gate_hl[:, 1], gate_raw[:], gate_hl[:, 0].bitcast(F32),
                                        ALU.subtract).then_inc(gate_ready, 1)
                dve.wait_ge(ssm_exp, 2)
                link(nc.vector.tensor_scalar(dtv[:], dtv[:], 1e-4, 1.0, ALU.max, ALU.min))
                ea, w, p, dtb = (ssm_w[:, k] for k in range(4))
                for t in range(T):
                    last = nc.vector.tensor_scalar(w[:, t, :], ea[:, t, :], dtv[:, t:t + 1], -1.0, ALU.mult, ALU.mult)
                link(last)
                link(nc.vector.tensor_tensor(dtb[:], ssm_in[:, 1], ssm_in[:, 2], ALU.mult))
                for t in range(T):
                    last = nc.vector.tensor_scalar(cbdt[:, :, t], dtb[:, t, :], dtv[:, t:t + 1], None, ALU.mult)
                link(last)
                link(nc.vector.tensor_scalar(w[:], w[:], -30.0, 0.5 ** EXPM1_DOUBLINGS, ALU.max, ALU.mult))
                link(nc.vector.tensor_scalar(p[:], w[:], 0.2, 1.0, ALU.mult, ALU.add))
                for k in (4.0, 3.0, 2.0):
                    link(nc.vector.scalar_tensor_tensor(p[:], p[:], 1.0 / k, w[:], ALU.mult, ALU.mult))
                    link(nc.vector.tensor_scalar(p[:], p[:], 1.0, None, ALU.add))
                link(nc.vector.tensor_tensor(p[:], p[:], w[:], ALU.mult))
                for _k in range(EXPM1_DOUBLINGS):
                    link(nc.vector.scalar_tensor_tensor(p[:], p[:], 2.0, p[:], ALU.add, ALU.mult))
                link(nc.vector.tensor_scalar(p[:], p[:], 1.0, 1e-8, ALU.add, ALU.max))
                link(nc.vector.tensor_scalar(abar[:].rearrange("p n t -> p t n"), p[:], 1.0 - 1e-8, None, ALU.min))

            def attention(b, scan):
                base, blocks = b * STEPS, b * BLOCKS

                def maxima(t, u):
                    par, q = u // T % 2, u % T
                    col = slice(q, q + 1)
                    dve.wait_ge(scores_ready, t * UN + (base + u + 1))
                    nc.vector.tensor_reduce(mx[:, col], sbank[u % 2][:], AX_X, ALU.max).then_inc(stat_done, 1)
                    dve.wait_ge(stat_done, t * (2 * UN) + (2 * base + 2 * u + 1))
                    nc.vector.tensor_scalar(mrun[:, 1 - par, col], mx[:, col], kq[:, b * T + q:b * T + q + 1], mrun[:, par, col],
                                            ALU.add, ALU.max).then_inc(stat_done, 1)
                    dve.wait_ge(stat_done, t * (2 * UN) + (2 * base + 2 * u + 2))
                    nc.vector.tensor_scalar(nbias[:, col], mrun[:, 1 - par, col], kq[:, b * T + q:b * T + q + 1], -SCALE,
                                            ALU.subtract, ALU.mult).then_inc(max_ready, 1)
                    nc.vector.tensor_tensor(dmax[:, col], mrun[:, par, col], mrun[:, 1 - par, col],
                                            ALU.subtract).then_inc(dmax_ready, 1)

                def turned_probs(t, u):
                    dve.wait_ge(pT_hi, t * UN + (base + u + 1))
                    nc.vector.tensor_tensor(probsT[u % 2][:, 1], tbank[u % 2][:].rearrange("p (j q) -> p j q", j=T),
                                            probsT[u % 2][:, 0].bitcast(F32), ALU.subtract).then_inc(pT_split, 1)

                def context_block(t, u):
                    par, dd = (u // T + 1) % 2, u % T
                    dve.wait_ge(cT_hi, t * UN + (blocks + u + 1))
                    nc.vector.tensor_tensor(ctxT[par][:, 1, dd, :], cbank[dd % 2][:], ctxT[par][:, 0, dd, :].bitcast(F32),
                                            ALU.subtract).then_inc(cT_split, 1)

                def sums(t, u):
                    q = u % T
                    col = slice(q, q + 1)
                    dve.wait_ge(alpha_ready, t * UN + (base + u + 1))
                    dve.wait_ge(probs_ready, t * UN + (base + u + 1))
                    wait_pos(dve, sums_updated, 2 * base, t * (2 * UN) + 2 * (u - 3))
                    nc.vector.scalar_tensor_tensor(lsum[:, col], lsum[:, col], alpha[:, col], rsum[:, col],
                                                   ALU.mult, ALU.add).then_inc(sums_updated, 1)
                    dve.wait_ge(pv_ready, t * UN + (base + u + 1))
                    nc.vector.scalar_tensor_tensor(rows[:, q, :], rows[:, q, :], alpha[:, col], obank[u % 2][:],
                                                   ALU.mult, ALU.add).then_inc(sums_updated, 1)

                def trip(t, first, last):
                    for u in range(UN):
                        if not (last and u >= T):
                            context_block(t, u)
                        maxima(t, u)
                        if not (first and u < 1):
                            turned_probs(*((t, u - 1) if u else (t - 1, UN - 1)))
                        if scan:
                            scan_state(0, t * UN + u, u, t * T + u // 2, first and u < 2)
                        if not (first and u < 2):
                            sums(*((t, u - 2) if u >= 2 else (t - 1, u - 2 + UN)))

                dve.wait_ge(sums_zeroed, 3 * (b + 1))
                trips(dve, TRIPS, trip)
                turned_probs(TRIPS - 1, UN - 1)
                sums(TRIPS - 1, UN - 2)
                sums(TRIPS - 1, UN - 1)

            def scan_state(b, s, k, n, first):
                dst = h[1] if k % 2 else even_h[b][k // 2 % 2]
                if not first:
                    dve.wait_ge(odd_summed if k % 2 else summed, n + (b * SCANS // 2 - (b if k % 2 == 0 else 0)))
                col = abar[:].rearrange("p n d -> p (n d)")[:, bass.ds(s, 1)]
                scan = nc.vector.tensor_tensor_scan(dst[:], col.to_broadcast([P, S]), uT[:, k % T, :], 0.0,
                                                    ALU.mult, ALU.add)
                if k % 2 == 0:
                    scan.then_inc(scanned, 1)
                else:
                    scan.then_inc(odd_scanned, 1)
                    dve.wait_ge(odd_scanned, n + (b * SCANS // 2 + 1))
                    weight = cbdt[:].rearrange("p n d -> p (n d)")[:, bass.ds(s, 1)]
                    nc.vector.scalar_tensor_tensor(yT[:, k % T, :], h[1][:], weight, yT[:, k % T, :],
                                                   ALU.mult, ALU.add).then_inc(odd_summed, 1)

            def pool_context(b):
                dve.wait_ge(sums_updated, 2 * (b + 1) * STEPS)
                link(nc.vector.reciprocal(lsum[:], lsum[:]))
                for pair in range(2):
                    for t in (2 * pair, 2 * pair + 1):
                        last = nc.vector.tensor_scalar(rows[:, t, :], rows[:, t, :], lsum[:, t:t + 1], None, ALU.mult)
                    last.then_inc(rows_ready, 1)

            def middle(b):
                pool_context(b)
                lo_scaled(f"inT0.#@{b}", hlB)
                lo_rows(f"pooledT.#@{b}", hlA)
                lo_scaled(f"inT1.#@{b}", hlC)
                if b == 1:
                    lo_jobs("outT.#@0", hlF)
                for pair in range(2):
                    for k in (2 * pair, 2 * pair + 1):
                        add_to_x(f"x_attn.{k}@{b}", b, k)
                    dve.wait_ge(evacuated, JOB[f"x_attn.{2 * pair + 1}@{b}"] + 1)
                    last = normalize(xb[:, b], pair, resid[b], rows)
                last.then_inc(resid_ready, 1)
                if b == 1:
                    dve.wait_ge(resid_biased, 1)
                    for k in range(T):
                        project_tile(0, k)
                lo_rows(f"normT.#@{b}", hlF)
                for name, dst, own in (("u", uT, 0), ("z", zT, T)):
                    for k in range(T):
                        job = f"{name}.{k}@{b}"
                        if b == 1:
                            if name == "u":
                                add_mixed(0, k)
                            elif k % 2 == 0:
                                normalize(xb[:, 0], k // 2, rows)
                        dve.wait_ge(filled, JOB[job] + 1)
                        nc.vector.tensor_scalar(dst[:, k, :], bank[BANK[JOB[job]]][:], inbias[:, own + k:own + k + 1], None,
                                                ALU.add).then_inc(evacuated, 1)
                    if name == "u" and b == 0:
                        lo_jobs("ctx0T.#@1", ctxT[0])
                dve.wait_ge(evacuated, JOB[f"u.3@{b}"] + 1)
                dve.wait_ge(y_zeroed, b + 1)

                if b == 1:
                    gate(0)

            def project_tile(b, k):
                name = f"x_ssm.{k}@{b}"
                dve.wait_ge(filled, JOB[name] + 1)
                nc.vector.tensor_tensor(resid[b][:, k, :], bank[BANK[JOB[name]]][:], resid[b][:, k, :],
                                        ALU.add).then_inc(evacuated, 1)

            def add_mixed(b, k):
                dve.wait_ge(evacuated, JOB[f"x_ssm.{k}@{b}"] + 1)
                link(nc.vector.tensor_scalar(resid[b][:, k, :], resid[b][:, k, :], 10.0, -10.0, ALU.min, ALU.max))
                link(nc.vector.tensor_tensor(xb[:, b, k, :], xb[:, b, k, :], resid[b][:, k, :], ALU.add))

            def gated_tile(k):
                nc.vector.tensor_tensor(yT[:, k, :], yT[:, k, :], zT[:, k, :], ALU.mult).then_inc(gated, 1)

            def project_out(b, slot):
                dve.wait_ge(summed, (b + 1) * SCANS // 2)
                dve.wait_ge(odd_summed, (b + 1) * SCANS // 2)
                dve.wait_ge(z_gated, (b + 1) * T)
                keep_and_split(f"gated@{b}", gated_tile, yT, slot)
                dve.wait_ge(resid_biased, b + 1)
                for k in range(T):
                    project_tile(b, k)
                    add_mixed(b, k)
                    if k % 2:
                        normalize(xb[:, b], k // 2, rows)

            def gate(b):
                lo_rows(f"ffnT.#@{b}", hlD)
                name = f"logits@{b}"
                dve.wait_ge(filled, JOB[name] + 1)
                nc.vector.tensor_copy(onehotT[:], bank[BANK[JOB[name]]][0:E, :]).then_inc(evacuated, 1)
                name = f"logit_columns@{b}"
                dve.wait_ge(filled, JOB[name] + 1)
                for k in range(T):
                    last = nc.vector.tensor_tensor(logit[:, k, :], bank[BANK[JOB[name]]][:, k * E:(k + 1) * E], gbB[:], ALU.add)
                last.then_inc(evacuated, 1)
                dve.wait_ge(evacuated, JOB[name] + 1)
                link(nc.vector.tensor_reduce(lmax[:, 0], logit[:], AX_X, ALU.max))
                dve.wait_ge(desc_ready, E)
                for k in range(T):
                    last = nc.vector.scalar_tensor_tensor(pick[:, k, :], logit[:, k, :], lmax[:, 0, k:k + 1], desc[:],
                                                          ALU.is_equal, ALU.mult)
                link(last)
                link(nc.vector.tensor_reduce(lmax[:, 1], pick[:], AX_X, ALU.max))
                for k in range(T):
                    last = nc.vector.tensor_scalar(onehot[:, k, :], pick[:, k, :], lmax[:, 1, k:k + 1], None, ALU.is_equal)
                last.then_inc(onehot_ready, 1)

            def mix_experts(b, scan):
                name = f"onehotT@{b}"
                dve.wait_ge(filled, JOB[name] + 1)
                nc.vector.tensor_copy(onehotT[:], bank[BANK[JOB[name]]][0:E, :]).then_inc(evacuated, 1)
                for k in range(T):
                    name = f"expert_bias.{k}@{b}"
                    dve.wait_ge(filled, JOB[name] + 1)
                    nc.vector.tensor_tensor(xb[:, b, k, :], bank[BANK[JOB[name]]][:], xb[:, b, k, :],
                                            ALU.add).then_inc(evacuated, 1)
                job0 = JOB[f"expert.0@{b}"]
                weight = onehot[:].rearrange("p t e -> p (t e)")

                def trip(t, first, last):
                    for u in range(UN):
                        k = u % T
                        dve.wait_ge(filled, t * UN + (job0 + u + 1))
                        dve.wait_ge(evacuated, t * UN + (job0 + u + 1 - T))
                        nc.vector.scalar_tensor_tensor(xb[:, b, k, :], bank[BANK[job0 + u]][:],
                                                       weight[:, bass.ds(t * 2 + (k * E + u // T), 1)], xb[:, b, k, :],
                                                       ALU.mult, ALU.add).then_inc(evacuated, 1)
                        if scan:
                            for v in range(2):
                                scan_state(1, t * (2 * UN) + (2 * u + v), 2 * u + v, t * UN + u, False)

                trips(dve, MTRIPS, trip)

            prepare()
            attention(0, False)
            middle(0)
            attention(1, True)
            middle(1)
            mix_experts(0, True)
            lo_jobs("outT.#@1", hlF)
            project_out(1, hlC)
            gate(1)
            mix_experts(1, False)

        @block.gpsimd
        def _(pool):
            nc.gpsimd.memset(ident[:], 0.0).then_inc(ident_zero, 1)
            pool.wait_ge(ident_zero, 1)
            nc.gpsimd.affine_select(out=ident[:], in_=ident[:], compare_op=ALU.not_equal, fill=1.0, base=0,
                                    pattern=[[-1, P]], channel_multiplier=1).then_inc(ident_ready, 1)

            def lo_tiles(name, src, slot):
                for k in range(T):
                    pool.wait_ge(split_hi, SPLIT[name] + k + 1)
                    nc.gpsimd.tensor_tensor(slot[:, 1, k, :], src[:, k, :], slot[:, 0, k, :].bitcast(F32),
                                            ALU.subtract).then_inc(split_done, 1)

            def add_state(b, k, n, first):
                pool.wait_ge(scaled, n + (b * SCANS // 2 + 1))
                if not first:
                    pool.wait_ge(summed, n + (b * SCANS // 2 - 1))
                nc.gpsimd.tensor_tensor(yT[:, k % T, :], yT[:, k % T, :], even_h[b][k // 2 % 2][:], ALU.add).then_inc(summed, 1)

            def attention(b, scan):
                base = b * STEPS

                def natural(t, u):
                    par, j = (u + 2) // T % 2, (u + 2) % T
                    pool.wait_ge(nat_hi, t * UN + (base + u + 2 + 1))
                    nc.gpsimd.tensor_tensor(nat[par][:, 1, j, :], stage[par][:, j, :], nat[par][:, 0, j, :].bitcast(F32),
                                            ALU.subtract).then_inc(nat_split, 1)

                def trip(t, first, last):
                    for u in range(UN):
                        if not (last and u + 2 >= UN):
                            natural(t, u)
                        if scan and u % 2 == 0:
                            add_state(0, u, t * T + u // 2, first and u < T)

                for j in range(2):
                    pool.wait_ge(nat_hi, base + j + 1)
                    nc.gpsimd.tensor_tensor(nat[0][:, 1, j, :], stage[0][:, j, :], nat[0][:, 0, j, :].bitcast(F32),
                                            ALU.subtract).then_inc(nat_split, 1)
                trips(pool, TRIPS, trip)

            def middle(b):
                if b == 0:
                    lo_tiles("qc1", qc1, qc_hl)
                else:
                    gate_output(0)
                pool.wait_ge(resid_ready, b + 1)
                for t in range(T):
                    last = nc.gpsimd.tensor_tensor(resid[b][:, t, :], resid[b][:, t, :], outbB[:], ALU.add)
                last.then_inc(resid_biased, 1)
                if b == 0:
                    pool.wait_ge(inbias_ready, 1)
                else:
                    pool.wait_ge(kept_split, KEPT["gated@0"] + T)
                nc.gpsimd.memset(yT[:], 0.0).then_inc(y_zeroed, 1)
                pool.wait_ge(y_zeroed, b + 1)
                if b == 1:
                    first_weights(0)

            def gate_output(b):
                pool.wait_ge(summed, (b + 1) * SCANS // 2)
                pool.wait_ge(odd_summed, (b + 1) * SCANS // 2)
                pool.wait_ge(z_gated, (b + 1) * T)
                for k in range(T):
                    nc.gpsimd.tensor_tensor(yT[:, k, :], yT[:, k, :], zT[:, k, :], ALU.mult).then_inc(gated, 1)
                for k in range(T):
                    pool.wait_ge(kept_hi, KEPT[f"gated@{b}"] + k + 1)
                    nc.gpsimd.tensor_tensor(hlD[:, 1, k, :], yT[:, k, :], hlD[:, 0, k, :].bitcast(F32),
                                            ALU.subtract).then_inc(kept_split, 1)

            def clear_sums(b):
                pool.wait_ge(filled, JOB["key_bias" if b == 0 else "normT.3@0"] + 1)
                nc.gpsimd.memset(rows[:], 0.0).then_inc(sums_zeroed, 1)
                nc.gpsimd.memset(lsum[:], 0.0).then_inc(sums_zeroed, 1)
                nc.gpsimd.memset(mrun[:, 0], LOWEST).then_inc(sums_zeroed, 1)

            def weights(par, k, count):
                pool.wait_ge(split_hi, count)
                nc.gpsimd.tensor_tensor(weights_hl[par][:, 1, k, :], stage[par][:, k, :],
                                        weights_hl[par][:, 0, k, :].bitcast(F32), ALU.subtract).then_inc(split_done, 1)

            def first_weights(b):
                for k in range(T):
                    weights(0, k, SPLIT[f"W0@{b}"] + k + 1)

            def mix_experts(b, scan):
                split0 = SPLIT[f"W0@{b}"]

                def trip(t, first, last):
                    for u in range(UN):
                        for k in AHEAD[u % T] if not (last and u >= T) else ():
                            weights(1 - u // T, k, t * UN + (split0 + T + u // T * T + k + 1))
                        if scan:
                            add_state(1, 2 * u, t * UN + u, first and 2 * u < T)

                trips(pool, MTRIPS, trip)

            lo_tiles("hW", stage[1], hlB)
            lo_tiles("cW", zT, hlE)
            pool.wait_ge(rows_ready, ROWS["x1"])
            pool.wait_ge(evacuated, JOB["x_bias"] + 1)
            for b in range(B):
                for t in range(T):
                    last = nc.gpsimd.tensor_tensor(xb[:, b, t, :], xb[:, b, t, :], obB[:], ALU.add)
            last.then_inc(x_biased, 1)
            clear_sums(0)
            attention(0, False)
            middle(0)
            clear_sums(1)
            attention(1, True)
            middle(1)
            mix_experts(0, True)
            first_weights(1)
            mix_experts(1, False)


_INS = ["x", "ctx_1024", "L0_xattn_hW", "L0_xattn_hb", "L0_xattn_cW", "L0_xattn_cb", "L0_xattn_qW", "L0_xattn_qb",
        "L0_xattn_kW", "L0_xattn_kb", "L0_xattn_vW", "L0_xattn_vb", "L0_xattn_oW", "L0_xattn_ob", "L0_attn_A_log",
        "L0_attn_B_param", "L0_attn_C_param", "L0_attn_log_dt", "L0_attn_in_w", "L0_attn_in_b", "L0_attn_out_w",
        "L0_attn_out_b", "L0_attn_ln_g", "L0_attn_ln_b", "L0_ffn_gate_w", "L0_ffn_gate_b", "L0_ffn_expert_w",
        "L0_ffn_expert_b"]
_OUTS = [((B, S, D), "float32")]


def kernel(**inputs):
    import numpy as _np
    import concourse.bacc as _bacc
    from concourse import mybir as _mybir
    from concourse.bass_utils import run_bass_kernel_spmd as _run

    nc = _bacc.Bacc("TRN2", target_bir_lowering=False, num_devices=1)
    arrays, args = {}, []
    for name in _INS:
        a = _np.ascontiguousarray(inputs[name])
        arrays[f"in_{name}_dram"] = a
        args.append(nc.dram_tensor(f"in_{name}_dram", a.shape, _mybir.dt.from_np(a.dtype), kind="ExternalInput").ap())
    for i, (shape, dtype) in enumerate(_OUTS):
        dt = _mybir.dt.from_np(_np.dtype(dtype))
        args.append(nc.dram_tensor(f"out_{i}_dram", shape, dt, kind="ExternalOutput").ap())
    build(nc, *args)
    r = _run(nc, [arrays], core_ids=[0])
    got = tuple(r.results[0][f"out_{i}_dram"] for i in range(len(_OUTS)))
    return got[0]
```

```python
from contextlib import ExitStack

import concourse.bass as bass
from concourse import mybir

F32 = mybir.dt.float32
F32R = mybir.dt.float32r
I32 = mybir.dt.int32
ALU = mybir.AluOpType
ACT = mybir.ActivationFunctionType
AX_X = mybir.AxisListType.X

P = 128
B, S, D = 2, 512, 512
T = D // P
L = 8192
BLOCKS = L // P - T
CH = 512
NCH = L // CH
NS = 16
E = 8
UN = 8
STEPS = NCH * T
TRIPS = STEPS // UN
SCANS = NS * T
EARLY = 2 * T
MTRIPS = E * T // UN
GROUPS = [(range(0, 2), range(2, 4)), (range(T),)]
AHEAD = ((0, 1), (2, 3), (), ())
NBANK = 8
EPS = 1e-5
SCALE = float(D) ** -0.5
LOWEST = -3.0e38
PASSES = ((0, 0), (0, 1), (1, 0))
EXPM1_DOUBLINGS = 8
RSQRT_SEED = float(0x5F3759DF)



def tiles(*names):
    return [f"{n}.{k}" for n in names for k in range(T)]


def mid_jobs(b):
    names = [f"{n}@{b}" for n in tiles("inT0", "pooledT", "inT1")]
    names += tiles("outT") * b
    names += [f"{n}@{b}" for n in tiles("x_attn")]
    mixed = [f"{n}@0" for n in tiles("x_ssm")] * b
    names += mixed[:-1] + [f"{n}@{b}" for n in tiles("normT")] + mixed[-1:] + [f"{n}@{b}" for n in tiles("u")]
    names += [f"{n}@1" for n in tiles("ctx0T")] * (1 - b)
    z = [f"{n}@{b}" for n in tiles("z")]
    names += z[:-1] + [f"{n}@0" for n in tiles("ffnT")] * b + z[-1:]
    return names + [f"{n}@0" for n in ["logits", "logit_columns"]] * b


def expert_jobs(b):
    experts = [f"expert.{n}@{b}" for n in range(E * T)]
    return experts[:-UN] + ([f"onehotT@{b}"] + [f"{n}@{b}" for n in tiles("expert_bias")]) * b + experts[-UN:]


PREP_JOBS = (tiles("qWT", "x_to_q", "xT0") + ["vectors"] + tiles("kWT", "q0", "xT1", "q_to_ctx", "q1", "qc0", "vWT", "qc1")
             + tiles("ctx_to_v", "oWT") + ["key_row.0", "key_row.1", "x_bias", "key_bias"] + tiles("ctx_to_x", "qo0")
             + [f"{n}@0" for n in tiles("ctx0T")] + tiles("qo1"))
JOBS = (PREP_JOBS + mid_jobs(0) + mid_jobs(1) + expert_jobs(0)
        + ["onehotT@0"] + [f"{n}@1" for n in tiles("x_ssm")] + [f"{n}@0" for n in tiles("expert_bias")[:T // 2]]
        + [f"{n}@1" for n in tiles("ffnT")] + [f"{n}@0" for n in tiles("expert_bias")[T // 2:]]
        + [f"{n}@1" for n in ["logits", "logit_columns"]] + expert_jobs(1))
JOB = {name: n for n, name in enumerate(JOBS)}
AFTER = [JOB[f"inT0.0@{b}"] for b in range(B)]
BANK = [(n - AFTER[int(n >= AFTER[1])] + 6) % NBANK for n in range(len(JOBS))]
ROUNDED_KINDS = ("xT0", "xT1", "qWT", "x_to_q", "kWT", "q_to_ctx", "qc0", "vWT", "ctx_to_v", "oWT", "ctx_to_x",
                 "pooledT", "inT0", "inT1", "outT", "ffnT", "normT", "ctx0T")
ROUND = {name: k for k, name in enumerate(n for n in JOBS if n.split(".")[0] in ROUNDED_KINDS)}
TAKEN = {f"{n}@{b}": (b * 2 + m) * T + k for b in range(B) for m, kind in enumerate("uz") for k, n in enumerate(tiles(kind))}
SPLITS = ["cW", "qc1"] + [f"W{e}@{b}" for b in range(B) for e in range(E)]
SPLIT = {name: T * n for n, name in enumerate(SPLITS)}
KEPT = {name: T * n for n, name in enumerate(["hW", "q0", "q1", "gated@0", "gated@1"])}
ROWS = {name: 2 * n + 1 for n, name in enumerate(["x0", "x1", "norm@0", "norm@1", "ffn@0", "ffn@1"])}
LOADS = [("hW", 1), ("oW", 0)]
for _b in range(B):
    LOADS += [(f"chunk{_c}@{_b}", _c % 2) for _c in range(NCH)] + [(f"in0@{_b}", 0), (f"in1@{_b}", 1)]
LOADS += [("out_w", 0)]
for _b in range(B):
    LOADS += [(f"W{_e}@{_b}", _e % 2) for _e in range(E)]
BUF, LANDED = {}, {}
_seen = [0, 0]
for _name, _buf in LOADS:
    _seen[_buf] += 1
    BUF[_name], LANDED[_name] = _buf, 16 * _seen[_buf]


def build(nc, x, ctx_in, hW, hb, cW, cb, qW, qb, kW, kb, vW, vb, oW, ob, A_log, B_param, C_param, log_dt,
          in_w, in_b, out_w, out_b, ln_g, ln_b, gate_w, gate_b, expert_w, expert_b, out):
    with ExitStack() as ctx:
        def sb(name, shape, dt=F32):
            return ctx.enter_context(nc.sbuf_tensor(name, shape, dt))

        def sem(name):
            return ctx.enter_context(nc.semaphore(name))

        hlA, hlB, hlC, hlD, hlE, hlF = (sb(f"hl_{n}", [P, 2, T, D], F32R) for n in "ABCDEF")
        nat = [hlA, hlF]
        ctxT = [hlB, hlC]
        qc_hl = hlD
        ctx_to_x = hlE
        weights_hl = [hlE, hlB]
        vbias_hl = sb("vbias_hl", [P, 2, T], F32R)
        kbias_hl = sb("kbias_hl", [P, 2, T, 2], F32R)
        probsT = [sb(f"probsT{n}", [P, 2, T, P], F32R) for n in range(2)]
        stage = [sb(f"stage{n}", [P, T, D]) for n in range(2)]
        probs = [sb(f"probs{n}", [P, CH]) for n in range(2)]
        rows = sb("rows", [P, T, D])
        qc1 = sb("qc1", [P, T, S])
        xb = sb("xb", [P, B, T, D])
        uT = sb("uT", [P, T, S])
        zT = sb("zT", [P, T, S])
        yT = sb("yT", [P, T, S])
        h = [sb(f"h{n}", [P, S]) for n in range(2)]
        even_h = [[h[0], h[0]], [h[0], probs[0]]]
        resid0 = sb("resid0", [P, T, D])
        resid = [resid0, qc1]
        qT = [rows, resid0]
        ident = sb("ident", [P, P])
        obB = sb("obB", [P, D])
        outbB = sb("outbB", [P, D])
        eb = qc1[0:E, 0, :]
        eb_hl = sb("eb_hl", [E, 2, D], F32R)
        onehotT = sb("onehotT", [E, T * P], F32R)
        logitT = probs[1]
        key_row = [h[1], probs[1]]
        vrows = sb("vrows", [32, P])
        vecs = sb("vecs", [P, 32])
        gate_raw = sb("gate_raw", [P, T, E])
        gate_hl = sb("gate_hl", [P, 2, T, E], F32R)
        gbB = sb("gbB", [P, E])
        desc = sb("desc", [P, E])
        logit = sb("logit", [P, T, E])
        pick = sb("pick", [P, T, E])
        onehot = sb("onehot", [P, T, E])
        lmax = sb("lmax", [P, 2, T])
        bnst = sb("bnst", [P, T, 6])
        mv = sb("mv", [P, T, 2])
        rstd = sb("rstd", [P, 2, T])
        var = sb("var", [P, 2, T])
        seed = sb("seed", [P, 2, T], I32)
        newton = sb("newton", [P, 2, T])
        inbias = sb("inbias", [P, 2 * T])
        qbias = sb("qbias", [P, T])
        kbias = sb("kbias", [P, T])
        vbias = sb("vbias", [P, T])
        kq = sb("kq", [P, B * T])
        mrun = sb("mrun", [P, 2, T])
        mx = sb("mx", [P, T])
        nbias = sb("nbias", [P, T])
        dmax = sb("dmax", [P, T])
        alpha = sb("alpha", [P, T])
        rsum = sb("rsum", [P, T])
        lsum = sb("lsum", [P, T])
        ssm_in = sb("ssm_in", [P, 3, T, NS])
        ssm_w = sb("ssm_w", [P, 4, T, NS])
        dtv = sb("dtv", [P, T])
        tick = sb("tick", [P, 2 * B * T])
        abar = sb("abar", [P, NS, T])
        cbdt = sb("cbdt", [P, NS, T])

        bank = [ctx.enter_context(nc.psum_tensor(f"bank{n}", [P, 512], F32)) for n in range(NBANK)]
        sbank, tbank, obank, cbank = bank[0:2], bank[2:4], bank[4:6], bank[6:8]

        in_x = [sem(f"in_x{b}") for b in range(B)]
        in_q = [sem(f"in_q{half}") for half in range(2)]
        in_stage = [sem(f"in_stage{n}") for n in range(2)]
        in_k, in_c, in_v, in_vec, in_bias, in_ssm, in_small = (sem(n) for n in (
            "in_k", "in_c", "in_v", "in_vec", "in_bias", "in_ssm", "in_small"))
        stored = sem("stored")
        ident_zero, ident_ready, desc_ready = sem("ident_zero"), sem("ident_ready"), sem("desc_ready")
        filled, rounded, evacuated = sem("filled"), sem("rounded"), sem("evacuated")
        split_hi, split_done = sem("split_hi"), sem("split_done")
        gated, kept_hi, kept_split = sem("gated"), sem("kept_hi"), sem("kept_split")
        rows_ready = sem("rows_ready")
        link_done = sem("link_done")
        vectors_ready, ssm_exp, gate_ready, kbias_ready = (sem(n) for n in (
            "vectors_ready", "ssm_exp", "gate_ready", "kbias_ready"))
        vbias_ready, bias_row_ready = sem("vbias_ready"), sem("bias_row_ready")
        x_biased, resid_ready, resid_biased = sem("x_biased"), sem("resid_ready"), sem("resid_biased")
        taken, y_zeroed, onehot_ready = sem("taken"), sem("y_zeroed"), sem("onehot_ready")
        sums_zeroed, inbias_ready, in_lnb = sem("sums_zeroed"), sem("inbias_ready"), sem("in_lnb")
        scores_ready, stat_done, max_ready, dmax_ready, probs_ready, alpha_ready = (sem(n) for n in (
            "scores_ready", "stat_done", "max_ready", "dmax_ready", "probs_ready", "alpha_ready"))
        pT_ready, pT_hi, pT_split = sem("pT_ready"), sem("pT_hi"), sem("pT_split")
        cT_ready, cT_hi, cT_split = sem("cT_ready"), sem("cT_hi"), sem("cT_split")
        nat_hi, nat_split = sem("nat_hi"), sem("nat_split")
        pv_ready, sums_updated = sem("pv_ready"), sem("sums_updated")
        scanned, scaled, summed = sem("scanned"), sem("scaled"), sem("summed")
        odd_scanned, odd_summed = sem("odd_scanned"), sem("odd_summed")

        block = ctx.enter_context(nc.Block())

        def matrix(w):
            return w.rearrange("(t p) n -> p t n", p=P)

        def across(v):
            return v.rearrange("(a n) -> a n", a=1).partition_broadcast(P)

        ctx_rows = ctx_in.rearrange("b (c p j) d -> (b c) p j d", p=P, j=T)
        experts = expert_w.rearrange("e (t p) n -> e p t n", p=P)

        def wait_pos(eng, s, base, value):
            if not isinstance(value, int) or value > 0:
                eng.wait_ge(s, value + base)

        def job_base(b, last):
            n = E * T - UN if last else 0
            return JOB[f"expert.{n}@{b}"] - n

        def scans_done(u, first, last):
            return first and u < EARLY // 4 or last and u >= UN - EARLY // 4

        def expert_bank(b, n):
            n0 = JOB[f"expert.0@{b}"]
            return bank[BANK[n0 + (n - n0) % NBANK]]

        def trips(eng, n, body):
            body(0, True, False)
            with eng.Fori(1, n - 1) as t:
                body(t, False, False)
            body(n - 1, False, True)

        @block.sync
        def _(sp):
            def load(name, src):
                sp.dma_start(stage[BUF[name]][:], src).then_inc(in_stage[BUF[name]], 16)

            for half in range(2):
                two = slice(2 * half, 2 * half + 2)
                sp.dma_start(stage[0][:, two], matrix(qW)[:, two]).then_inc(in_q[half], 16)
            load("hW", matrix(hW))
            sp.dma_start(xb[:, 0], matrix(x[0])).then_inc(in_x[0], 16)
            sp.dma_start(zT[:], matrix(cW)).then_inc(in_c, 16)
            sp.dma_start(uT[:], matrix(kW)).then_inc(in_k, 16)
            sp.dma_start(xb[:, 1], matrix(x[1])).then_inc(in_x[1], 16)
            sp.dma_start(yT[:], matrix(vW)).then_inc(in_v, 16)
            for k, v in ((0, qb), (4, kb), (8, vb), (12, in_b), (20, ln_g), (24, ln_b), (28, log_dt)):
                n = v.shape[0] // P
                sp.dma_start(vrows[k:k + n, :], v.rearrange("(t p) -> t p", p=P)).then_inc(in_vec, 16)
            sp.dma_start(probs[0][:], across(hb)).then_inc(in_bias, 16)
            sp.dma_start(probs[1][:], across(cb)).then_inc(in_bias, 16)
            for k, v in enumerate((A_log, B_param, C_param)):
                sp.dma_start(ssm_in[:, k], matrix(v)).then_inc(in_ssm, 16)
            sp.dma_start(obB[:], across(ob)).then_inc(in_small, 16)
            sp.dma_start(outbB[:], across(out_b)).then_inc(in_small, 16)
            sp.dma_start(gbB[:], across(gate_b)).then_inc(in_small, 16)
            sp.dma_start(gate_raw[:], matrix(gate_w)).then_inc(in_small, 16)
            sp.dma_start(eb, expert_b).then_inc(in_small, 16)

            def attention_loads(b):
                base, blocks = b * STEPS, b * BLOCKS
                sp.wait_ge(filled, JOB[f"ctx0T.3@{b}"] + 1)
                for c in range(2, NCH):
                    if c > 2:
                        sp.wait_ge(cT_ready, blocks + T * (c - 2))
                    sp.wait_ge(nat_split, base + T * (c - 1))
                    load(f"chunk{c}@{b}", ctx_rows[b * NCH + c])
                for c in range(2):
                    sp.wait_ge(cT_ready, blocks + BLOCKS - T + T * c)
                    sp.wait_ge(nat_split, base + STEPS - T + T * c)
                    load(f"in{c}@{b}", matrix(in_w[c * D:(c + 1) * D]))

            def expert_loads(b):
                if b == 0:
                    sp.wait_ge(filled, JOB["outT.3"] + 1)
                else:
                    sp.wait_ge(split_done, SPLIT[f"W{E - 2}@0"] + T)
                load(f"W0@{b}", experts[0])
                if b == 0:
                    sp.wait_ge(filled, JOB["inT1.3@1"] + 1)
                else:
                    sp.wait_ge(split_done, SPLIT[f"W{E - 1}@0"] + T)
                load(f"W1@{b}", experts[1])
                for e in range(2, E):
                    sp.wait_ge(split_done, SPLIT[f"W{e - 2}@{b}"] + T)
                    load(f"W{e}@{b}", experts[e])

            sp.wait_ge(filled, JOB["qWT.3"] + 1)
            sp.wait_ge(evacuated, JOB["q0.0"] + 1)
            load("oW", matrix(oW))
            sp.dma_start(probs[0][:], across(ln_b)).then_inc(in_lnb, 16)
            sp.wait_ge(kept_split, KEPT["hW"] + T)
            load("chunk1@0", ctx_rows[1])
            sp.wait_ge(filled, JOB["kWT.3"] + 1)
            sp.wait_ge(kbias_ready, 1)
            sp.dma_start(uT[:], matrix(in_w[0:D])).then_inc(in_k, 16)
            sp.wait_ge(filled, JOB["vWT.3"] + 1)
            sp.wait_ge(vbias_ready, 1)
            sp.dma_start(yT[:], matrix(in_w[D:2 * D])).then_inc(in_v, 16)
            sp.wait_ge(filled, JOB["oWT.3"] + 1)
            load("chunk0@0", ctx_rows[0])
            attention_loads(0)
            for c in range(2):
                sp.wait_ge(filled, JOB[f"inT{c}.3@0"] + 1)
                load(f"chunk{c}@1", ctx_rows[NCH + c])
            attention_loads(1)
            sp.wait_ge(filled, JOB["inT0.3@1"] + 1)
            load("out_w", matrix(out_w))
            expert_loads(0)
            expert_loads(1)
            sp.wait_ge(evacuated, JOB[f"expert_bias.{T - 1}@0"] + 1)
            sp.dma_start(matrix(out[0]), xb[:, 0]).then_inc(stored, 16)
            for t in range(T):
                sp.wait_ge(evacuated, JOB[f"expert.{E * T - T + t}@1"] + 1)
                sp.dma_start(matrix(out[1])[:, t], xb[:, 1, t]).then_inc(stored, 16)
            sp.wait_ge(stored, 16 * (1 + T))

        @block.tensor
        def _(pe):
            def open_bank(name):
                n = JOB[name]
                if n >= NBANK:
                    pe.wait_ge(evacuated, n - NBANK + 1)
                return bank[BANK[n]]

            def product(dst, lhs, k, rhs, kept=None, turned_by=None):
                for t in range(T):
                    if kept is not None:
                        pe.wait_ge(kept_split, KEPT[kept] + t + 1)
                    if turned_by is not None:
                        evacuated_from(f"{turned_by}.{t}")
                    for a, c in PASSES:
                        last = nc.tensor.matmul(dst, lhs[:, a, t, k * P:(k + 1) * P], rhs[:, c, t, :],
                                                start=(t == 0 and (a, c) == PASSES[0]),
                                                stop=(t == T - 1 and (a, c) == PASSES[-1]))
                return last

            def turned(dst, src, k):
                for t in range(T):
                    last = nc.tensor.transpose(dst[:, t * P:(t + 1) * P], src[:, t, k * P:(k + 1) * P], ident[:])
                return last

            def evacuated_from(name):
                pe.wait_ge(evacuated, JOB[name] + 1)

            def split_of(name):
                pe.wait_ge(split_done, SPLIT[name] + T)

            def kept_split_of(name):
                pe.wait_ge(kept_split, KEPT[name] + T)

            def transposes(name, src):
                for k in range(T):
                    job = name.replace("#", str(k))
                    turned(open_bank(job), src, k).then_inc(filled, 1)

            def row_transposes(name, src, first):
                for k in range(T):
                    pe.wait_ge(rows_ready, first + k // 2)
                    turn_rows(name.replace("#", str(k)), src, k)

            def turn_rows(job, src, k):
                dst = open_bank(job)
                for t in range(T):
                    last = nc.tensor.transpose(dst[:, t * P:(t + 1) * P], src[:, k, t * P:(t + 1) * P], ident[:])
                last.then_inc(filled, 1)

            def products(name, lhs, rhs):
                for k in range(T):
                    job = name.replace("#", str(k))
                    product(open_bank(job)[:], lhs, k, rhs).then_inc(filled, 1)

            def prepare():
                pe.wait_ge(ident_ready, 1)
                for half in range(2):
                    pe.wait_ge(in_q[half], 16)
                    for k in range(T):
                        dst = open_bank(f"qWT.{k}")
                        for t in (2 * half, 2 * half + 1):
                            last = nc.tensor.transpose(dst[:, t * P:(t + 1) * P], stage[0][:, t, k * P:(k + 1) * P], ident[:])
                        if half == 1:
                            last.then_inc(filled, 1)
                for k in range(T):
                    product(open_bank(f"x_to_q.{k}")[:], hlB, k, hlA, kept="hW" if k == 0 else None,
                            turned_by="qWT" if k == 0 else None).then_inc(filled, 1)
                row_transposes("xT0.#", rows, ROWS["x0"])
                pe.wait_ge(in_vec, 16 * 7)
                nc.tensor.transpose(open_bank("vectors")[:, 0:32], vrows[:], ident[0:32, 0:32]).then_inc(filled, 1)
                pe.wait_ge(in_k, 16)
                transposes("kWT.#", uT)
                evacuated_from("xT0.3")
                products("q0.#", hlC, hlD)
                row_transposes("xT1.#", resid0, ROWS["x1"])
                split_of("cW")
                products("q_to_ctx.#", hlF, hlE)
                evacuated_from("xT1.3")
                products("q1.#", hlC, hlD)
                kept_split_of("q0")
                evacuated_from("q_to_ctx.3")
                products("qc0.#", hlB, hlA)
                pe.wait_ge(in_v, 16)
                transposes("vWT.#", yT)
                kept_split_of("q1")
                products("qc1.#", hlB, hlF)
                evacuated_from("vWT.3")
                products("ctx_to_v.#", hlC, hlE)
                pe.wait_ge(in_stage[0], LANDED["oW"])
                transposes("oWT.#", stage[0])
                pe.wait_ge(kbias_ready, 1)
                for n in range(B):
                    dst = open_bank(f"key_row.{n}")
                    for t in range(T):
                        for a, c in PASSES:
                            last = nc.tensor.matmul(dst[0:2, :], kbias_hl[:, a, t, :], (hlA, hlF)[n][:, c, t, :],
                                                    start=(t == 0 and (a, c) == PASSES[0]),
                                                    stop=(t == T - 1 and (a, c) == PASSES[-1]))
                    last.then_inc(filled, 1)
                evacuated_from("oWT.3")
                pe.wait_ge(vbias_ready, 1)
                dst = open_bank("x_bias")
                for t in range(T):
                    for a, c in PASSES:
                        last = nc.tensor.matmul(dst[:], vbias_hl[:, a, t:t + 1].to_broadcast([P, P]), hlC[:, c, t, :],
                                                start=(t == 0 and (a, c) == PASSES[0]),
                                                stop=(t == T - 1 and (a, c) == PASSES[-1]))
                last.then_inc(filled, 1)
                evacuated_from("key_row.1")
                dst = open_bank("key_bias")
                for n in range(B * T):
                    last = nc.tensor.transpose(dst[:, 2 * n:2 * n + 2], key_row[n // T][0:2, n % T * P:(n % T + 1) * P],
                                               ident[0:2, 0:2])
                last.then_inc(filled, 1)
                products("ctx_to_x.#", hlB, hlC)
                products("qo0.#", hlA, hlC)
                pe.wait_ge(in_stage[0], LANDED["chunk0@0"])
                transposes("ctx0T.#@0", stage[0])
                products("qo1.#", hlF, hlC)

            def attention(b, jobs_before):
                base, blocks = b * STEPS, b * BLOCKS
                load0 = [LANDED[f"chunk0@{b}"], LANDED[f"chunk1@{b}"]]

                def context_block(t, u):
                    par, dd = (u // T + 1) % 2, u % T
                    if dd == 0:
                        pe.wait_ge(in_stage[par], (t + (u // T + 1) // 2) * 16 + load0[par])
                    wait_pos(pe, cT_split, blocks, t * UN + (u - 1))
                    turned(cbank[dd % 2], stage[par], dd).then_inc(cT_ready, 1)

                def scores(t, u):
                    par, q = u // T % 2, u % T
                    if q == 0:
                        wait_pos(pe, cT_split, blocks, t * UN + u)
                    wait_pos(pe, probs_ready, base, t * UN + (u - 1))
                    product(sbank[u % 2][:], qc_hl, q, ctxT[par]).then_inc(scores_ready, 1)

                def turn_probs(t, u):
                    pe.wait_ge(probs_ready, t * UN + (base + u + 1))
                    wait_pos(pe, pT_split, base, t * UN + (u - 1))
                    for j in range(T):
                        last = nc.tensor.transpose(tbank[u % 2][:, j * P:(j + 1) * P],
                                                   probs[u % 2][:, j * P:(j + 1) * P], ident[:])
                    last.then_inc(pT_ready, 1)

                def weigh(t, u):
                    par = u // T % 2
                    pe.wait_ge(pT_split, t * UN + (base + u + 1))
                    if u % T == 0:
                        pe.wait_ge(nat_split, t * UN + (base + u + T))
                    wait_pos(pe, sums_updated, 2 * base, t * (2 * UN) + 2 * (u - 1))
                    for j in range(T):
                        for a, c in PASSES:
                            last = nc.tensor.matmul(obank[u % 2][:], probsT[u % 2][:, a, j, :], nat[par][:, c, j, :],
                                                    start=(j == 0 and (a, c) == PASSES[0]),
                                                    stop=(j == T - 1 and (a, c) == PASSES[-1]))
                    last.then_inc(pv_ready, 1)

                def back(t, u, n):
                    return (t, u - n) if u >= n else (t - 1, u - n + UN)

                def trip(t, first, last):
                    for u in range(UN):
                        if not (last and u >= T):
                            context_block(t, u)
                        scores(t, u)
                        if first and u == 1:
                            pe.wait_ge(evacuated, jobs_before)
                        if not (first and u < 1):
                            turn_probs(*back(t, u, 1))
                        if not (first and u < 2):
                            weigh(*back(t, u, 2))

                if b == 1:
                    split_of("qc1")
                pe.wait_ge(evacuated, jobs_before - T)
                trips(pe, TRIPS, trip)
                turn_probs(TRIPS - 1, UN - 1)
                weigh(TRIPS - 1, UN - 2)
                pe.wait_ge(in_stage[0], LANDED[f"in0@{b}"])
                pe.wait_ge(cT_split, blocks + BLOCKS)
                pe.wait_ge(probs_ready, base + STEPS)
                transposes(f"inT0.#@{b}", stage[0])
                weigh(TRIPS - 1, UN - 1)

            def middle(b):
                for k in range(T):
                    pe.wait_ge(sums_updated, 2 * ((b + 1) * STEPS - T + k + 1))
                    turn_rows(f"pooledT.{k}@{b}", rows, k)
                pe.wait_ge(in_stage[1], LANDED[f"in1@{b}"])
                transposes(f"inT1.#@{b}", stage[1])
                if b == 1:
                    pe.wait_ge(in_stage[0], LANDED["out_w"])
                    transposes("outT.#", stage[0])
                for k in range(T):
                    evacuated_from(f"pooledT.{k}@{b}")
                    product(open_bank(f"x_attn.{k}@{b}")[:], hlA, k, ctx_to_x).then_inc(filled, 1)
                if b == 1:
                    project_out(0, range(T - 1))
                normT = hlF if b == 0 else hlA
                if b == 0:
                    for half in range(2):
                        for k in (2 * half, 2 * half + 1):
                            pe.wait_ge(rows_ready, ROWS["norm@0"] + half)
                            turn_rows(f"normT.{k}@0", rows, k)
                        evacuated_from(f"normT.{2 * half + 1}@0")
                        cols = slice(half * S // 2, (half + 1) * S // 2)
                        for k in range(T):
                            dst = open_bank(f"u.{k}@0") if half == 0 else bank[BANK[JOB[f"u.{k}@0"]]]
                            last = product(dst[:, cols], hlB, k, normT[:, :, :, cols])
                            if half == 1:
                                last.then_inc(filled, 1)
                else:
                    row_transposes("normT.#@1", rows, ROWS["norm@1"])
                    project_out(0, range(T - 1, T))
                    evacuated_from("normT.3@1")
                    products("u.#@1", hlB, normT)
                if b == 0:
                    pe.wait_ge(in_stage[0], LANDED["chunk0@1"])
                    transposes("ctx0T.#@1", stage[0])
                for k in range(T):
                    if b == 1 and k == T - 1:
                        turn_ffn(0)
                    product(open_bank(f"z.{k}@{b}")[:], hlC, k, normT).then_inc(filled, 1)
                if b == 1:
                    gate_logits(0)

            def project_out(b, ks):
                evacuated_from("outT.3")
                for k in ks:
                    product(open_bank(f"x_ssm.{k}@{b}")[:], hlD if b == 0 else hlC, k, hlF,
                            kept=f"gated@{b}" if k == 0 else None).then_inc(filled, 1)

            def turn_ffn(b):
                row_transposes(f"ffnT.#@{b}", rows, ROWS[f"ffn@{b}"])

            def gate_logits(b):
                evacuated_from(f"ffnT.3@{b}")
                pe.wait_ge(gate_ready, 1)
                dst = open_bank(f"logits@{b}")
                for t in range(T):
                    for a, c in PASSES:
                        last = nc.tensor.matmul(dst[0:E, :], gate_hl[:, a, t, :], hlD[:, c, t, :],
                                                start=(t == 0 and (a, c) == PASSES[0]),
                                                stop=(t == T - 1 and (a, c) == PASSES[-1]))
                last.then_inc(filled, 1)
                evacuated_from(f"logits@{b}")
                dst = open_bank(f"logit_columns@{b}")
                for k in range(T):
                    last = nc.tensor.transpose(dst[:, k * E:(k + 1) * E], logitT[0:E, k * P:(k + 1) * P], ident[0:E, 0:E])
                last.then_inc(filled, 1)

            def mix_experts(b):
                split0 = SPLIT[f"W0@{b}"]

                def trip(t, job0):
                    for u in range(UN):
                        if u % T == 0:
                            pe.wait_ge(split_done, t * UN + (split0 + u + T))
                        pe.wait_ge(evacuated, t * UN + (job0 + u - NBANK + 1))
                        product(expert_bank(b, job0 + u)[:], hlD, u % T, weights_hl[u // T]).then_inc(filled, 1)

                with pe.Fori(0, MTRIPS - b) as t:
                    trip(t, JOB[f"expert.0@{b}"])
                if b == 1:
                    turn_onehot(1)
                    expert_biases(1, range(T))
                    trip(MTRIPS - 1, job_base(1, True))

            def turn_onehot(b):
                pe.wait_ge(onehot_ready, b + 1)
                dst = open_bank(f"onehotT@{b}")
                for k in range(T):
                    last = nc.tensor.transpose(dst[0:E, k * P:(k + 1) * P], onehot[:, k, :], ident[:])
                last.then_inc(filled, 1)

            def expert_biases(b, ks):
                evacuated_from(f"onehotT@{b}")
                for k in ks:
                    dst = open_bank(f"expert_bias.{k}@{b}")
                    for c in range(2):
                        last = nc.tensor.matmul(dst[:], onehotT[:, k * P:(k + 1) * P], eb_hl[:, c, :], start=(c == 0), stop=(c == 1))
                    last.then_inc(filled, 1)

            prepare()
            attention(0, len(PREP_JOBS))
            middle(0)
            attention(1, JOB["z.3@0"] + 1)
            middle(1)
            mix_experts(0)
            turn_onehot(0)
            project_out(1, range(T))
            expert_biases(0, range(T // 2))
            turn_ffn(1)
            expert_biases(0, range(T // 2, T))
            gate_logits(1)
            mix_experts(1)

        @block.scalar
        def _(act):
            def round_job(name, dst):
                act.wait_ge(filled, JOB[name] + 1)
                nc.scalar.activation(dst, bank[BANK[JOB[name]]][:], ACT.Copy).then_inc(rounded, 1)

            def round_jobs(name, slot):
                for k in range(T):
                    round_job(name.replace("#", str(k)), slot[:, 0, k, :])

            def round_rows(name, slot):
                for k in range(T):
                    job = name.replace("#", str(k))
                    act.wait_ge(filled, JOB[job] + 1)
                    nc.scalar.activation(slot[:, 0, :, k * P:(k + 1) * P],
                                         bank[BANK[JOB[job]]][:].rearrange("p (t q) -> p t q", t=T), ACT.Copy).then_inc(rounded, 1)

            def round_scaled(name, slot):
                for k in range(T):
                    job = name.replace("#", str(k))
                    act.wait_ge(filled, JOB[job] + 1)
                    nc.scalar.activation(slot[:, 0, k, :], bank[BANK[JOB[job]]][:], ACT.Copy,
                                         scale=vecs[:, 20 + k:21 + k]).then_inc(rounded, 1)

            def round_tiles(src, slot):
                for k in range(T):
                    nc.scalar.activation(slot[:, 0, k, :], src[:, k, :], ACT.Copy).then_inc(split_hi, 1)

            def round_kept(ready, count, src, slot):
                for k in range(T):
                    act.wait_ge(ready, count + k + 1)
                    nc.scalar.activation(slot[:, 0, k, :], src[:, k, :], ACT.Copy).then_inc(kept_hi, 1)

            def prepare():
                round_jobs("qWT.#", hlA)
                act.wait_ge(in_stage[1], LANDED["hW"])
                for k in range(T):
                    nc.scalar.activation(hlB[:, 0, k, :], stage[1][:, k, :], ACT.Copy).then_inc(kept_hi, 1)
                act.wait_ge(in_c, 16)
                round_tiles(zT, hlE)
                round_jobs("x_to_q.#", hlC)
                round_rows("xT0.#", hlD)
                round_jobs("kWT.#", hlF)
                round_kept(evacuated, JOB["q0.0"], qT[0], hlA)
                round_rows("xT1.#", hlD)
                act.wait_ge(in_ssm, 16 * 3)
                act.wait_ge(vectors_ready, 1)
                nc.scalar.activation(ssm_w[:, 0], ssm_in[:, 0], ACT.Exp).then_inc(ssm_exp, 1)
                nc.scalar.activation(dtv[:], vecs[:, 28:32], ACT.Exp).then_inc(ssm_exp, 1)
                round_jobs("q_to_ctx.#", hlB)
                round_kept(evacuated, JOB["q1.0"], qT[1], hlF)
                round_jobs("qc0.#", hlD)
                round_jobs("vWT.#", hlC)
                round_jobs("ctx_to_v.#", hlB)
                round_jobs("oWT.#", hlC)
                round_jobs("ctx_to_x.#", ctx_to_x)
                round_jobs("ctx0T.#@0", ctxT[0])

            def attention(b, jobs_before, scan):
                base, blocks = b * STEPS, b * BLOCKS
                load0 = [LANDED[f"chunk0@{b}"], LANDED[f"chunk1@{b}"]]

                def natural(t, u):
                    g = u + 2
                    par, j = g // T % 2, g % T
                    if j == 0 or (j == 2 and u == 0):
                        act.wait_ge(in_stage[par], (t + g // T // 2) * 16 + load0[par])
                    wait_pos(act, pv_ready, base, t * UN + (g // T - 1) * T)
                    nc.scalar.activation(nat[par][:, 0, j, :], stage[par][:, j, :], ACT.Copy).then_inc(nat_hi, 1)

                def context_block(t, u):
                    par, dd = (u // T + 1) % 2, u % T
                    act.wait_ge(cT_ready, t * UN + (blocks + u + 1))
                    nc.scalar.activation(ctxT[par][:, 0, dd, :], cbank[dd % 2][:], ACT.Copy).then_inc(cT_hi, 1)

                def turned_probs(t, u):
                    act.wait_ge(pT_ready, t * UN + (base + u + 1))
                    nc.scalar.activation(probsT[u % 2][:, 0], tbank[u % 2][:].rearrange("p (j q) -> p j q", j=T),
                                         ACT.Copy).then_inc(pT_hi, 1)

                def exponentials(t, u):
                    q = u % T
                    wait_pos(act, pT_ready, base, t * UN + (u - 1))
                    wait_pos(act, sums_updated, 2 * base, t * (2 * UN) + 2 * (u - 3))
                    act.wait_ge(max_ready, t * UN + (base + u + 1))
                    nc.scalar.activation(probs[u % 2][:], sbank[u % 2][:], ACT.Exp, bias=nbias[:, q:q + 1], scale=SCALE,
                                         accum_out=rsum[:, q:q + 1]).then_inc(probs_ready, 1)
                    act.wait_ge(dmax_ready, t * UN + (base + u + 1))
                    nc.scalar.activation(alpha[:, q:q + 1], dmax[:, q:q + 1], ACT.Exp, scale=SCALE).then_inc(alpha_ready, 1)

                def trip(t, first, last):
                    for u in range(UN):
                        if not (last and u >= T):
                            context_block(t, u)
                        exponentials(t, u)
                        if not (first and u < 1):
                            turned_probs(*((t, u - 1) if u else (t - 1, UN - 1)))
                        if not (last and u + 2 >= UN):
                            natural(t, u)
                        if scan and u % 2 == 0:
                            scale_state(0, t * UN + u, t * T + u // 2, u // 2)

                act.wait_ge(filled, jobs_before)
                act.wait_ge(in_stage[0], load0[0])
                for j in range(2):
                    nc.scalar.activation(nat[0][:, 0, j, :], stage[0][:, j, :], ACT.Copy).then_inc(nat_hi, 1)
                trips(act, TRIPS, trip)
                turned_probs(TRIPS - 1, UN - 1)

            def scale_state(b, s, n, k):
                act.wait_ge(scanned, n + (b * SCANS // 2 + 1))
                col = cbdt[:].rearrange("p n d -> p (n d)")[:, bass.ds(s, 1)]
                nc.scalar.activation(even_h[b][k % 2][:], even_h[b][k % 2][:], ACT.Copy, scale=col).then_inc(scaled, 1)

            def middle(b):
                round_scaled(f"inT0.#@{b}", hlB)
                round_rows(f"pooledT.#@{b}", hlA)
                round_scaled(f"inT1.#@{b}", hlC)
                if b == 0:
                    act.wait_ge(scores_ready, STEPS)
                    round_tiles(qc1, qc_hl)
                else:
                    round_jobs("outT.#", hlF)
                    round_kept(gated, 0 * T, yT, hlD)
                round_rows(f"normT.#@{b}", hlF if b == 0 else hlA)
                scan_inputs(b)
                if b == 0:
                    round_jobs("ctx0T.#@1", ctxT[0])
                    gates(0, range(T))
                else:
                    first_weights(0)
                    gates(1, range(T - 1))
                    for n in range(EARLY // 4):
                        scale_state(1, 2 * n, n, n)
                    round_rows("ffnT.#@0", hlD)
                    gates(1, range(T - 1, T))
                    for n in range(EARLY // 4, EARLY // 2):
                        scale_state(1, 2 * n, n, n)

            def take(job, k, dst, own, func):
                act.wait_ge(filled, JOB[job] + 1)
                nc.scalar.activation(dst[:, k, :], bank[BANK[JOB[job]]][:], func,
                                     bias=inbias[:, own + k:own + k + 1]).then_inc(taken, 1)

            def scan_inputs(b):
                if b == 0:
                    act.wait_ge(inbias_ready, 1)
                else:
                    act.wait_ge(scanned, SCANS // 2)
                    act.wait_ge(odd_scanned, SCANS // 2)
                for k in range(T):
                    take(f"u.{k}@{b}", k, uT, 0, ACT.Identity)

            def gates(b, ks):
                for k in ks:
                    take(f"z.{k}@{b}", k, zT, T, ACT.Silu)

            def weights(par, k, landed, used):
                act.wait_ge(in_stage[par], landed)
                act.wait_ge(filled, used)
                nc.scalar.activation(weights_hl[par][:, 0, k, :], stage[par][:, k, :], ACT.Copy).then_inc(split_hi, 1)

            def first_weights(b):
                used = JOB["x_attn.3@1"] if b == 0 else JOB[f"expert.{E * T - T - 1}@0"]
                for k in range(T):
                    weights(0, k, LANDED[f"W0@{b}"], used + 1)

            def mix_experts(b, scan):
                job0 = JOB[f"expert.0@{b}"]
                loads = [LANDED[f"W0@{b}"], LANDED[f"W1@{b}"]]

                def trip(t, first, last):
                    for u in range(UN):
                        for k in AHEAD[u % T] if not (last and u >= T) else ():
                            par = 1 - u // T
                            weights(par, k, (t + u // T) * 16 + loads[par], t * UN + (job0 + u // T * T))
                        if scan and not scans_done(u, first, last):
                            scale_state(1, t * (2 * UN) + (2 * u + EARLY // 2), t * UN + (u + EARLY // 4), u + EARLY // 4)

                trips(act, MTRIPS, trip)

            prepare()
            attention(0, len(PREP_JOBS), False)
            middle(0)
            attention(1, JOB["z.3@0"] + 1, True)
            middle(1)
            mix_experts(0, True)
            round_kept(gated, 1 * T, yT, hlC)
            first_weights(1)
            round_rows("ffnT.#@1", hlD)
            mix_experts(1, False)

        @block.vector
        def _(dve):
            links = [0]

            def link(ins):
                links[0] += 1
                ins.then_inc(link_done, 1)
                dve.wait_ge(link_done, links[0])

            def lo_job(name, slot, k):
                dve.wait_ge(rounded, ROUND[name] + 1)
                nc.vector.tensor_tensor(slot[:, 1, k, :], bank[BANK[JOB[name]]][:], slot[:, 0, k, :].bitcast(F32),
                                        ALU.subtract).then_inc(evacuated, 1)

            def lo_jobs(name, slot):
                for k in range(T):
                    lo_job(name.replace("#", str(k)), slot, k)

            def lo_rows(name, slot, ks=range(T)):
                for k in ks:
                    job = name.replace("#", str(k))
                    cols = slice(k * P, (k + 1) * P)
                    dve.wait_ge(rounded, ROUND[job] + 1)
                    nc.vector.tensor_tensor(slot[:, 1, :, cols], bank[BANK[JOB[job]]][:].rearrange("p (t q) -> p t q", t=T),
                                            slot[:, 0, :, cols].bitcast(F32), ALU.subtract).then_inc(evacuated, 1)

            def lo_scaled(name, slot):
                for k in range(T):
                    job = name.replace("#", str(k))
                    dve.wait_ge(rounded, ROUND[job] + 1)
                    nc.vector.scalar_tensor_tensor(slot[:, 1, k, :], bank[BANK[JOB[job]]][:], vecs[:, 20 + k:21 + k],
                                                   slot[:, 0, k, :].bitcast(F32), ALU.mult, ALU.subtract).then_inc(evacuated, 1)

            def normalize(src, group, dst, dst2=None):
                norms = 1 if dst2 is None else 2
                cols = slice(group[0], group[-1] + 1)
                for t in group:
                    last = nc.vector.bn_aggr(mv[:, t, :], bnst[:, t, :])
                link(last)
                link(nc.vector.tensor_scalar(var[:, 0, cols], mv[:, cols, 1], EPS, None, ALU.add))
                if norms == 2:
                    link(nc.vector.scalar_tensor_tensor(var[:, 1, cols], var[:, 0, cols], EPS, mv[:, cols, 1], ALU.mult, ALU.add))
                v, r, a = (m[:, 0:norms, cols] for m in (var, rstd, newton))
                link(nc.vector.tensor_scalar(seed[:, 0:norms, cols], v.bitcast(I32), 1, None, ALU.logical_shift_right))
                link(nc.vector.tensor_scalar(r.bitcast(I32), seed[:, 0:norms, cols], -1.0, RSQRT_SEED, ALU.mult, ALU.add))
                for _k in range(3):
                    link(nc.vector.tensor_tensor(a, r, r, ALU.mult))
                    link(nc.vector.scalar_tensor_tensor(a, a, -0.5, v, ALU.mult, ALU.mult))
                    link(nc.vector.scalar_tensor_tensor(r, a, 1.5, r, ALU.add, ALU.mult))
                for n, out_rows in ((0, dst),) if dst2 is None else ((1, dst2), (0, dst)):
                    for t in group:
                        last = nc.vector.tensor_scalar(out_rows[:, t, :], src[:, t, :], mv[:, t, 0:1], rstd[:, n, t:t + 1],
                                                       ALU.subtract, ALU.mult)
                        if n == norms - 1 and t % 2:
                            last.then_inc(rows_ready, 1)
                return last

            def row_statistics(src, t):
                return nc.vector.bn_stats(bnst[:, t, :], src[:, t, :])

            def lo_kept(name, src, slot, k):
                dve.wait_ge(kept_hi, KEPT[name] + k + 1)
                nc.vector.tensor_tensor(slot[:, 1, k, :], src[:, k, :], slot[:, 0, k, :].bitcast(F32),
                                        ALU.subtract).then_inc(kept_split, 1)

            def split_kept(name, src, slot):
                for k in range(T):
                    lo_kept(name, src, slot, k)

            def keep_and_split(name, make, src, slot):
                for k in range(T + 1):
                    if k < T:
                        make(k)
                    if k > 0:
                        lo_kept(name, src, slot, k - 1)

            def folded_bias(dst, w, v, own):
                for t in range(T):
                    link(nc.vector.tensor_tensor_reduce(h[0][:], w[:, t, :], v[:], 1.0, 0.0, ALU.mult, ALU.add,
                                                        dst[:, t:t + 1]))
                return nc.vector.tensor_tensor(dst, dst, vecs[:, own:own + T], ALU.add)

            def first_norm(b, dst):
                dve.wait_ge(in_x[b], 16)
                for t in range(T):
                    last = row_statistics(xb[:, b], t)
                link(last)
                normalize(xb[:, b], range(T), dst)

            def prepare():
                nc.vector.memset(desc[:], 1.0).then_inc(desc_ready, 1)
                for e in range(E - 1):
                    dve.wait_ge(desc_ready, e + 1)
                    nc.vector.memset(desc[:, e:e + 1], float(E - e)).then_inc(desc_ready, 1)
                lo_jobs("qWT.#", hlA)
                split_kept("hW", stage[1], hlB)
                first_norm(0, rows)
                lo_jobs("x_to_q.#", hlC)
                lo_rows("xT0.#", hlD)
                dve.wait_ge(filled, JOB["vectors"] + 1)
                nc.vector.tensor_copy(vecs[:], bank[BANK[JOB["vectors"]]][:, 0:32]).then_inc(evacuated, 1)
                dve.wait_ge(evacuated, JOB["vectors"] + 1)
                nc.vector.tensor_copy(dtv[:], vecs[:, 28:32]).then_inc(vectors_ready, 1)
                dve.wait_ge(in_bias, 32)
                link(folded_bias(qbias[:], stage[0], probs[0], 0))
                first_norm(1, resid0)
                lo_jobs("kWT.#", hlF)
                keep_and_split("q0", lambda k: queries(0, k), qT[0], hlA)
                lo_rows("xT1.#", hlD)
                dve.wait_ge(in_k, 16)
                link(folded_bias(kbias[:], uT, probs[1], 4))
                for c in range(2):
                    last = nc.vector.tensor_copy(kbias_hl[:, 0, :, c], kbias[:])
                link(last)
                for c in range(2):
                    last = nc.vector.tensor_tensor(kbias_hl[:, 1, :, c], kbias[:], kbias_hl[:, 0, :, c].bitcast(F32), ALU.subtract)
                last.then_inc(kbias_ready, 1)
                lo_jobs("q_to_ctx.#", hlB)
                keep_and_split("q1", lambda k: queries(1, k), qT[1], hlF)
                dve.wait_ge(in_v, 16)
                link(folded_bias(vbias[:], yT, probs[1], 8))
                link(nc.vector.tensor_copy(vbias_hl[:, 0], vbias[:]))
                nc.vector.tensor_tensor(vbias_hl[:, 1], vbias[:], vbias_hl[:, 0].bitcast(F32), ALU.subtract).then_inc(vbias_ready, 1)
                lo_jobs("qc0.#", hlD)
                lo_jobs("vWT.#", hlC)
                small_parameters()
                for k in range(T):
                    dve.wait_ge(filled, JOB[f"qc1.{k}"] + 1)
                    nc.vector.tensor_copy(qc1[:, k, :], bank[BANK[JOB[f"qc1.{k}"]]][:]).then_inc(evacuated, 1)
                lo_jobs("ctx_to_v.#", hlB)
                lo_jobs("oWT.#", hlC)
                for n in range(B):
                    dve.wait_ge(filled, JOB[f"key_row.{n}"] + 1)
                    nc.vector.tensor_copy(key_row[n][0:2, :], bank[BANK[JOB[f"key_row.{n}"]]][0:2, :]).then_inc(evacuated, 1)
                dve.wait_ge(filled, JOB["x_bias"] + 1)
                nc.vector.tensor_tensor(obB[:], bank[BANK[JOB["x_bias"]]][:], obB[:], ALU.add).then_inc(evacuated, 1)
                dve.wait_ge(filled, JOB["key_bias"] + 1)
                nc.vector.tensor_copy(kq[:], bank[BANK[JOB["key_bias"]]][:, 0:2 * B * T].rearrange("p (n c) -> p n c", c=2)[:, :, 0]
                                      ).then_inc(evacuated, 1)
                lo_jobs("ctx_to_x.#", ctx_to_x)
                dve.wait_ge(in_lnb, 16)
                dve.wait_ge(in_k, 32)
                link(folded_bias(inbias[:, 0:T], uT, probs[0], 12))
                dve.wait_ge(in_v, 32)
                folded_bias(inbias[:, T:2 * T], yT, probs[0], 16).then_inc(inbias_ready, 1)
                dve.wait_ge(x_biased, 1)
                for k in range(T):
                    add_to_x(f"qo0.{k}", 0, k)
                lo_jobs("ctx0T.#@0", ctxT[0])
                for k in range(T):
                    add_to_x(f"qo1.{k}", 1, k)

            def add_to_x(job, b, k):
                dve.wait_ge(filled, JOB[job] + 1)
                nc.vector.tensor_tensor(xb[:, b, k, :], bank[BANK[JOB[job]]][:], xb[:, b, k, :],
                                        ALU.add).then_inc(evacuated, 1)

            def queries(b, k):
                dve.wait_ge(filled, JOB[f"q{b}.{k}"] + 1)
                ins = nc.vector.tensor_scalar(qT[b][:, k, :], bank[BANK[JOB[f"q{b}.{k}"]]][:], qbias[:, k:k + 1], None,
                                              ALU.add)
                ins.then_inc(evacuated, 1)

            def small_parameters():
                dve.wait_ge(in_small, 16 * 5)
                nc.vector.tensor_copy(eb_hl[:, 0], eb)
                link(nc.vector.tensor_copy(gate_hl[:, 0], gate_raw[:]))
                nc.vector.tensor_tensor(eb_hl[:, 1], eb, eb_hl[:, 0].bitcast(F32), ALU.subtract)
                nc.vector.tensor_tensor(gate_hl[:, 1], gate_raw[:], gate_hl[:, 0].bitcast(F32),
                                        ALU.subtract).then_inc(gate_ready, 1)
                dve.wait_ge(ssm_exp, 2)
                link(nc.vector.tensor_scalar(dtv[:], dtv[:], 1e-4, 1.0, ALU.max, ALU.min))
                ea, w, p, dtb = (ssm_w[:, k] for k in range(4))
                for t in range(T):
                    last = nc.vector.tensor_scalar(w[:, t, :], ea[:, t, :], dtv[:, t:t + 1], -1.0, ALU.mult, ALU.mult)
                link(last)
                link(nc.vector.tensor_tensor(dtb[:], ssm_in[:, 1], ssm_in[:, 2], ALU.mult))
                for t in range(T):
                    last = nc.vector.tensor_scalar(cbdt[:, :, t], dtb[:, t, :], dtv[:, t:t + 1], None, ALU.mult)
                link(last)
                link(nc.vector.tensor_scalar(w[:], w[:], -30.0, 0.5 ** EXPM1_DOUBLINGS, ALU.max, ALU.mult))
                link(nc.vector.tensor_scalar(p[:], w[:], 0.2, 1.0, ALU.mult, ALU.add))
                for k in (4.0, 3.0, 2.0):
                    link(nc.vector.scalar_tensor_tensor(p[:], p[:], 1.0 / k, w[:], ALU.mult, ALU.mult))
                    link(nc.vector.tensor_scalar(p[:], p[:], 1.0, None, ALU.add))
                link(nc.vector.tensor_tensor(p[:], p[:], w[:], ALU.mult))
                for _k in range(EXPM1_DOUBLINGS):
                    link(nc.vector.scalar_tensor_tensor(p[:], p[:], 2.0, p[:], ALU.add, ALU.mult))
                link(nc.vector.tensor_scalar(p[:], p[:], 1.0, 1e-8, ALU.add, ALU.max))
                link(nc.vector.tensor_scalar(abar[:].rearrange("p n t -> p t n"), p[:], 1.0 - 1e-8, None, ALU.min))

            def attention(b, scan):
                base, blocks = b * STEPS, b * BLOCKS

                def maxima(t, u):
                    par, q = u // T % 2, u % T
                    col = slice(q, q + 1)
                    dve.wait_ge(scores_ready, t * UN + (base + u + 1))
                    nc.vector.tensor_reduce(mx[:, col], sbank[u % 2][:], AX_X, ALU.max).then_inc(stat_done, 1)
                    dve.wait_ge(stat_done, t * (2 * UN) + (2 * base + 2 * u + 1))
                    nc.vector.tensor_scalar(mrun[:, 1 - par, col], mx[:, col], kq[:, b * T + q:b * T + q + 1], mrun[:, par, col],
                                            ALU.add, ALU.max).then_inc(stat_done, 1)
                    dve.wait_ge(stat_done, t * (2 * UN) + (2 * base + 2 * u + 2))
                    nc.vector.tensor_scalar(nbias[:, col], mrun[:, 1 - par, col], kq[:, b * T + q:b * T + q + 1], -SCALE,
                                            ALU.subtract, ALU.mult).then_inc(max_ready, 1)
                    nc.vector.tensor_tensor(dmax[:, col], mrun[:, par, col], mrun[:, 1 - par, col],
                                            ALU.subtract).then_inc(dmax_ready, 1)

                def turned_probs(t, u):
                    dve.wait_ge(pT_hi, t * UN + (base + u + 1))
                    nc.vector.tensor_tensor(probsT[u % 2][:, 1], tbank[u % 2][:].rearrange("p (j q) -> p j q", j=T),
                                            probsT[u % 2][:, 0].bitcast(F32), ALU.subtract).then_inc(pT_split, 1)

                def context_block(t, u):
                    par, dd = (u // T + 1) % 2, u % T
                    dve.wait_ge(cT_hi, t * UN + (blocks + u + 1))
                    nc.vector.tensor_tensor(ctxT[par][:, 1, dd, :], cbank[dd % 2][:], ctxT[par][:, 0, dd, :].bitcast(F32),
                                            ALU.subtract).then_inc(cT_split, 1)

                def sums(t, u):
                    q = u % T
                    col = slice(q, q + 1)
                    dve.wait_ge(alpha_ready, t * UN + (base + u + 1))
                    dve.wait_ge(probs_ready, t * UN + (base + u + 1))
                    wait_pos(dve, sums_updated, 2 * base, t * (2 * UN) + 2 * (u - 3))
                    nc.vector.scalar_tensor_tensor(lsum[:, col], lsum[:, col], alpha[:, col], rsum[:, col],
                                                   ALU.mult, ALU.add).then_inc(sums_updated, 1)
                    dve.wait_ge(pv_ready, t * UN + (base + u + 1))
                    nc.vector.scalar_tensor_tensor(rows[:, q, :], rows[:, q, :], alpha[:, col], obank[u % 2][:],
                                                   ALU.mult, ALU.add).then_inc(sums_updated, 1)

                def trip(t, first, last):
                    for u in range(UN):
                        if not (last and u >= T):
                            context_block(t, u)
                        maxima(t, u)
                        if not (first and u < 1):
                            turned_probs(*((t, u - 1) if u else (t - 1, UN - 1)))
                        if scan:
                            scan_state(0, t * UN + u, u, t * T + u // 2, first and u < 2)
                            if u % 2:
                                add_state(0, t * UN + u, u, t * T + u // 2)
                        if not (first and u < 2):
                            sums(*((t, u - 2) if u >= 2 else (t - 1, u - 2 + UN)))

                dve.wait_ge(sums_zeroed, 3 * (b + 1))
                trips(dve, TRIPS, trip)
                turned_probs(TRIPS - 1, UN - 1)
                sums(TRIPS - 1, UN - 2)
                sums(TRIPS - 1, UN - 1)

            def scan_state(b, s, k, n, first):
                dst = h[1] if k % 2 else even_h[b][k // 2 % 2]
                if not first:
                    dve.wait_ge(odd_summed if k % 2 else summed, n + (b * SCANS // 2 - (b if k % 2 == 0 else 0)))
                col = abar[:].rearrange("p n d -> p (n d)")[:, bass.ds(s, 1)]
                scan = nc.vector.tensor_tensor_scan(dst[:], col.to_broadcast([P, S]), uT[:, k % T, :], 0.0,
                                                    ALU.mult, ALU.add)
                scan.then_inc(odd_scanned if k % 2 else scanned, 1)

            def add_state(b, s, k, n):
                dve.wait_ge(odd_scanned, n + (b * SCANS // 2 + 1))
                weight = cbdt[:].rearrange("p n d -> p (n d)")[:, bass.ds(s, 1)]
                nc.vector.scalar_tensor_tensor(yT[:, k % T, :], h[1][:], weight, yT[:, k % T, :],
                                               ALU.mult, ALU.add).then_inc(odd_summed, 1)

            def scan_two(s, k, n):
                scan_state(1, s + 1, k + 1, n, False)
                scan_state(1, s, k, n, False)
                add_state(1, s + 1, k + 1, n)

            def add_attention(b, k):
                job = f"x_attn.{k}@{b}"
                dve.wait_ge(filled, JOB[job] + 1)
                nc.vector.scalar_tensor_tensor(xb[:, b, k, :], bank[BANK[JOB[job]]][:], lsum[:, k:k + 1], xb[:, b, k, :],
                                               ALU.mult, ALU.add).then_inc(evacuated, 1)

            def middle(b):
                dve.wait_ge(sums_updated, 2 * (b + 1) * STEPS)
                link(nc.vector.reciprocal(lsum[:], lsum[:]))
                lo_scaled(f"inT0.#@{b}", hlB)
                lo_rows(f"pooledT.#@{b}", hlA)
                lo_scaled(f"inT1.#@{b}", hlC)
                if b == 1:
                    lo_jobs("outT.#", hlF)
                for group in GROUPS[b]:
                    if group[0] == 0:
                        for k in group:
                            add_attention(b, k)
                            dve.wait_ge(evacuated, JOB[f"x_attn.{k}@{b}"] + 1)
                            last = row_statistics(xb[:, b], k)
                    else:
                        for k in group:
                            add_attention(b, k)
                        lo_rows("normT.#@0", hlF, range(group[0]))
                        dve.wait_ge(evacuated, JOB["x_attn.3@0"] + 1)
                        for k in group:
                            last = row_statistics(xb[:, b], k)
                    link(last)
                    last = normalize(xb[:, b], group, resid[b], rows)
                last.then_inc(resid_ready, 1)
                if b == 1:
                    dve.wait_ge(resid_biased, 1)
                    for k in range(T - 1):
                        project_tile(0, k)
                lo_rows(f"normT.#@{b}", hlF if b == 0 else hlA, GROUPS[b][-1])
                if b == 1:
                    project_tile(0, T - 1)
                if b == 0:
                    note_taken("u", 0, range(T))
                    lo_jobs("ctx0T.#@1", ctxT[0])
                    note_taken("z", 0, range(T))
                    dve.wait_ge(y_zeroed, 1)
                else:
                    for k in range(T):
                        last = add_mixed(0, k)
                    link(last)
                    normalize(xb[:, 0], range(T), rows)
                    note_taken("u", 1, range(T))
                    dve.wait_ge(y_zeroed, 2)
                    early_scans(range(EARLY // 2))
                    note_taken("z", 1, range(T - 1))
                    lo_rows("ffnT.#@0", hlD)
                    note_taken("z", 1, range(T - 1, T))
                    early_scans(range(EARLY // 2, EARLY - 2))
                    gate(0)

            def note_taken(kind, b, ks):
                for k in ks:
                    n = TAKEN[f"{kind}.{k}@{b}"]
                    dve.wait_ge(taken, n + 1)
                    nc.vector.memset(tick[:, n:n + 1], 0.0).then_inc(evacuated, 1)

            def early_scans(columns):
                for s in columns[::2]:
                    scan_two(s, s, s // 2)

            def project_tile(b, k):
                name = f"x_ssm.{k}@{b}"
                dve.wait_ge(filled, JOB[name] + 1)
                nc.vector.tensor_tensor(resid[b][:, k, :], bank[BANK[JOB[name]]][:], resid[b][:, k, :],
                                        ALU.add).then_inc(evacuated, 1)

            def add_mixed(b, k):
                dve.wait_ge(evacuated, JOB[f"x_ssm.{k}@{b}"] + 1)
                link(nc.vector.tensor_scalar(resid[b][:, k, :], resid[b][:, k, :], 10.0, -10.0, ALU.min, ALU.max))
                link(nc.vector.tensor_tensor(xb[:, b, k, :], xb[:, b, k, :], resid[b][:, k, :], ALU.add))
                return row_statistics(xb[:, b], k)

            def gate_output(b):
                dve.wait_ge(summed, (b + 1) * SCANS // 2)
                dve.wait_ge(odd_summed, (b + 1) * SCANS // 2)
                dve.wait_ge(taken, TAKEN[f"z.{T - 1}@{b}"] + 1)
                for k in range(T):
                    nc.vector.tensor_tensor(yT[:, k, :], yT[:, k, :], zT[:, k, :], ALU.mult).then_inc(gated, 1)

            def project_out(b):
                dve.wait_ge(resid_biased, b + 1)
                for k in range(T):
                    project_tile(b, k)
                    last = add_mixed(b, k)
                link(last)
                normalize(xb[:, b], range(T), rows)

            def gate(b):
                name = f"logits@{b}"
                dve.wait_ge(filled, JOB[name] + 1)
                nc.vector.tensor_copy(logitT[0:E], bank[BANK[JOB[name]]][0:E, :]).then_inc(evacuated, 1)
                if b == 0:
                    early_scans(range(EARLY - 2, EARLY))
                name = f"logit_columns@{b}"
                dve.wait_ge(filled, JOB[name] + 1)
                for k in range(T):
                    last = nc.vector.tensor_tensor(logit[:, k, :], bank[BANK[JOB[name]]][:, k * E:(k + 1) * E], gbB[:], ALU.add)
                last.then_inc(evacuated, 1)
                dve.wait_ge(evacuated, JOB[name] + 1)
                link(nc.vector.tensor_reduce(lmax[:, 0], logit[:], AX_X, ALU.max))
                dve.wait_ge(desc_ready, E)
                for k in range(T):
                    last = nc.vector.scalar_tensor_tensor(pick[:, k, :], logit[:, k, :], lmax[:, 0, k:k + 1], desc[:],
                                                          ALU.is_equal, ALU.mult)
                link(last)
                link(nc.vector.tensor_reduce(lmax[:, 1], pick[:], AX_X, ALU.max))
                for k in range(T):
                    last = nc.vector.tensor_scalar(onehot[:, k, :], pick[:, k, :], lmax[:, 1, k:k + 1], None, ALU.is_equal)
                last.then_inc(onehot_ready, 1)

            def keep_onehot(b):
                name = f"onehotT@{b}"
                dve.wait_ge(filled, JOB[name] + 1)
                nc.vector.tensor_copy(onehotT[:], bank[BANK[JOB[name]]][0:E, :]).then_inc(evacuated, 1)

            def expert_biases(b, ks):
                for k in ks:
                    name = f"expert_bias.{k}@{b}"
                    dve.wait_ge(filled, JOB[name] + 1)
                    dve.wait_ge(evacuated, JOB[f"expert.{E * T - b * UN - T + k}@{b}"] + 1)
                    nc.vector.tensor_tensor(xb[:, b, k, :], bank[BANK[JOB[name]]][:], xb[:, b, k, :],
                                            ALU.add).then_inc(evacuated, 1)

            def mix_experts(b, scan):
                weight = onehot[:].rearrange("p t e -> p (t e)")

                def trip(t, first, last):
                    if last and b == 1:
                        keep_onehot(1)
                        expert_biases(1, range(T))
                    job0 = job_base(b, last)
                    for u in range(UN):
                        k = u % T
                        if last and scan and u == UN - EARLY // 4 + 1:
                            split_kept("gated@1", yT, hlC)
                        dve.wait_ge(filled, t * UN + (job0 + u + 1))
                        dve.wait_ge(evacuated, t * UN + (job0 + u + 1 - T))
                        nc.vector.scalar_tensor_tensor(xb[:, b, k, :], expert_bank(b, job0 + u)[:],
                                                       weight[:, bass.ds(t * 2 + (k * E + u // T), 1)], xb[:, b, k, :],
                                                       ALU.mult, ALU.add).then_inc(evacuated, 1)
                        if scan and not scans_done(u, first, last):
                            scan_two(t * (2 * UN) + (2 * u + EARLY // 2), 2 * u + EARLY // 2, t * UN + (u + EARLY // 4))
                        if last and scan and u == UN - EARLY // 4:
                            gate_output(1)

                dve.wait_ge(onehot_ready, b + 1)
                trips(dve, MTRIPS, trip)

            prepare()
            attention(0, False)
            middle(0)
            attention(1, True)
            middle(1)
            mix_experts(0, True)
            keep_onehot(0)
            project_out(1)
            expert_biases(0, range(T // 2))
            lo_rows("ffnT.#@1", hlD)
            expert_biases(0, range(T // 2, T))
            gate(1)
            mix_experts(1, False)

        @block.gpsimd
        def _(pool):
            nc.gpsimd.memset(ident[:], 0.0).then_inc(ident_zero, 1)
            pool.wait_ge(ident_zero, 1)
            nc.gpsimd.affine_select(out=ident[:], in_=ident[:], compare_op=ALU.not_equal, fill=1.0, base=0,
                                    pattern=[[-1, P]], channel_multiplier=1).then_inc(ident_ready, 1)

            def lo_tiles(name, src, slot):
                for k in range(T):
                    pool.wait_ge(split_hi, SPLIT[name] + k + 1)
                    nc.gpsimd.tensor_tensor(slot[:, 1, k, :], src[:, k, :], slot[:, 0, k, :].bitcast(F32),
                                            ALU.subtract).then_inc(split_done, 1)

            def add_state(b, k, n, first):
                pool.wait_ge(scaled, n + (b * SCANS // 2 + 1))
                if not first:
                    pool.wait_ge(summed, n + (b * SCANS // 2 - 1))
                nc.gpsimd.tensor_tensor(yT[:, k % T, :], yT[:, k % T, :], even_h[b][k // 2 % 2][:], ALU.add).then_inc(summed, 1)

            def attention(b, scan):
                base = b * STEPS

                def natural(t, u):
                    par, j = (u + 2) // T % 2, (u + 2) % T
                    pool.wait_ge(nat_hi, t * UN + (base + u + 2 + 1))
                    nc.gpsimd.tensor_tensor(nat[par][:, 1, j, :], stage[par][:, j, :], nat[par][:, 0, j, :].bitcast(F32),
                                            ALU.subtract).then_inc(nat_split, 1)

                def trip(t, first, last):
                    for u in range(UN):
                        if not (last and u + 2 >= UN):
                            natural(t, u)
                        if scan and u % 2 == 0:
                            add_state(0, u, t * T + u // 2, first and u < T)

                for j in range(2):
                    pool.wait_ge(nat_hi, base + j + 1)
                    nc.gpsimd.tensor_tensor(nat[0][:, 1, j, :], stage[0][:, j, :], nat[0][:, 0, j, :].bitcast(F32),
                                            ALU.subtract).then_inc(nat_split, 1)
                trips(pool, TRIPS, trip)

            def middle(b):
                if b == 0:
                    lo_tiles("qc1", qc1, qc_hl)
                else:
                    gate_output(0)
                pool.wait_ge(resid_ready, b + 1)
                for t in range(T):
                    last = nc.gpsimd.tensor_tensor(resid[b][:, t, :], resid[b][:, t, :], outbB[:], ALU.add)
                last.then_inc(resid_biased, 1)
                if b == 0:
                    pool.wait_ge(inbias_ready, 1)
                else:
                    pool.wait_ge(kept_split, KEPT["gated@0"] + T)
                nc.gpsimd.memset(yT[:], 0.0).then_inc(y_zeroed, 1)
                pool.wait_ge(y_zeroed, b + 1)
                if b == 1:
                    first_weights(0)
                    for n in range(EARLY // 2):
                        add_state(1, 2 * n, n, False)

            def gate_output(b):
                pool.wait_ge(summed, (b + 1) * SCANS // 2)
                pool.wait_ge(odd_summed, (b + 1) * SCANS // 2)
                pool.wait_ge(taken, TAKEN[f"z.{T - 1}@{b}"] + 1)
                for k in range(T):
                    nc.gpsimd.tensor_tensor(yT[:, k, :], yT[:, k, :], zT[:, k, :], ALU.mult).then_inc(gated, 1)
                for k in range(T):
                    pool.wait_ge(kept_hi, KEPT[f"gated@{b}"] + k + 1)
                    nc.gpsimd.tensor_tensor(hlD[:, 1, k, :], yT[:, k, :], hlD[:, 0, k, :].bitcast(F32),
                                            ALU.subtract).then_inc(kept_split, 1)

            def clear_sums(b):
                pool.wait_ge(filled, JOB["key_bias" if b == 0 else "normT.3@0"] + 1)
                nc.gpsimd.memset(rows[:], 0.0).then_inc(sums_zeroed, 1)
                nc.gpsimd.memset(lsum[:], 0.0).then_inc(sums_zeroed, 1)
                nc.gpsimd.memset(mrun[:, 0], LOWEST).then_inc(sums_zeroed, 1)

            def weights(par, k, count):
                pool.wait_ge(split_hi, count)
                nc.gpsimd.tensor_tensor(weights_hl[par][:, 1, k, :], stage[par][:, k, :],
                                        weights_hl[par][:, 0, k, :].bitcast(F32), ALU.subtract).then_inc(split_done, 1)

            def first_weights(b):
                for k in range(T):
                    weights(0, k, SPLIT[f"W0@{b}"] + k + 1)

            def mix_experts(b, scan):
                split0 = SPLIT[f"W0@{b}"]

                def trip(t, first, last):
                    for u in range(UN):
                        for k in AHEAD[u % T] if not (last and u >= T) else ():
                            weights(1 - u // T, k, t * UN + (split0 + T + u // T * T + k + 1))
                        if scan and not scans_done(u, first, last):
                            add_state(1, 2 * u + EARLY // 2, t * UN + (u + EARLY // 4), False)

                trips(pool, MTRIPS, trip)

            lo_tiles("cW", zT, hlE)
            pool.wait_ge(rows_ready, ROWS["x1"])
            pool.wait_ge(evacuated, JOB["x_bias"] + 1)
            for b in range(B):
                for t in range(T):
                    last = nc.gpsimd.tensor_tensor(xb[:, b, t, :], xb[:, b, t, :], obB[:], ALU.add)
            last.then_inc(x_biased, 1)
            clear_sums(0)
            attention(0, False)
            middle(0)
            clear_sums(1)
            attention(1, True)
            middle(1)
            mix_experts(0, True)
            first_weights(1)
            mix_experts(1, False)


_INS = ["x", "ctx_1024", "L0_xattn_hW", "L0_xattn_hb", "L0_xattn_cW", "L0_xattn_cb", "L0_xattn_qW", "L0_xattn_qb",
        "L0_xattn_kW", "L0_xattn_kb", "L0_xattn_vW", "L0_xattn_vb", "L0_xattn_oW", "L0_xattn_ob", "L0_attn_A_log",
        "L0_attn_B_param", "L0_attn_C_param", "L0_attn_log_dt", "L0_attn_in_w", "L0_attn_in_b", "L0_attn_out_w",
        "L0_attn_out_b", "L0_attn_ln_g", "L0_attn_ln_b", "L0_ffn_gate_w", "L0_ffn_gate_b", "L0_ffn_expert_w",
        "L0_ffn_expert_b"]
_OUTS = [((B, S, D), "float32")]


def kernel(**inputs):
    import numpy as _np
    import concourse.bacc as _bacc
    from concourse import mybir as _mybir
    from concourse.bass_utils import run_bass_kernel_spmd as _run

    nc = _bacc.Bacc("TRN2", target_bir_lowering=False, num_devices=1)
    arrays, args = {}, []
    for name in _INS:
        a = _np.ascontiguousarray(inputs[name])
        arrays[f"in_{name}_dram"] = a
        args.append(nc.dram_tensor(f"in_{name}_dram", a.shape, _mybir.dt.from_np(a.dtype), kind="ExternalInput").ap())
    for i, (shape, dtype) in enumerate(_OUTS):
        dt = _mybir.dt.from_np(_np.dtype(dtype))
        args.append(nc.dram_tensor(f"out_{i}_dram", shape, dt, kind="ExternalOutput").ap())
    build(nc, *args)
    r = _run(nc, [arrays], core_ids=[0])
    got = tuple(r.results[0][f"out_{i}_dram"] for i in range(len(_OUTS)))
    return got[0]
```
